# Optimizing a Trainium2 kernel written in Bass

```python
import numpy as np
import jax
import jax.numpy as jnp

def _softmax(x, axis=-1):
    return jax.nn.softmax(x, axis=axis)

def _gelu(x):
    return jax.nn.gelu(x, approximate=True)

def _silu(x):
    return jax.nn.silu(x)

def _sigmoid(x):
    return jax.nn.sigmoid(x)

def _layernorm(x, axis=-1, eps=1e-05):
    m = jnp.mean(x, axis=axis, keepdims=True)
    v = jnp.var(x, axis=axis, keepdims=True)
    return (x - m) / jnp.sqrt(v + eps)

def _scatter_add(tgt, idx, src, axis=0):
    return tgt.at[idx].add(src)

def _segment_sum(src, seg, n):
    return jax.ops.segment_sum(src, seg, n)
kernel_name = 'mk_seq_preln_d2_jaxref_r8_bded95'

def setup_inputs(seed: int=0):
    np.random.seed(seed)
    _w = jnp.asarray

    def _L0_attn_setup():
        import math
        import jax, jax.numpy as jnp
        import numpy as np
        B, T, D_MODEL = (4, 256, 128)
        H, HD = (16, 64)
        NF = 128
        EPS = 1e-06
        INV_SQRT_NF = 1.0 / math.sqrt(NF)

        def make_orf(key, head_dim, n_features, dtype=jnp.float32):
            n_blocks = math.ceil(n_features / head_dim)
            keys = jax.random.split(key, n_blocks)
            blocks = []
            for k in keys:
                g = jax.random.normal(k, (head_dim, head_dim), dtype)
                qm, _ = jnp.linalg.qr(g)
                blocks.append(qm)
            W = jnp.concatenate(blocks, axis=1)[:, :n_features]
            return W * jnp.asarray(math.sqrt(head_dim), dtype)

        def _favor_plus(x, W):
            sq = 0.5 * jnp.sum(x * x, axis=-1, keepdims=True)
            return jnp.exp(x @ W - sq) * INV_SQRT_NF

        def _causal_linear_attention(qp, kp, v):
            Bb, Hh = (qp.shape[0], qp.shape[1])

            def step(carry, qkv):
                S, z = carry
                q_t, k_t, v_t = qkv
                S = S + jnp.einsum('bhd,bhe->bhde', k_t, v_t)
                z = z + k_t
                num = jnp.einsum('bhd,bhde->bhe', q_t, S)
                den = jnp.einsum('bhd,bhd->bh', q_t, z) + EPS
                return ((S, z), num / den[..., None])
            S0 = jnp.zeros((Bb, Hh, NF, HD), qp.dtype)
            z0 = jnp.zeros((Bb, Hh, NF), qp.dtype)
            xs = (jnp.moveaxis(qp, 2, 0), jnp.moveaxis(kp, 2, 0), jnp.moveaxis(v, 2, 0))
            _, ys = jax.lax.scan(step, (S0, z0), xs)
            return jnp.moveaxis(ys, 0, 2)
        key = jax.random.key(seed)
        k0, k1, k2, k3, k4, k5 = jax.random.split(key, 6)
        s = 1.0 / math.sqrt(D_MODEL)
        x = jax.random.normal(k0, (B, T, D_MODEL), jnp.float32)
        Wq = jax.random.uniform(k1, (D_MODEL, H * HD), jnp.float32, -s, s)
        Wk = jax.random.uniform(k2, (D_MODEL, H * HD), jnp.float32, -s, s)
        Wv = jax.random.uniform(k3, (D_MODEL, H * HD), jnp.float32, -s, s)
        Wo = jax.random.uniform(k4, (H * HD, D_MODEL), jnp.float32, -s, s)
        W_feat = make_orf(k5, HD, NF)
        return {'x': x, 'Wq': Wq, 'Wk': Wk, 'Wv': Wv, 'Wo': Wo, 'W_feat': W_feat}
    _L0_attn_in = _L0_attn_setup()

    def _L0_ffn_setup():
        import jax, jax.numpy as jnp
        import numpy as np
        DMODEL = 128
        N_EXPERTS = 32
        EXPERT_SIZE = 64
        N_HEADS = 4
        WEIGHT_SCALE = 1.0
        key = jax.random.key(seed)
        k0, k1, k2, k3 = jax.random.split(key, 4)
        x = jax.random.normal(k0, (2, 256, DMODEL), dtype=jnp.float32)
        expert_sel = jax.random.normal(k1, (N_EXPERTS, DMODEL), dtype=jnp.float32) * DMODEL ** (-0.5)
        keys = jax.random.normal(k2, (N_EXPERTS, DMODEL, EXPERT_SIZE), dtype=jnp.float32) * DMODEL ** (-0.5)
        values = jax.random.normal(k3, (N_EXPERTS, EXPERT_SIZE, DMODEL), dtype=jnp.float32) * (N_EXPERTS * EXPERT_SIZE) ** (-0.5)
        return {'x': x, 'expert_sel': expert_sel, 'keys': keys, 'values': values}
    _L0_ffn_in = _L0_ffn_setup()

    def _L1_attn_setup():
        import jax, jax.numpy as jnp
        import numpy as np
        from jax import lax
        L, B, T, C, F = (4, 4, 256, 128, 512)
        EPS = 1e-05

        def layernorm(x, w, b):
            m = jnp.mean(x, axis=-1, keepdims=True)
            v = jnp.var(x, axis=-1, keepdims=True)
            return (x - m) * lax.rsqrt(v + EPS) * w + b

        def time_shift(x):
            return jnp.pad(x, ((0, 0), (1, 0), (0, 0)))[:, :-1]

        def wkv(time_decay, time_first, k, v):
            w = -jnp.exp(time_decay)
            u = time_first
            kt = jnp.swapaxes(k, 0, 1)
            vt = jnp.swapaxes(v, 0, 1)
            Bn, Cn = (k.shape[0], k.shape[2])
            init = (jnp.zeros((Bn, Cn), k.dtype), jnp.zeros((Bn, Cn), k.dtype), jnp.full((Bn, Cn), -1e+38, k.dtype))

            def step(carry, kv):
                aa, bb, pp = carry
                kk, vv = kv
                ww = u + kk
                qq = jnp.maximum(pp, ww)
                e1 = jnp.exp(pp - qq)
                e2 = jnp.exp(ww - qq)
                out = (e1 * aa + e2 * vv) / (e1 * bb + e2)
                ww2 = pp + w
                qq2 = jnp.maximum(ww2, kk)
                e1b = jnp.exp(ww2 - qq2)
                e2b = jnp.exp(kk - qq2)
                return ((e1b * aa + e2b * vv, e1b * bb + e2b, qq2), out)
            _, out = lax.scan(step, init, (kt, vt))
            return jnp.swapaxes(out, 0, 1)
        key = jax.random.key(seed)
        ks = jax.random.split(key, 16)
        s = 0.02
        d = {}
        d['x'] = jax.random.normal(ks[0], (B, T, C), jnp.float32)
        d['ln0_w'] = jnp.ones((C,), jnp.float32)
        d['ln0_b'] = jnp.zeros((C,), jnp.float32)
        d['ln1_w'] = jnp.ones((L, C), jnp.float32)
        d['ln1_b'] = jnp.zeros((L, C), jnp.float32)
        d['ln2_w'] = jnp.ones((L, C), jnp.float32)
        d['ln2_b'] = jnp.zeros((L, C), jnp.float32)
        d['time_decay'] = jax.random.normal(ks[1], (L, C), jnp.float32) * 0.5
        d['time_first'] = jax.random.normal(ks[2], (L, C), jnp.float32) * 0.5 + jnp.float32(np.log(0.3))
        d['tmk'] = jax.random.uniform(ks[3], (L, C), jnp.float32)
        d['tmv'] = jax.random.uniform(ks[4], (L, C), jnp.float32)
        d['tmr'] = jax.random.uniform(ks[5], (L, C), jnp.float32)
        d['Wk'] = jax.random.normal(ks[6], (L, C, C), jnp.float32) * s
        d['Wv'] = jax.random.normal(ks[7], (L, C, C), jnp.float32) * s
        d['Wr'] = jax.random.normal(ks[8], (L, C, C), jnp.float32) * s
        d['Wo'] = jax.random.normal(ks[9], (L, C, C), jnp.float32) * s
        d['cmk'] = jax.random.uniform(ks[10], (L, C), jnp.float32)
        d['cmr'] = jax.random.uniform(ks[11], (L, C), jnp.float32)
        d['Wck'] = jax.random.normal(ks[12], (L, F, C), jnp.float32) * s
        d['Wcv'] = jax.random.normal(ks[13], (L, C, F), jnp.float32) * s
        d['Wcr'] = jax.random.normal(ks[14], (L, C, C), jnp.float32) * s
        return d
    _L1_attn_in = _L1_attn_setup()

    def _L1_ffn_setup():
        import jax, jax.numpy as jnp
        import numpy as np
        B, L, D = (4, 128, 128)
        E, H, K = (16, 64, 8)
        EPS = 1e-12

        def _l2norm(v, axis=-1):
            n = jnp.sqrt(jnp.sum(v * v, axis=axis, keepdims=True))
            return v / jnp.maximum(n, EPS)
        if __name__ == '__main__':
            out = reference(**setup_inputs())
            print(out.shape)
        key = jax.random.key(seed)
        ks = jax.random.split(key, 8)
        s = lambda fan_in: 1.0 / np.sqrt(fan_in)
        return {'x': jax.random.normal(ks[0], (B, L, D), jnp.float32), 'gate_w': jax.random.normal(ks[1], (E, D), jnp.float32) * s(D), 'w_gate': jax.random.normal(ks[2], (E, D, H), jnp.float32) * s(D), 'w_up': jax.random.normal(ks[3], (E, D, H), jnp.float32) * s(D), 'w_down': jax.random.normal(ks[4], (E, H, D), jnp.float32) * s(H), 'sw_gate': jax.random.normal(ks[5], (D, H), jnp.float32) * s(D), 'sw_up': jax.random.normal(ks[6], (D, H), jnp.float32) * s(D), 'sw_down': jax.random.normal(ks[7], (H, D), jnp.float32) * s(H)}
    _L1_ffn_in = _L1_ffn_setup()
    _d = {'L0_attn_x': _L0_attn_in['x'], 'L0_attn_Wq': _L0_attn_in['Wq'], 'L0_attn_Wk': _L0_attn_in['Wk'], 'L0_attn_Wv': _L0_attn_in['Wv'], 'L0_attn_Wo': _L0_attn_in['Wo'], 'L0_attn_W_feat': _L0_attn_in['W_feat'], 'L0_ffn_expert_sel': _L0_ffn_in['expert_sel'], 'L0_ffn_keys': _L0_ffn_in['keys'], 'L0_ffn_values': _L0_ffn_in['values'], 'L1_attn_ln0_w': _L1_attn_in['ln0_w'], 'L1_attn_ln0_b': _L1_attn_in['ln0_b'], 'L1_attn_ln1_w': _L1_attn_in['ln1_w'], 'L1_attn_ln1_b': _L1_attn_in['ln1_b'], 'L1_attn_ln2_w': _L1_attn_in['ln2_w'], 'L1_attn_ln2_b': _L1_attn_in['ln2_b'], 'L1_attn_time_decay': _L1_attn_in['time_decay'], 'L1_attn_time_first': _L1_attn_in['time_first'], 'L1_attn_tmk': _L1_attn_in['tmk'], 'L1_attn_tmv': _L1_attn_in['tmv'], 'L1_attn_tmr': _L1_attn_in['tmr'], 'L1_attn_Wk': _L1_attn_in['Wk'], 'L1_attn_Wv': _L1_attn_in['Wv'], 'L1_attn_Wr': _L1_attn_in['Wr'], 'L1_attn_Wo': _L1_attn_in['Wo'], 'L1_attn_cmk': _L1_attn_in['cmk'], 'L1_attn_cmr': _L1_attn_in['cmr'], 'L1_attn_Wck': _L1_attn_in['Wck'], 'L1_attn_Wcv': _L1_attn_in['Wcv'], 'L1_attn_Wcr': _L1_attn_in['Wcr'], 'L1_ffn_gate_w': _L1_ffn_in['gate_w'], 'L1_ffn_w_gate': _L1_ffn_in['w_gate'], 'L1_ffn_w_up': _L1_ffn_in['w_up'], 'L1_ffn_w_down': _L1_ffn_in['w_down'], 'L1_ffn_sw_gate': _L1_ffn_in['sw_gate'], 'L1_ffn_sw_up': _L1_ffn_in['sw_up'], 'L1_ffn_sw_down': _L1_ffn_in['sw_down']}
    _x0 = _d['L0_attn_x']
    _d['L0_attn_x'] = jax.random.normal(jax.random.fold_in(jax.random.key(seed), 1), (8, 256, 128), dtype=_x0.dtype)
    del _x0
    return _d

def reference(L0_attn_x, L0_attn_Wq, L0_attn_Wk, L0_attn_Wv, L0_attn_Wo, L0_attn_W_feat, L0_ffn_expert_sel, L0_ffn_keys, L0_ffn_values, L1_attn_ln0_w, L1_attn_ln0_b, L1_attn_ln1_w, L1_attn_ln1_b, L1_attn_ln2_w, L1_attn_ln2_b, L1_attn_time_decay, L1_attn_time_first, L1_attn_tmk, L1_attn_tmv, L1_attn_tmr, L1_attn_Wk, L1_attn_Wv, L1_attn_Wr, L1_attn_Wo, L1_attn_cmk, L1_attn_cmr, L1_attn_Wck, L1_attn_Wcv, L1_attn_Wcr, L1_ffn_gate_w, L1_ffn_w_gate, L1_ffn_w_up, L1_ffn_w_down, L1_ffn_sw_gate, L1_ffn_sw_up, L1_ffn_sw_down):

    def _L0_attn_ref(x, Wq, Wk, Wv, Wo, W_feat):
        import math
        import jax, jax.numpy as jnp
        import numpy as np
        B, T, D_MODEL = (4, 256, 128)
        H, HD = (16, 64)
        NF = 128
        EPS = 1e-06
        INV_SQRT_NF = 1.0 / math.sqrt(NF)

        def make_orf(key, head_dim, n_features, dtype=jnp.float32):
            n_blocks = math.ceil(n_features / head_dim)
            keys = jax.random.split(key, n_blocks)
            blocks = []
            for k in keys:
                g = jax.random.normal(k, (head_dim, head_dim), dtype)
                qm, _ = jnp.linalg.qr(g)
                blocks.append(qm)
            W = jnp.concatenate(blocks, axis=1)[:, :n_features]
            return W * jnp.asarray(math.sqrt(head_dim), dtype)

        def _favor_plus(x, W):
            sq = 0.5 * jnp.sum(x * x, axis=-1, keepdims=True)
            return jnp.exp(x @ W - sq) * INV_SQRT_NF

        def _causal_linear_attention(qp, kp, v):
            Bb, Hh = (qp.shape[0], qp.shape[1])

            def step(carry, qkv):
                S, z = carry
                q_t, k_t, v_t = qkv
                S = S + jnp.einsum('bhd,bhe->bhde', k_t, v_t)
                z = z + k_t
                num = jnp.einsum('bhd,bhde->bhe', q_t, S)
                den = jnp.einsum('bhd,bhd->bh', q_t, z) + EPS
                return ((S, z), num / den[..., None])
            S0 = jnp.zeros((Bb, Hh, NF, HD), qp.dtype)
            z0 = jnp.zeros((Bb, Hh, NF), qp.dtype)
            xs = (jnp.moveaxis(qp, 2, 0), jnp.moveaxis(kp, 2, 0), jnp.moveaxis(v, 2, 0))
            _, ys = jax.lax.scan(step, (S0, z0), xs)
            return jnp.moveaxis(ys, 0, 2)
        Bb, Tt, _ = x.shape

        def heads(W):
            return (x @ W).reshape(Bb, Tt, H, HD).transpose(0, 2, 1, 3)
        q, k, v = (heads(Wq), heads(Wk), heads(Wv))
        qp = _favor_plus(q, W_feat)
        kp = _favor_plus(k, W_feat)
        y = _causal_linear_attention(qp, kp, v)
        y = y.transpose(0, 2, 1, 3).reshape(Bb, Tt, H * HD)
        return y @ Wo

    def _L0_ffn_ref(x, expert_sel, keys, values):
        import jax, jax.numpy as jnp
        import numpy as np
        DMODEL = 128
        N_EXPERTS = 32
        EXPERT_SIZE = 64
        N_HEADS = 4
        WEIGHT_SCALE = 1.0
        B, S, D = x.shape
        xt = x.reshape(-1, D)
        N = xt.shape[0]
        sel_logits = jnp.einsum('nd,ed->ne', xt, expert_sel)
        gates = jax.nn.sigmoid(sel_logits)
        sel_val, sel_idx = jax.lax.top_k(gates, N_HEADS)
        gate_full = jnp.zeros_like(gates).at[jnp.arange(N)[:, None], sel_idx].set(sel_val)
        scores = jax.nn.relu(jnp.einsum('nd,edf->nef', xt, keys))
        scores = scores * gate_full[:, :, None]
        out = jnp.einsum('nef,efv->nv', scores, values)
        return out.reshape(B, S, -1)

    def _L1_attn_ref(x, ln0_w, ln0_b, ln1_w, ln1_b, ln2_w, ln2_b, time_decay, time_first, tmk, tmv, tmr, Wk, Wv, Wr, Wo, cmk, cmr, Wck, Wcv, Wcr):
        import jax, jax.numpy as jnp
        import numpy as np
        from jax import lax
        L, B, T, C, F = (4, 4, 256, 128, 512)
        EPS = 1e-05

        def layernorm(x, w, b):
            m = jnp.mean(x, axis=-1, keepdims=True)
            v = jnp.var(x, axis=-1, keepdims=True)
            return (x - m) * lax.rsqrt(v + EPS) * w + b

        def time_shift(x):
            return jnp.pad(x, ((0, 0), (1, 0), (0, 0)))[:, :-1]

        def wkv(time_decay, time_first, k, v):
            w = -jnp.exp(time_decay)
            u = time_first
            kt = jnp.swapaxes(k, 0, 1)
            vt = jnp.swapaxes(v, 0, 1)
            Bn, Cn = (k.shape[0], k.shape[2])
            init = (jnp.zeros((Bn, Cn), k.dtype), jnp.zeros((Bn, Cn), k.dtype), jnp.full((Bn, Cn), -1e+38, k.dtype))

            def step(carry, kv):
                aa, bb, pp = carry
                kk, vv = kv
                ww = u + kk
                qq = jnp.maximum(pp, ww)
                e1 = jnp.exp(pp - qq)
                e2 = jnp.exp(ww - qq)
                out = (e1 * aa + e2 * vv) / (e1 * bb + e2)
                ww2 = pp + w
                qq2 = jnp.maximum(ww2, kk)
                e1b = jnp.exp(ww2 - qq2)
                e2b = jnp.exp(kk - qq2)
                return ((e1b * aa + e2b * vv, e1b * bb + e2b, qq2), out)
            _, out = lax.scan(step, init, (kt, vt))
            return jnp.swapaxes(out, 0, 1)
        x = layernorm(x, ln0_w, ln0_b)
        for l in range(L):
            h = layernorm(x, ln1_w[l], ln1_b[l])
            hh = time_shift(h)
            xk = h * tmk[l] + hh * (1 - tmk[l])
            xv = h * tmv[l] + hh * (1 - tmv[l])
            xr = h * tmr[l] + hh * (1 - tmr[l])
            k = jnp.einsum('btc,oc->bto', xk, Wk[l])
            v = jnp.einsum('btc,oc->bto', xv, Wv[l])
            sr = jax.nn.sigmoid(jnp.einsum('btc,oc->bto', xr, Wr[l]))
            rwkv = sr * wkv(time_decay[l], time_first[l], k, v)
            x = x + jnp.einsum('bto,co->btc', rwkv, Wo[l])
            h = layernorm(x, ln2_w[l], ln2_b[l])
            hh = time_shift(h)
            xk = h * cmk[l] + hh * (1 - cmk[l])
            xr = h * cmr[l] + hh * (1 - cmr[l])
            kf = jnp.einsum('btc,fc->btf', xk, Wck[l])
            kf = jnp.square(jax.nn.relu(kf))
            kv = jnp.einsum('btf,cf->btc', kf, Wcv[l])
            x = x + jax.nn.sigmoid(jnp.einsum('btc,oc->bto', xr, Wcr[l])) * kv
        return x

    def _L1_ffn_ref(x, gate_w, w_gate, w_up, w_down, sw_gate, sw_up, sw_down):
        import jax, jax.numpy as jnp
        import numpy as np
        B, L, D = (4, 128, 128)
        E, H, K = (16, 64, 8)
        EPS = 1e-12

        def _l2norm(v, axis=-1):
            n = jnp.sqrt(jnp.sum(v * v, axis=axis, keepdims=True))
            return v / jnp.maximum(n, EPS)
        if __name__ == '__main__':
            out = reference(**setup_inputs())
            print(out.shape)
        b, l, d = x.shape
        xf = x.reshape(-1, d)
        logits = _l2norm(xf) @ _l2norm(gate_w).T
        scores = jax.nn.sigmoid(logits)
        topk_scores, topk_idx = jax.lax.top_k(scores, K)
        topk_w = topk_scores / jnp.sum(topk_scores, axis=-1, keepdims=True)
        combine = jnp.sum(jax.nn.one_hot(topk_idx, E, dtype=xf.dtype) * topk_w[..., None], axis=1)
        g = jnp.einsum('nd,edh->neh', xf, w_gate)
        u = jnp.einsum('nd,edh->neh', xf, w_up)
        y = jnp.einsum('neh,ehd->ned', jax.nn.silu(g) * u, w_down)
        routed = jnp.einsum('ned,ne->nd', y, combine)
        shared = jax.nn.silu(xf @ sw_gate) * (xf @ sw_up) @ sw_down
        return (routed + shared).reshape(b, l, d)
    x = L0_attn_x
    x = x + _L0_attn_ref(_layernorm(x, axis=-1), L0_attn_Wq, L0_attn_Wk, L0_attn_Wv, L0_attn_Wo, L0_attn_W_feat)
    x = x + _L0_ffn_ref(_layernorm(x, axis=-1), L0_ffn_expert_sel, L0_ffn_keys, L0_ffn_values)
    x = x + _L1_attn_ref(_layernorm(x, axis=-1), L1_attn_ln0_w, L1_attn_ln0_b, L1_attn_ln1_w, L1_attn_ln1_b, L1_attn_ln2_w, L1_attn_ln2_b, L1_attn_time_decay, L1_attn_time_first, L1_attn_tmk, L1_attn_tmv, L1_attn_tmr, L1_attn_Wk, L1_attn_Wv, L1_attn_Wr, L1_attn_Wo, L1_attn_cmk, L1_attn_cmr, L1_attn_Wck, L1_attn_Wcv, L1_attn_Wcr)
    x = x + _L1_ffn_ref(_layernorm(x, axis=-1), L1_ffn_gate_w, L1_ffn_w_gate, L1_ffn_w_up, L1_ffn_w_down, L1_ffn_sw_gate, L1_ffn_sw_up, L1_ffn_sw_down)
    return x

_drawn_inputs = setup_inputs


def setup_inputs(seed=0):
    import zlib

    import numpy as np

    out = dict(_drawn_inputs(seed))
    spreads = {'L1_attn_ln0_w': (1.0, 0.2),
     'L1_attn_ln0_b': (0.0, 0.1),
     'L1_attn_ln1_w': (1.0, 0.6),
     'L1_attn_ln1_b': (0.0, 0.8),
     'L1_attn_ln2_w': (1.0, 0.6),
     'L1_attn_ln2_b': (0.0, 0.8)}
    factors = {'L1_attn_time_decay': 8.0,
     'L1_attn_time_first': 8.0,
     'L1_attn_tmk': 8.0,
     'L1_attn_tmv': 8.0,
     'L1_attn_tmr': 8.0,
     'L1_attn_Wk': 8.0,
     'L1_attn_Wv': 3.435,
     'L1_attn_Wr': 8.0,
     'L1_attn_Wo': 3.53,
     'L1_attn_cmk': 8.0,
     'L1_attn_cmr': 8.0,
     'L1_attn_Wck': 5.207,
     'L1_attn_Wcv': 4.698,
     'L1_attn_Wcr': 8.0,
     'L1_ffn_gate_w': 8.0,
     'L1_ffn_w_gate': 8.0,
     'L1_ffn_w_up': 8.0,
     'L1_ffn_w_down': 8.0,
     'L1_ffn_sw_gate': 8.0,
     'L1_ffn_sw_up': 8.0,
     'L1_ffn_sw_down': 8.0}
    for name, (base, spread) in spreads.items():
        noise = np.random.default_rng([zlib.crc32(name.encode()), seed]).standard_normal(out[name].shape)
        drawn = base * np.exp(spread * noise) if base else spread * noise
        out[name] = jnp.asarray(drawn.astype(out[name].dtype))
    for name, factor in factors.items():
        out[name] = (out[name] * factor).astype(out[name].dtype)
    return out
```

```python
from contextlib import ExitStack

import concourse.bass as bass
from concourse import mybir

F32 = mybir.dt.float32
BF16 = mybir.dt.bfloat16
ALU = mybir.AluOpType
ACT = mybir.ActivationFunctionType
AX = mybir.AxisListType

P = 128
B, T = 8, 256
N = B * T
G = 512
NG = N // G
NT = G // P
SEQ = G // T
H, HD, NF = 16, 64, 128
NP = H // 2
E0, K0 = 32, 4
C0 = E0 // 2
E1, K1 = 16, 8
C1 = E1 // 2 + 1
L = 4
FC = 4
T1 = T + 1
NVEC = 12
LNW, LNB, MK, MV, MR, DECAY, FIRST, LN2W, LN2B, CMK, CMR = range(11)
LN_EPS = 1e-5
DEN_EPS = 1e-6 * NF
NORM_EPS2 = 1e-24
SIG_MIN = -80.0
FAR = -1e38
TAKEN = 3e38
UNUSED = -3e38

PER_GROUP = [
    (2 * NT, ["v_done", "v_evac"]),
    (NP, ["yt_done", "yt_copied", "wo_done"]),
    (16, ["proj_done", "stack_odd", "stack_even", "odd_copied", "av_done", "ynormed",
         "up_done", "gbc_done", "relu_done", "h_done", "down_done"]),
    (32, ["feat_done", "feat_exp", "score_done", "masked", "den_ready"]),
    (C1, ["g_done", "u_done", "silu_done", "su_done", "h1_done", "down1_done"]),
    (C1 - 1, ["cbc_done"]),
    (3, ["gate_norm"]),
    (2, ["logit_scaled"]),
    (1, ["ng_ready", "x1_added", "x2_added", "y_added", "rng_ready", "logit_done", "logit_copied", "logit_bounded",
        "top_found", "top_packed", "top_replaced", "gate_exp", "gate_sum", "gate_recip", "gate_mask",
        "gate_masked", "part_hi", "part_r1", "part_mid", "parts_ready", "gt_done", "gt_copied", "sq_ready",
        "ss_guard", "ss_inv"]),
]
SEMS = [
    "x_in", "wqkv_in", "wfeat_in", "wo_in", "const_in", "sel0_in", "keys_in", "vals_in", "wrwkv_in", "vec_in",
    "rgate_in", "wgu_in", "wdn_in", "shared_in", "esel_in", "sel1_in",
    "ln_centered", "ln_squared", "ln_var", "ln_logged", "ln_rstd", "ln_normed",
    "const_ready", "sel_ready", "ones_ready",
    "ng_ready", "v_done", "v_evac", "proj_done", "stack_odd", "stack_even", "odd_copied", "feat_done", "feat_exp",
    "score_done", "masked", "av_done", "den_ready", "ynormed", "yt_done", "yt_copied", "wo_done", "x1_added",
    "rng_ready", "logit_done", "logit_copied", "logit_bounded", "top_found", "top_packed", "top_replaced", "gate_exp", "gate_sum",
    "gate_recip", "gate_mask", "gate_masked", "gate_norm", "part_hi", "part_r1", "part_mid", "part_r2", "parts_ready", "gt_done", "gt_copied",
    "up_done", "gbc_done", "relu_done", "h_done", "down_done", "x2_added",
    "ln0_affined",
    "centered1", "squared1", "var1", "logged1", "rstd1", "normed1", "affined1", "diff1", "mixed1", "kvr_done",
    "k_copied", "v_copied", "r_copied", "r_bounded", "r_exp", "decay_exp", "decay_neg", "decay_bc",
    "p_scanned", "a1_done", "a2_done", "d1_done", "d_below", "d_above", "e3_done", "e4_done", "e1_done", "e2_done", "kv_done",
    "aa_scanned", "bb_scanned", "t1_done", "t2_done", "num_done", "t3_done", "den_done", "den2_done", "rec_done",
    "rw_done", "o_done", "x_mid",
    "centered2", "squared2", "var2", "logged2", "rstd2", "normed2", "affined2", "diff2", "mixed2",
    "ck_done", "ck_relu", "ck_squared", "cr_done", "cr_copied", "cr_bounded", "cr_exp", "cr_sum", "cr_recip", "cv_done", "kv_gated", "x_out",
    "gw_sq", "gw_ss", "gw_guard", "gw_inv", "sq_ready", "ss_guard", "ss_inv", "logit_scaled", "x3_added",
    "g_done", "u_done", "cbc_done", "silu_done", "su_done", "h1_done", "down1_done", "y_added", "out_stored",
]


def two_blocks(nc, ins, out):
    with ExitStack() as ctx:
        def sb(name, shape, dt=F32):
            return ctx.enter_context(nc.sbuf_tensor(name, shape, dt))

        S = {name: ctx.enter_context(nc.semaphore(name)) for name in SEMS}
        bank = [ctx.enter_context(nc.psum_tensor(f"bank{i}", [P, G], F32)) for i in range(8)]

        x = sb("x", [P, N])
        nrm = sb("nrm", [P, N])
        ng = sb("ng", [P, G])
        wq, wk, wv = (sb(n, [P, H * HD]) for n in ("wq", "wk", "wv"))
        wfeat = sb("wfeat", [P, 2, NF])
        wo = sb("wo", [P, NP, P])
        consts = sb("consts", [P, 4 * P + 3 * P])
        center, mean, ident, ones = (consts[:, i * P:(i + 1) * P] for i in range(4))
        causal = consts[:, 4 * P:7 * P]
        esel = sb("esel", [P, E0])
        big = sb("big", [P, 4096 + 2 * C1 * P + C1 * P])
        keys = big[:, 0:E0 * 64]
        vals = big[:, E0 * 64:E0 * 64 + C0 * P].rearrange("p (c d) -> p c d", c=C0)
        wrwkv = sb("wrwkv", [P, L, 13, P])
        vec = sb("vec", [P, L + 1, NVEC])
        rgate = sb("rgate", [P, E1])
        wgu = big[:, 4096:4096 + 2 * C1 * P].rearrange("p (s e) -> p s e", s=2)
        wdn = big[:, 4096 + 2 * C1 * P:4096 + 2 * C1 * P + C1 * P].rearrange("p (c d) -> p c d", c=C1)
        sel = sb("sel", [3 * E0, C0 * P], BF16)
        self32 = sb("self32", [3 * E0, C0 * P])
        lnsq = sb("lnsq", [P, NG, G])
        lnr = sb("lnr", [P, NG, G])
        gt = sb("gt", [3 * E0, N], BF16)

        stack = sb("stack", [P, 2, 2, G])
        feat = sb("feat", [P, 2, 2, 2, G])
        v_aug = sb("v_aug", [P, NT, H, HD + 1])
        scores = sb("scores", [P, 4, 3 * P])
        den = sb("den", [P, 2, 4])
        rden = sb("rden", [P, 2, 4])
        ynorm = sb("ynorm", [P, NT, 2, HD])
        yt = sb("yt", [P, G])

        lg = sb("lg", [P, NT, E0 + 4])
        ex = sb("ex", [P, NT, E0])
        gs = sb("gs", [P, NT, E0])
        gr = sb("gr", [P, NT, E0])
        top = sb("top", [P, NT, 8])
        top2 = sb("top2", [P, NT, 8])
        repl = sb("repl", [P, NT, E0 + 4])
        msk = sb("msk", [P, NT, E0])
        gm = sb("gm", [P, NT, E0])
        gn = sb("gn", [P, NT, E0])
        gsum = sb("gsum", [P, NT])
        gsr = sb("gsr", [P, NT])
        r1 = sb("r1", [P, NT, E0])
        r2 = sb("r2", [P, NT, E0])
        parts = sb("parts", [P, NT, 3 * E0], BF16)
        identb = sb("identb", [P, P], BF16)
        hr = sb("hr", [P, 2, G])
        hh = sb("hh", [P, 3, G])

        minus_half = sb("minus_half", [P, E1])
        expdec = sb("expdec", [P, L])
        negdec = sb("negdec", [P, L])

        def ones_half(n):
            return minus_half[:, 0:n]

        def dec_col(l):
            return expdec[:, l:l + 1]

        def fixed(eng):
            eng.wait_ge(S["const_in"], 16)

        def Ccol(i):
            return vec[:, L, i:i + 1]

        block = ctx.enter_context(nc.Block())

        dram = ins

        @block.sync
        def _(sp):
            sp.dma_start(x[:, :], dram["x"]).then_inc(S["x_in"], 16)
            sp.dma_start(consts[:, :], dram["consts"]).then_inc(S["const_in"], 16)
            sp.dma_start(wv[:, :], dram["wv"]).then_inc(S["wqkv_in"], 16)
            sp.dma_start(wq[:, :], dram["wq"]).then_inc(S["wqkv_in"], 16)
            sp.dma_start(wk[:, :], dram["wk"]).then_inc(S["wqkv_in"], 16)
            sp.dma_start(wfeat[:, :, :], dram["wfeat"]).then_inc(S["wfeat_in"], 16)
            sp.dma_start(wo[:, :, :], dram["wo"]).then_inc(S["wo_in"], 16)
            sp.dma_start(vec[:, :, :], dram["vec"]).then_inc(S["vec_in"], 16)
            sp.dma_start(esel[:, :], dram["esel"]).then_inc(S["esel_in"], 16)
            sp.dma_start(self32[:, :], dram["sel0"]).then_inc(S["sel0_in"], 16)
            sp.dma_start(keys, dram["keys"]).then_inc(S["keys_in"], 16)
            sp.dma_start(vals, dram["vals"]).then_inc(S["vals_in"], 16)
            sp.dma_start(wrwkv[:, :, :, :], dram["wrwkv"]).then_inc(S["wrwkv_in"], 16)
            sp.dma_start(rgate[:, :], dram["rgate"]).then_inc(S["rgate_in"], 16)
            sp.dma_start(wgu, dram["wgu"]).then_inc(S["wgu_in"], 16)
            sp.dma_start(wdn, dram["wdn"]).then_inc(S["wdn_in"], 16)
            sp.wait_ge(S["sel_ready"], 1)
            sp.dma_start(self32[0:3 * E1, 0:(C1 - 1) * P], dram["sel1"]).then_inc(S["sel1_in"], 16)
            with sp.Fori(1, NG + 1) as g:
                sp.wait_ge(S["y_added"], g + 1)
                sp.dma_start(out[:, bass.ds((g - 1) * G, G)], x[:, bass.ds((g - 1) * G, G)]).then_inc(S["out_stored"], 16)
            sp.wait_ge(S["out_stored"], 16 * NG)

        rs = sb("rs", [P, N])
        h1 = stack[:, :, :, :].rearrange("p a b c -> p (a b c)")[:, 0:SEQ * T1].rearrange("p (s t) -> p s t", s=SEQ)
        h2 = stack[:, :, :, :].rearrange("p a b c -> p (a b c)")[:, 1024:1024 + SEQ * T1].rearrange("p (s t) -> p s t", s=SEQ)
        fb = feat[:, :, :, :, :].rearrange("p a b c d -> p (a b c) d")
        va = v_aug[:, :, :, :].rearrange("p a b c -> p (a b c)")
        hn1, dif1 = fb[:, 0, :], fb[:, 1, :]
        xk, xv, xr = fb[:, 2, :], fb[:, 3, :], fb[:, 4, :]
        hn2, dif2 = fb[:, 5, :], fb[:, 6, :]
        xck = fb[:, 7, :]
        xcr = yt[:, :]
        kp = [va[:, i * 514:(i + 1) * 514] for i in range(2)]
        vs = [va[:, 1028 + i * G:1028 + (i + 1) * G] for i in range(2)]
        er = [va[:, 2052 + i * G:2052 + (i + 1) * G] for i in range(2)]
        pm = va[:, 3076:3076 + 514]
        dec = va[:, 3590:3590 + 514]
        W2 = SEQ * T1
        d2 = big[:, 6 * W2:6 * W2 + G]
        e3b = big[:, 0 * W2:1 * W2]
        e4b = big[:, 1 * W2:2 * W2]
        kvb = big[:, 2 * W2:3 * W2]
        aa = big[:, 3 * W2:4 * W2]
        bb = big[:, 4 * W2:5 * W2]
        reset = big[:, 5 * W2:6 * W2]
        a1, a2 = wq[:, 0:G], wq[:, G:2 * G]
        d1, e1 = wk[:, 0:G], wk[:, G:2 * G]
        e2, t1 = wv[:, 0:G], wv[:, G:2 * G]
        wof = wo[:, :, :].rearrange("p a b -> p (a b)")
        t2, t3 = wof[:, 0:G], wof[:, G:2 * G]
        scf = scores[:, :, :].rearrange("p a b -> p (a b)")
        dn, dn2, rec = scf[:, 0:G], scf[:, G:2 * G], scf[:, 2 * G:3 * G]
        num = hr[:, 0, :]
        rw = hr[:, 1, :]
        ckr = lnsq
        sq1, rs1 = hh[:, 0, :], hh[:, 1, :]
        sq2, rs2 = hh[:, 2, :], ng[:, :]
        ecr = lnr[:, 0, :]
        scr = lnr[:, 1, :]
        rcr = lnr[:, 2, :]
        kvg = lnr[:, 3, :]

        def seqs(ap):
            return ap.rearrange("p (s t) -> p s t", s=SEQ)

        def cur(buf):
            return buf.rearrange("p (s t) -> p s t", s=SEQ)[:, :, 1:T1]

        def prev(buf):
            return buf.rearrange("p (s t) -> p s t", s=SEQ)[:, :, 0:T]

        ITEMS = L * NG
        STEPS = ITEMS + 2

        @block.tensor
        def _(pe):
            def layernorm(first, src, ready):
                for g in range(NG):
                    ready(pe, g)
                    pe.matmul(bank[g][:, :], center, src[:, g * G:(g + 1) * G], start=True,
                              stop=True).then_inc(S["ln_centered"], 1)
                for g in range(NG):
                    pe.wait_ge(S["ln_squared"], first + g + 1)
                    pe.matmul(bank[4 + g][:, :], mean, lnsq[:, g, :], start=True,
                              stop=True).then_inc(S["ln_var"], 1)

            pe.wait_ge(S["const_in"], 16)
            pe.wait_ge(S["x_in"], 16)
            layernorm(0, x, lambda e, g: None)

            pe.wait_ge(S["ln_normed"], NG)
            pe.wait_ge(S["wqkv_in"], 48)
            pe.wait_ge(S["wfeat_in"], 16)
            pe.wait_ge(S["wo_in"], 16)
            PROJ, FEAT, SC, AV, YT, OUT = (0, 1), (2, 3), 4, 5, 6, 7
            with pe.Fori(1, NG + 1) as g:
                pe.wait_ge(S["ng_ready"], g + 1)
                for u in range(2 * NT):
                    if u < 2:
                        pe.wait_ge(S["stack_odd"], 16 * g)
                        pe.wait_ge(S["stack_even"], 16 * g)
                    else:
                        pe.wait_ge(S["v_evac"], 8 * g + u - 1)
                    pe.matmul(bank[PROJ[u % 2]][:, :], ng[:, (u // 2) * P:(u // 2 + 1) * P],
                              wv[:, (u % 2) * G:(u % 2 + 1) * G], start=True, stop=True).then_inc(S["v_done"], 1)

                def proj(p, s):
                    if p == 0:
                        pe.wait_ge(S["v_evac"], 8 * g + 7 + s)
                    else:
                        pe.wait_ge(S["stack_odd"], 16 * g + 2 * (p - 1) + s + 1)
                        pe.wait_ge(S["stack_even"], 16 * g + 2 * (p - 1) + s + 1)
                    w = wq if s == 0 else wk
                    pe.matmul(bank[PROJ[s]][:, :], w[:, p * P:(p + 1) * P], ng[:, :], start=True,
                              stop=True).then_inc(S["proj_done"], 1)

                def features(p, s, h):
                    f = 4 * p + 2 * s + h
                    pe.wait_ge(S["stack_odd"], 16 * g + 2 * p + s + 1)
                    pe.wait_ge(S["stack_even"], 16 * g + 2 * p + s + 1)
                    pe.wait_ge(S["feat_exp"], 32 * g + max(f - 1, 0))
                    pe.matmul(bank[FEAT[f % 2]][:, :], wfeat[:, h, :], stack[:, s, h, :], start=True,
                              stop=True).then_inc(S["feat_done"], 1)

                def score(p, i):
                    b, h = i // 2, i % 2
                    fq, fk = feat[:, p % 2, 0, h, :], feat[:, p % 2, 1, h, :]
                    pe.wait_ge(S["feat_exp"], 32 * g + 4 * p + 4)
                    pe.wait_ge(S["masked"], 32 * g + 4 * p + i)
                    pe.matmul(bank[SC][:, 0:T], fk[:, b * T:b * T + P], fq[:, b * T:(b + 1) * T],
                              start=True, stop=True)
                    pe.matmul(bank[SC][:, T:T + P], fk[:, b * T + P:(b + 1) * T],
                              fq[:, b * T + P:(b + 1) * T], start=True, stop=True).then_inc(S["score_done"], 1)

                def attend(p, b):
                    pe.wait_ge(S["masked"], 32 * g + 4 * p + 2 * b + 2)
                    pe.wait_ge(S["ynormed"], 16 * g + 2 * p + b)
                    W = HD + 1
                    for h in range(2):
                        sc = scores[:, 2 * b + h, :]
                        o = bank[AV][:, 2 * h * W:(2 * h + 1) * W]
                        pe.matmul(o, sc[:, 0:P], v_aug[:, 2 * b, 2 * p + h, :], start=True, stop=True)
                        o = bank[AV][:, (2 * h + 1) * W:(2 * h + 2) * W]
                        pe.matmul(o, sc[:, P:2 * P], v_aug[:, 2 * b, 2 * p + h, :], start=True, stop=False)
                        mm = pe.matmul(o, sc[:, 2 * P:3 * P], v_aug[:, 2 * b + 1, 2 * p + h, :],
                                       start=False, stop=True)
                    mm.then_inc(S["av_done"], 1)

                def turn(p):
                    pe.wait_ge(S["ynormed"], 16 * g + 2 * p + 2)
                    pe.wait_ge(S["yt_copied"], 8 * g + p)
                    for t in range(NT):
                        mm = pe.transpose(bank[YT][:, t * P:(t + 1) * P],
                                          ynorm[:, t, :, :].rearrange("p h e -> p (h e)"), ident)
                    mm.then_inc(S["yt_done"], 1)

                def project_out(p):
                    pe.wait_ge(S["yt_copied"], 8 * g + p + 1)
                    if p == 0:
                        pe.wait_ge(S["x1_added"], g)
                    pe.matmul(bank[OUT][:, :], wo[:, p, :], yt[:, :], start=(p == 0),
                              stop=(p == NP - 1)).then_inc(S["wo_done"], 1)

                pe.wait_ge(S["v_evac"], 8 * g + 8)
                for p in range(NP + 2):
                    a, c, d = p < NP, 1 <= p <= NP, p >= 2
                    if c:
                        score(p - 1, 0)
                    if d:
                        turn(p - 2)
                    if a:
                        proj(p, 0)
                    if c:
                        score(p - 1, 1)
                    if d:
                        project_out(p - 2)
                    if a:
                        proj(p, 1)
                    if c:
                        score(p - 1, 2)
                    if a:
                        features(p, 0, 0)
                    if c:
                        attend(p - 1, 0)
                        score(p - 1, 3)
                    if a:
                        features(p, 0, 1)
                        features(p, 1, 0)
                    if c:
                        attend(p - 1, 1)
                    if a:
                        features(p, 1, 1)

            pe.wait_ge(S["x1_added"], NG + 1)
            layernorm(NG, x, lambda e, g: None)
            pe.wait_ge(S["ln_normed"], 2 * NG)
            pe.wait_ge(S["esel_in"], 16)

            def routing(base, cols, E, w):
                with pe.Fori(1, NG + 1) as g:
                    pe.wait_ge(S["rng_ready"], base + g + 1)
                    pe.wait_ge(S["logit_copied"], base + g)
                    if E == E1:
                        pe.wait_ge(S["sq_ready"], g + 1)
                    for t in range(NT):
                        mm = pe.matmul(bank[0][:, t * cols:t * cols + E], ng[:, t * P:(t + 1) * P], w,
                                       start=True, stop=True)
                        if E == E1:
                            mm = pe.matmul(bank[0][:, t * cols + E:t * cols + E + 1], lnsq[:, 0, t * P:(t + 1) * P],
                                           ones[:, 0:1], start=True, stop=True)
                    mm.then_inc(S["logit_done"], 1)
                    fixed(pe)
                    pe.wait_ge(S["parts_ready"], base + g + 1)
                    pe.wait_ge(S["gt_copied"], base + g)
                    for t in range(NT):
                        mm = pe.transpose(bank[1][0:3 * E, :].bitcast(BF16)[:, t * P:(t + 1) * P],
                                          parts[:, t, 0:3 * E], identb[:, :])
                    mm.then_inc(S["gt_done"], 1)

            routing(0, E0, E0, esel[:, :])
            pe.wait_ge(S["gt_copied"], NG + 1)
            pe.wait_ge(S["keys_in"], 16)
            pe.wait_ge(S["vals_in"], 16)
            pe.wait_ge(S["sel_ready"], 1)
            with pe.Fori(1, NG + 1) as g:
                def up(c):
                    pe.wait_ge(S["relu_done"], 16 * g + max(c - 1, 0))
                    pe.matmul(bank[2 + c % 2][:, :], keys[:, c * P:(c + 1) * P], nrm[:, bass.ds((g - 1) * G, G)],
                              start=True, stop=True).then_inc(S["up_done"], 1)
                    pe.wait_ge(S["h_done"], 16 * g + max(c - 1, 0))
                    pe.matmul(bank[4 + c % 2][:, :], sel[:, c * P:(c + 1) * P], gt[:, bass.ds((g - 1) * G, G)],
                              start=True, stop=True).then_inc(S["gbc_done"], 1)

                def down(c):
                    if c == 0:
                        pe.wait_ge(S["x2_added"], g)
                    pe.wait_ge(S["h_done"], 16 * g + c + 1)
                    pe.matmul(bank[6][:, :], vals[:, c, :], hh[:, c % 3, :], start=(c == 0),
                              stop=(c == C0 - 1)).then_inc(S["down_done"], 1)

                for c in range(C0 + 2):
                    if c < C0:
                        up(c)
                    if c >= 2:
                        down(c - 2)

            pe.wait_ge(S["x2_added"], NG + 1)
            layernorm(2 * NG, x, lambda e, g: None)
            layernorm(3 * NG, nrm, lambda e, g: e.wait_ge(S["ln_normed"], 3 * NG if g == 0 else 3 * NG))

            pe.wait_ge(S["wrwkv_in"], 16)
            pe.wait_ge(S["ln_normed"], 4 * NG)
            CEN1, CEN2, VAR, OV, KCR, RCV = 0, 1, 2, 3, 4, 5

            def enter_a(n):
                if n < NG:
                    pe.wait_ge(S["ln0_affined"], n + 1)
                else:
                    pe.wait_ge(S["x_out"], n - NG + 1)
                if n >= 1:
                    pe.wait_ge(S["normed1"], n)
                g = n % NG
                pe.matmul(bank[CEN1][:, :], center, rs[:, g * G:(g + 1) * G], start=True,
                          stop=True).then_inc(S["centered1"], 1)

            def enter_b(n):
                pe.wait_ge(S["squared1"], n + 1)
                if n >= 3:
                    pe.wait_ge(S["logged2"], n - 2)
                pe.matmul(bank[VAR][:, :], mean, sq1, start=True, stop=True).then_inc(S["var1"], 1)

            def enter_c(n):
                l = n // NG
                if n >= 2:
                    pe.wait_ge(S["x_mid"], n - 1)
                    if n >= 3:
                        pe.wait_ge(S["cr_copied"], n - 2)
                        pe.wait_ge(S["kv_gated"], n - 2)
                for i, (b, src) in enumerate(((KCR, xk), (OV, xv), (RCV, xr))):
                    pe.wait_ge(S["mixed1"], 3 * n + i + 1)
                    if n >= 1 and b == KCR:
                        pe.wait_ge(S["k_copied"], n)
                    if n >= 1 and b == OV:
                        pe.wait_ge(S["v_copied"], n)
                    if n >= 1 and b == RCV:
                        pe.wait_ge(S["r_copied"], n)
                    pe.matmul(bank[b][:, :], wrwkv[:, l, i, :], src, start=True, stop=True).then_inc(S["kvr_done"], 1)

            def leave_o(n):
                pe.wait_ge(S["rw_done"], n + 1)
                pe.wait_ge(S["v_copied"], min(n + 2, ITEMS))
                pe.matmul(bank[OV][:, :], wrwkv[:, n // NG, 3, :], rw, start=True, stop=True).then_inc(S["o_done"], 1)

            def leave_a(n):
                pe.wait_ge(S["x_mid"], n + 1)
                if n >= 1:
                    pe.wait_ge(S["normed2"], n)
                g = n % NG
                pe.matmul(bank[CEN2][:, :], center, rs[:, g * G:(g + 1) * G], start=True,
                          stop=True).then_inc(S["centered2"], 1)

            def leave_b(n):
                pe.wait_ge(S["squared2"], n + 1)
                pe.wait_ge(S["logged1"], min(n + 3, ITEMS))
                pe.matmul(bank[VAR][:, :], mean, sq2, start=True, stop=True).then_inc(S["var2"], 1)

            def leave_c(n):
                l = n // NG
                pe.wait_ge(S["mixed2"], 2 * n + 1)
                pe.wait_ge(S["k_copied"], min(n + 3, ITEMS))
                pe.matmul(bank[KCR][:, :], wrwkv[:, l, 8, :], xcr, start=True, stop=True).then_inc(S["cr_done"], 1)
                pe.wait_ge(S["mixed2"], 2 * n + 2)
                for j in range(FC):
                    if 4 * n + j >= 2:
                        pe.wait_ge(S["ck_relu"], 4 * n + j - 1)
                    pe.matmul(bank[6 + j % 2][:, :], wrwkv[:, l, 4 + j, :], xck, start=True,
                              stop=True).then_inc(S["ck_done"], 1)
                pe.wait_ge(S["r_copied"], min(n + 3, ITEMS))
                for j in range(FC):
                    pe.wait_ge(S["ck_squared"], 4 * n + j + 1)
                    mm = pe.matmul(bank[RCV][:, :], wrwkv[:, l, 9 + j, :], ckr[:, j, :], start=(j == 0),
                                   stop=(j == FC - 1))
                mm.then_inc(S["cv_done"], 1)

            for s in range(STEPS):
                a, c = s < ITEMS, s >= 2
                if c:
                    leave_o(s - 2)
                if a:
                    enter_a(s)
                if c:
                    leave_a(s - 2)
                if a:
                    enter_b(s)
                if c:
                    leave_b(s - 2)
                if a:
                    enter_c(s)
                if c:
                    leave_c(s - 2)

            pe.wait_ge(S["x3_added"], NG)
            layernorm(4 * NG, x, lambda e, g: None)
            pe.wait_ge(S["ln_normed"], 5 * NG)
            pe.wait_ge(S["gw_sq"], 1)
            pe.matmul(bank[7][:, 0:E1], ones, msk[:, 0, 0:E1], start=True, stop=True).then_inc(S["gw_ss"], 1)
            routing(NG, E1 + 1, E1, rgate[:, :])
            pe.wait_ge(S["gt_copied"], 2 * NG + 1)
            pe.wait_ge(S["wgu_in"], 16)
            pe.wait_ge(S["wdn_in"], 16)
            pe.wait_ge(S["sel_ready"], 2)
            with pe.Fori(1, NG + 1) as g:
                def up1(c):
                    m = P
                    fixed(pe)
                    pe.wait_ge(S["silu_done"], C1 * g + max(c - 1, 0))
                    pe.matmul(bank[0 + c % 2][0:m, :], wgu[:, 0, c * P:c * P + m], nrm[:, bass.ds((g - 1) * G, G)],
                              start=True, stop=True).then_inc(S["g_done"], 1)
                    fixed(pe)
                    pe.wait_ge(S["su_done"], C1 * g + max(c - 1, 0))
                    pe.matmul(bank[2 + c % 2][0:m, :], wgu[:, 1, c * P:c * P + m], nrm[:, bass.ds((g - 1) * G, G)],
                              start=True, stop=True).then_inc(S["u_done"], 1)
                    if c < C1 - 1:
                        fixed(pe)
                        pe.wait_ge(S["h1_done"], C1 * g + max(c - 1, 0))
                        pe.matmul(bank[4 + c % 2][:, :], sel[0:3 * E1, c * P:(c + 1) * P],
                                  gt[0:3 * E1, bass.ds((g - 1) * G, G)], start=True, stop=True).then_inc(S["cbc_done"], 1)

                def down1(c):
                    m = P
                    if c == 0:
                        pe.wait_ge(S["y_added"], g)
                    pe.wait_ge(S["h1_done"], C1 * g + c + 1)
                    pe.matmul(bank[6][:, :], wdn[0:m, c, :], hh[0:m, c % 3, :], start=(c == 0),
                              stop=(c == C1 - 1)).then_inc(S["down1_done"], 1)

                for c in range(C1 + 2):
                    if c < C1:
                        up1(c)
                    if c >= 2:
                        down1(c - 2)

        @block.scalar
        def _(act):
            nc.scalar.preload_act_table_set("natural_log_exp_and_others")
            act.wait_ge(S["vec_in"], 16)

            def layernorm(first):
                for g in range(NG):
                    act.wait_ge(S["ln_centered"], first + g + 1)
                    if first:
                        act.wait_ge(S["ln_var"], first)
                    act.activation(lnsq[:, g, :], bank[g][:, :], ACT.Square).then_inc(S["ln_squared"], 1)
                for g in range(NG):
                    act.wait_ge(S["ln_var"], first + g + 1)
                    if first:
                        act.wait_ge(S["ln_normed"], first)
                    act.activation(lnr[:, g, :], bank[4 + g][:, :], ACT.Ln, bias=Ccol(0)).then_inc(S["ln_logged"], 1)
                for g in range(NG):
                    act.wait_ge(S["ln_logged"], first + g + 1)
                    act.activation(lnr[:, g, :], lnr[:, g, :], ACT.Exp, scale=-0.5).then_inc(S["ln_rstd"], 1)

            layernorm(0)

            PROJ, FEAT = (0, 1), (2, 3)
            with act.Fori(1, NG + 1) as g:
                def squares(p, s):
                    act.wait_ge(S["proj_done"], 16 * g + 2 * p + s + 1)
                    act.wait_ge(S["feat_done"], 32 * g + (4 * (p - 1) + 2 * s + 2 if p else 0))
                    act.activation(stack[0:64, s, 0, :], bank[PROJ[s]][0:64, :], ACT.Identity)
                    act.activation(stack[64:128, s, 0, :], bank[PROJ[s]][0:64, :],
                                   ACT.Square).then_inc(S["stack_even"], 1)

                def exps(p):
                    for f in range(4 * p, 4 * p + 4):
                        act.wait_ge(S["feat_done"], 32 * g + f + 1)
                        act.wait_ge(S["score_done"], 32 * g + (4 * (p - 1) if p >= 2 else 0))
                        act.activation(feat[:, p % 2, (f // 2) % 2, f % 2, :], bank[FEAT[f % 2]][:, :],
                                       ACT.Exp).then_inc(S["feat_exp"], 1)

                for p in range(NP):
                    squares(p, 0)
                    squares(p, 1)
                    exps(p)

            layernorm(NG)

            def routing(base, E, src):
                with act.Fori(1, NG + 1) as g:
                    if E == E1:
                        act.wait_ge(S["rng_ready"], base + g + 1)
                        act.wait_ge(S["logit_done"], base + g)
                        act.activation(lnsq[:, 0, :], ng[:, :], ACT.Square).then_inc(S["sq_ready"], 1)
                        act.wait_ge(S["logit_scaled"], 2 * g + 2)
                    else:
                        act.wait_ge(S["logit_bounded"], base + g + 1)
                    act.wait_ge(S["gate_sum"], base + g)
                    act.activation(ex[:, :, 0:E], src[:, :, 0:E], ACT.Exp, scale=-1.0).then_inc(S["gate_exp"], 1)

            routing(0, E0, gn)
            with act.Fori(1, NG + 1) as g:
                for c in range(C0):
                    act.wait_ge(S["up_done"], 16 * g + c + 1)
                    act.wait_ge(S["h_done"], 16 * g + max(c - 1, 0))
                    act.activation(hr[:, c % 2, :], bank[2 + c % 2][:, :], ACT.Relu).then_inc(S["relu_done"], 1)

            layernorm(2 * NG)
            layernorm(3 * NG)

            for g in range(NG):
                act.wait_ge(S["ln_normed"], 3 * NG + g + 1)
                act.activation(rs[:, g * G:(g + 1) * G], nrm[:, g * G:(g + 1) * G], ACT.Identity,
                               bias=Ccol(2), scale=Ccol(1)).then_inc(S["ln0_affined"], 1)
            for l in range(L):
                act.activation(dec_col(l), vec[:, l, DECAY:DECAY + 1], ACT.Exp).then_inc(S["decay_exp"], 1)

            def enter_sq(n):
                act.wait_ge(S["centered1"], n + 1)
                if n >= 1:
                    act.wait_ge(S["var1"], n)
                act.activation(sq1, bank[0][:, :], ACT.Square).then_inc(S["squared1"], 1)

            def enter_rstd(n):
                l = n // NG
                act.wait_ge(S["var1"], n + 1)
                if n >= 1:
                    act.wait_ge(S["normed1"], n)
                act.activation(rs1, bank[2][:, :], ACT.Ln, bias=Ccol(0)).then_inc(S["logged1"], 1)
                act.wait_ge(S["logged1"], n + 1)
                act.activation(rs1, rs1, ACT.Exp, scale=-0.5).then_inc(S["rstd1"], 1)

            def enter_affine(n):
                l = n // NG
                act.wait_ge(S["normed1"], n + 1)
                if n >= 1:
                    act.wait_ge(S["mixed1"], 3 * n)
                    act.wait_ge(S["diff1"], n)
                act.activation(h1[:, :, 1:T1], seqs(hn1), ACT.Identity, bias=vec[:, l, LNB:LNB + 1],
                               scale=vec[:, l, LNW:LNW + 1]).then_inc(S["affined1"], 1)

            def enter_evac(n):
                act.wait_ge(S["kvr_done"], 3 * n + 1)
                if n >= 2:
                    act.wait_ge(S["a2_done"], n - 1)
                    act.wait_ge(S["d1_done"], n - 1)
                    act.wait_ge(S["t2_done"], n - 1)
                    act.wait_ge(S["kv_done"], n - 1)
                    act.wait_ge(S["den2_done"], n - 1)
                act.activation(cur(kp[n % 2]), seqs(bank[4][:, :]), ACT.Identity).then_inc(S["k_copied"], 1)
                act.wait_ge(S["kvr_done"], 3 * n + 2)
                act.activation(vs[n % 2], bank[3][:, :], ACT.Identity).then_inc(S["v_copied"], 1)
                act.wait_ge(S["kvr_done"], 3 * n + 3)
                act.activation(er[n % 2], bank[5][:, :], ACT.Identity).then_inc(S["r_copied"], 1)

            def scan_exps(n):
                act.wait_ge(S["a1_done"], n + 1)
                if n >= 1:
                    act.wait_ge(S["aa_scanned"], n)
                    act.wait_ge(S["bb_scanned"], n)
                act.activation(cur(e3b[:, :]), seqs(a1), ACT.Exp).then_inc(S["e3_done"], 1)
                act.wait_ge(S["a2_done"], n + 1)
                if n >= 1:
                    act.wait_ge(S["kv_done"], n)
                act.activation(cur(e4b[:, :]), seqs(a2), ACT.Exp).then_inc(S["e4_done"], 1)
                act.wait_ge(S["d_above"], n + 1)
                if n >= 1:
                    act.wait_ge(S["t1_done"], n)
                    act.wait_ge(S["t3_done"], n)
                    act.wait_ge(S["t2_done"], n)
                    act.wait_ge(S["den_done"], n)
                act.activation(e1, d1, ACT.Exp, scale=-1.0).then_inc(S["e1_done"], 1)
                act.wait_ge(S["d_below"], n + 1)
                act.activation(e2, d2, ACT.Exp).then_inc(S["e2_done"], 1)
                act.wait_ge(S["r_bounded"], n + 1)
                act.activation(er[n % 2], er[n % 2], ACT.Exp, scale=-1.0).then_inc(S["r_exp"], 1)

            def leave_sq(n):
                act.wait_ge(S["centered2"], n + 1)
                if n >= 1:
                    act.wait_ge(S["var2"], n)
                act.activation(sq2, bank[1][:, :], ACT.Square).then_inc(S["squared2"], 1)

            def leave_rstd(n):
                act.wait_ge(S["var2"], n + 1)
                if n >= 1:
                    act.wait_ge(S["normed2"], n)
                act.activation(rs2, bank[2][:, :], ACT.Ln, bias=Ccol(0)).then_inc(S["logged2"], 1)
                act.wait_ge(S["logged2"], n + 1)
                act.activation(rs2, rs2, ACT.Exp, scale=-0.5).then_inc(S["rstd2"], 1)

            def leave_affine(n):
                l = n // NG
                act.wait_ge(S["normed2"], n + 1)
                if n >= 1:
                    act.wait_ge(S["mixed2"], 2 * n)
                    act.wait_ge(S["diff2"], n)
                act.activation(h2[:, :, 1:T1], seqs(hn2), ACT.Identity, bias=vec[:, l, LN2B:LN2B + 1],
                               scale=vec[:, l, LN2W:LN2W + 1]).then_inc(S["affined2"], 1)

            def leave_relu(n):
                act.wait_ge(S["cr_done"], n + 1)
                if n >= 1:
                    act.wait_ge(S["cr_sum"], n)
                act.activation(ecr, bank[4][:, :], ACT.Identity).then_inc(S["cr_copied"], 1)
                for j in range(FC):
                    act.wait_ge(S["ck_done"], 4 * n + j + 1)
                    if n >= 1:
                        act.wait_ge(S["cv_done"], n)
                    act.activation(ckr[:, j, :], bank[6 + j % 2][:, :], ACT.Relu).then_inc(S["ck_relu"], 1)
                act.wait_ge(S["cr_bounded"], n + 1)
                act.activation(ecr, ecr, ACT.Exp, scale=-1.0).then_inc(S["cr_exp"], 1)

            for s in range(STEPS):
                a, w, c = s < ITEMS, 1 <= s <= ITEMS, s >= 2
                if a:
                    enter_sq(s)
                if c:
                    leave_sq(s - 2)
                if a:
                    enter_rstd(s)
                    enter_affine(s)
                if c:
                    leave_rstd(s - 2)
                    leave_affine(s - 2)
                if w:
                    scan_exps(s - 1)
                if a:
                    enter_evac(s)
                if c:
                    leave_relu(s - 2)

            layernorm(4 * NG)
            routing(NG, E1, lg)
            with act.Fori(1, NG + 1) as g:
                for c in range(C1):
                    m = P
                    act.wait_ge(S["g_done"], C1 * g + c + 1)
                    act.wait_ge(S["su_done"], C1 * g + max(c - 1, 0))
                    act.activation(hr[0:m, c % 2, :], bank[0 + c % 2][0:m, :], ACT.Silu).then_inc(S["silu_done"], 1)

        @block.gpsimd
        def _(pool):
            for count, names in PER_GROUP:
                for name in names:
                    pool.sem_inc(S[name], count)
            pool.wait_ge(S["sel0_in"], 16)
            pool.tensor_copy(sel[:, :], self32[:, :]).then_inc(S["sel_ready"], 1)
            with pool.Fori(1, NG + 1) as g:
                pool.wait_ge(S["ln_normed"], NG)
                pool.wait_ge(S["proj_done"], 16 * g)
                pool.tensor_copy(ng[:, :], nrm[:, bass.ds((g - 1) * G, G)]).then_inc(S["ng_ready"], 1)

            def routing(base):
                with pool.Fori(1, NG + 1) as g:
                    pool.wait_ge(S["ln_normed"], 2 * NG if base == 0 else 5 * NG)
                    pool.wait_ge(S["logit_done"], base + g)
                    if base:
                        pool.wait_ge(S["sq_ready"], g)
                    pool.tensor_copy(ng[:, :], nrm[:, bass.ds((g - 1) * G, G)]).then_inc(S["rng_ready"], 1)
                    if base:
                        pool.wait_ge(S["ss_guard"], g + 1)
                        pool.wait_ge(S["logit_scaled"], 2 * g)
                        pool.tensor_tensor(gsr[:, :], gsum[:, :], ones_half(NT), ALU.pow).then_inc(S["ss_inv"], 1)

            routing(0)
            pool.wait_ge(S["x2_added"], NG + 1)
            pool.memset(h1[:, :, 0:1], 0.0)
            pool.memset(h2[:, :, 0:1], 0.0)
            for i in range(2):
                pool.memset(kp[i].rearrange("p (s t) -> p s t", s=SEQ)[:, :, 0:1], FAR)
            pool.memset(e3b[:, :], 0.0)
            pool.memset(e4b[:, :], 0.0)
            pool.memset(kvb[:, :], 0.0)
            pool.memset(reset[:, :], 0.0).then_inc(S["ones_ready"], 1)
            pool.wait_ge(S["ones_ready"], 1)
            pool.memset(reset[:, :].rearrange("p (s t) -> p s t", s=SEQ)[:, :, 0:1], FAR).then_inc(S["ones_ready"], 1)

            def enter(n):
                pool.wait_ge(S["affined1"], n + 1)
                if n >= 1:
                    pool.wait_ge(S["mixed1"], 3 * n)
                pool.tensor_tensor(seqs(dif1), h1[:, :, 1:T1], h1[:, :, 0:T], ALU.subtract).then_inc(S["diff1"], 1)

            def scan_a(n):
                pool.wait_ge(S["p_scanned"], n + 1)
                pool.wait_ge(S["k_copied"], n + 1)
                if n >= 1:
                    pool.wait_ge(S["e4_done"], n)
                pool.tensor_tensor(seqs(a2), cur(kp[n % 2]), cur(pm), ALU.subtract).then_inc(S["a2_done"], 1)

                pool.wait_ge(S["d1_done"], n + 1)
                if n >= 1:
                    pool.wait_ge(S["e2_done"], n)
                pool.tensor_scalar(d2, d1, 0.0, None, ALU.min).then_inc(S["d_below"], 1)
                pool.wait_ge(S["d_below"], n + 1)
                pool.tensor_scalar(d1, d1, 0.0, None, ALU.max).then_inc(S["d_above"], 1)

            def scan_b(n):
                pool.wait_ge(S["t1_done"], n + 1)
                pool.wait_ge(S["t2_done"], n + 1)
                if n >= 1:
                    pool.wait_ge(S["rw_done"], n)
                pool.tensor_tensor(num, t1, t2, ALU.add).then_inc(S["num_done"], 1)

            def leave(n):
                pool.wait_ge(S["affined2"], n + 1)
                if n >= 1:
                    pool.wait_ge(S["mixed2"], 2 * n)
                pool.tensor_tensor(seqs(dif2), h2[:, :, 1:T1], h2[:, :, 0:T], ALU.subtract).then_inc(S["diff2"], 1)

            def bound_r(n):
                pool.wait_ge(S["r_copied"], n + 1)
                pool.tensor_scalar(er[n % 2], er[n % 2], SIG_MIN, None, ALU.max).then_inc(S["r_bounded"], 1)

            def squares(n):
                pool.wait_ge(S["cr_copied"], n + 1)
                pool.tensor_scalar(ecr, ecr, SIG_MIN, None, ALU.max).then_inc(S["cr_bounded"], 1)
                for j in range(FC):
                    pool.wait_ge(S["ck_relu"], 4 * n + j + 1)
                    pool.tensor_tensor(ckr[:, j, :], ckr[:, j, :], ckr[:, j, :], ALU.mult).then_inc(S["ck_squared"], 1)

            for s in range(STEPS):
                if s < ITEMS:
                    enter(s)
                if 1 <= s <= ITEMS:
                    scan_a(s - 1)
                if s >= 2:
                    leave(s - 2)
                if 1 <= s <= ITEMS:
                    scan_b(s - 1)
                if s < ITEMS:
                    bound_r(s)
                if s >= 2:
                    squares(s - 2)

            pool.wait_ge(S["sel1_in"], 16)
            pool.wait_ge(S["x3_added"], NG)
            pool.tensor_copy(sel[0:3 * E1, 0:(C1 - 1) * P], self32[0:3 * E1, 0:(C1 - 1) * P]).then_inc(S["sel_ready"], 1)
            pool.wait_ge(S["gw_guard"], 1)
            pool.tensor_tensor(gn[:, 3, 0:E1], gn[:, 2, 0:E1], ones_half(E1), ALU.pow).then_inc(S["gw_inv"], 1)
            routing(NG)

        @block.vector
        def _(dve):
            def layernorm(first, g_src=None):
                for g in range(NG):
                    dve.wait_ge(S["ln_rstd"], first + g + 1)
                    dve.tensor_tensor(nrm[:, g * G:(g + 1) * G], bank[g][:, :], lnr[:, g, :],
                                      ALU.mult).then_inc(S["ln_normed"], 1)

            dve.wait_ge(S["const_in"], 16)
            dve.tensor_copy(identb[:, :], ident)
            dve.memset(minus_half[:, :], -0.5)
            dve.memset(lg[:, :, :], UNUSED)
            dve.memset(top2[:, :, :], UNUSED)
            dve.memset(v_aug[:, :, :, HD:HD + 1], 1.0).then_inc(S["const_ready"], 1)
            dve.wait_ge(S["const_ready"], 1)
            layernorm(0)

            PROJ, SC, AV, YT, OUT = (0, 1), 4, 5, 6, 7
            with dve.Fori(1, NG + 1) as g:
                dve.wait_ge(S["av_done"], 16 * g)
                for u in range(2 * NT):
                    dve.wait_ge(S["v_done"], 8 * g + u + 1)
                    hv = H // 2
                    dve.tensor_copy(v_aug[:, u // 2, (u % 2) * hv:(u % 2 + 1) * hv, 0:HD],
                                    bank[PROJ[u % 2]][:, :].rearrange("p (h e) -> p h e", h=hv)
                                    ).then_inc(S["v_evac"], 1)

                def copies(p, s):
                    dve.wait_ge(S["proj_done"], 16 * g + 2 * p + s + 1)
                    dve.wait_ge(S["feat_done"], 32 * g + (4 * (p - 1) + 2 * s + 2 if p else 0))
                    y = stack[64:128, s, 1, :]
                    dve.tensor_copy(y, bank[PROJ[s]][64:128, :]).then_inc(S["odd_copied"], 1)
                    dve.wait_ge(S["odd_copied"], 16 * g + 2 * p + s + 1)
                    dve.tensor_tensor(stack[0:64, s, 1, :], y, y, ALU.mult).then_inc(S["stack_odd"], 1)

                def mask(p, i):
                    dve.wait_ge(S["score_done"], 32 * g + 4 * p + i + 1)
                    dve.wait_ge(S["av_done"], 16 * g + (2 * (p - 1) + i // 2 + 1 if p else 0))
                    dve.tensor_tensor(scores[:, i, :], bank[SC][:, 0:3 * P], causal, ALU.mult).then_inc(S["masked"], 1)

                def normalise(p, b):
                    n = 2 * p + b
                    av = bank[AV][:, 0:4 * (HD + 1)].rearrange("p (h j e) -> p h j e", h=2, j=2)
                    dve.wait_ge(S["av_done"], 16 * g + n + 1)
                    dve.tensor_scalar(den[:, b, :], av[:, :, :, HD], DEN_EPS, None, ALU.add).then_inc(S["den_ready"], 1)
                    dve.wait_ge(S["den_ready"], 32 * g + 2 * n + 1)
                    dve.reciprocal(rden[:, b, :], den[:, b, :]).then_inc(S["den_ready"], 1)
                    dve.wait_ge(S["den_ready"], 32 * g + 2 * n + 2)
                    dve.wait_ge(S["yt_done"], 8 * g + p)
                    for h in range(2):
                        ins_ = dve.tensor_tensor(ynorm[:, 2 * b:2 * b + 2, h, :], av[:, h, :, 0:HD],
                                                 rden[:, b, 2 * h:2 * h + 2].unsqueeze(2).to_broadcast([P, 2, HD]),
                                                 ALU.mult)
                    ins_.then_inc(S["ynormed"], 1)

                def copy_yt(p):
                    dve.wait_ge(S["yt_done"], 8 * g + p + 1)
                    dve.wait_ge(S["wo_done"], 8 * g + p)
                    dve.tensor_copy(yt[:, :], bank[YT][:, :]).then_inc(S["yt_copied"], 1)

                for p in range(NP + 2):
                    a, c, d = p < NP, 1 <= p <= NP, p >= 2
                    if c:
                        mask(p - 1, 0)
                    if d:
                        copy_yt(p - 2)
                    if a:
                        copies(p, 0)
                    if c:
                        mask(p - 1, 1)
                    if a:
                        copies(p, 1)
                    if c:
                        mask(p - 1, 2)
                        normalise(p - 1, 0)
                        mask(p - 1, 3)
                        normalise(p - 1, 1)
                dve.wait_ge(S["wo_done"], 8 * g + 8)
                xg = x[:, bass.ds((g - 1) * G, G)]
                dve.tensor_tensor(xg, bank[OUT][:, :], xg, ALU.add).then_inc(S["x1_added"], 1)

            layernorm(NG)

            def routing(base, E, K):
                with dve.Fori(1, NG + 1) as g:
                    n = base + g + 1
                    dve.wait_ge(S["logit_done"], n)
                    dve.wait_ge(S["gate_exp"], base + g)
                    if E == E0:
                        dve.tensor_copy(lg[:, :, 0:E], bank[0][:, 0:NT * E].rearrange("p (t e) -> p t e", t=NT)
                                        ).then_inc(S["logit_copied"], 1)
                        dve.wait_ge(S["logit_copied"], n)
                        dve.tensor_scalar(gn[:, :, 0:E], lg[:, :, 0:E], SIG_MIN, None,
                                          ALU.max).then_inc(S["logit_bounded"], 1)
                    else:
                        raw = bank[0][:, 0:NT * (E + 1)].rearrange("p (t e) -> p t e", t=NT)
                        dve.tensor_scalar(gsum[:, :], raw[:, :, E], NORM_EPS2, None, ALU.max).then_inc(S["ss_guard"], 1)
                        dve.wait_ge(S["ss_inv"], g + 1)
                        dve.tensor_tensor(lg[:, :, 0:E], raw[:, :, 0:E],
                                          gsr[:, :].unsqueeze(2).to_broadcast([P, NT, E]),
                                          ALU.mult).then_inc(S["logit_scaled"], 1)
                        dve.wait_ge(S["logit_scaled"], 2 * g + 1)
                        dve.tensor_tensor(lg[:, :, 0:E], lg[:, :, 0:E],
                                          gn[:, 3, 0:E].unsqueeze(1).to_broadcast([P, NT, E]),
                                          ALU.mult).then_inc(S["logit_scaled"], 1)
                        dve.wait_ge(S["logit_scaled"], 2 * g + 2)
                        dve.sem_inc(S["logit_copied"], 1)
                        fixed(dve)
                        dve.wait_ge(S["logit_copied"], n)
                    for t in range(NT):
                        last = dve.max(top[:, t, :], lg[:, t, 0:E])
                    last.then_inc(S["top_found"], 1)
                    if K < 8:
                        dve.wait_ge(S["top_found"], n)
                        dve.tensor_copy(top2[:, :, 0:K], top[:, :, 0:K]).then_inc(S["top_packed"], 1)
                        fixed(dve)
                        dve.wait_ge(S["top_packed"], n)
                    else:
                        fixed(dve)
                        dve.wait_ge(S["top_found"], n)
                    for t in range(NT):
                        if K < 8:
                            last = dve.match_replace(repl[:, t, :], top2[:, t, :], lg[:, t, :], TAKEN)
                        else:
                            last = dve.match_replace(repl[:, t, 0:E], top[:, t, :], lg[:, t, 0:E], TAKEN)
                    last.then_inc(S["top_replaced"], 1)
                    dve.wait_ge(S["top_replaced"], n)
                    dve.tensor_scalar(msk[:, :, 0:E], repl[:, :, 0:E], TAKEN, None,
                                      ALU.is_equal).then_inc(S["gate_mask"], 1)
                    dve.wait_ge(S["gate_exp"], n)
                    dve.tensor_scalar(gs[:, :, 0:E], ex[:, :, 0:E], 1.0, None, ALU.add).then_inc(S["gate_sum"], 1)
                    dve.wait_ge(S["gate_sum"], n)
                    dve.reciprocal(gr[:, :, 0:E], gs[:, :, 0:E]).then_inc(S["gate_recip"], 1)
                    dve.wait_ge(S["gate_recip"], n)
                    dve.wait_ge(S["gate_mask"], n)
                    dve.tensor_tensor(gm[:, :, 0:E], gr[:, :, 0:E], msk[:, :, 0:E], ALU.mult).then_inc(S["gate_masked"], 1)
                    dve.wait_ge(S["gate_masked"], n)
                    gates = gm
                    if E == E1:
                        dve.tensor_reduce(gsum[:, :], gm[:, :, 0:E], AX.X, ALU.add).then_inc(S["gate_norm"], 1)
                        dve.wait_ge(S["gate_norm"], 3 * g + 1)
                        dve.reciprocal(den[:, 0, :], gsum[:, :]).then_inc(S["gate_norm"], 1)
                        dve.wait_ge(S["gate_norm"], 3 * g + 2)
                        dve.tensor_tensor(gr[:, :, 0:E], gm[:, :, 0:E],
                                          den[:, 0, :].unsqueeze(2).to_broadcast([P, NT, E]),
                                          ALU.mult).then_inc(S["gate_norm"], 1)
                        dve.wait_ge(S["gate_norm"], 3 * g + 3)
                        gates = gr
                    dve.wait_ge(S["gt_done"], base + g)
                    hi, mid, lo = (parts[:, :, i * E:(i + 1) * E] for i in range(3))
                    dve.tensor_copy(hi, gates[:, :, 0:E]).then_inc(S["part_hi"], 1)
                    dve.wait_ge(S["part_hi"], n)
                    dve.tensor_tensor(r1[:, :, 0:E], gates[:, :, 0:E], hi, ALU.subtract).then_inc(S["part_r1"], 1)
                    dve.wait_ge(S["part_r1"], n)
                    dve.tensor_copy(mid, r1[:, :, 0:E]).then_inc(S["part_mid"], 1)
                    dve.wait_ge(S["part_mid"], n)
                    dve.tensor_tensor(lo, r1[:, :, 0:E], mid, ALU.subtract).then_inc(S["parts_ready"], 1)
                    dve.wait_ge(S["gt_done"], n)
                    dve.tensor_copy(gt[0:3 * E, bass.ds((g - 1) * G, G)],
                                    bank[1][0:3 * E, :].bitcast(BF16)[:, 0:G]).then_inc(S["gt_copied"], 1)

            routing(0, E0, K0)
            with dve.Fori(1, NG + 1) as g:
                for c in range(C0):
                    dve.wait_ge(S["relu_done"], 16 * g + c + 1)
                    dve.wait_ge(S["gbc_done"], 16 * g + c + 1)
                    dve.wait_ge(S["down_done"], 16 * g + max(c - 2, 0))
                    dve.tensor_tensor(hh[:, c % 3, :], bank[4 + c % 2][:, :], hr[:, c % 2, :],
                                      ALU.mult).then_inc(S["h_done"], 1)
                dve.wait_ge(S["down_done"], 16 * g + C0)
                xg = x[:, bass.ds((g - 1) * G, G)]
                dve.tensor_tensor(xg, bank[6][:, :], xg, ALU.add).then_inc(S["x2_added"], 1)

            layernorm(2 * NG)
            for g in range(NG):
                dve.wait_ge(S["ln_rstd"], 3 * NG + g + 1)
                dve.tensor_tensor(nrm[:, g * G:(g + 1) * G], bank[g][:, :], lnr[:, g, :],
                                  ALU.mult).then_inc(S["ln_normed"], 1)

            dve.wait_ge(S["decay_exp"], L)
            dve.wait_ge(S["ones_ready"], 2)
            dve.tensor_scalar(negdec[:, :], expdec[:, :], -1.0, None, ALU.mult).then_inc(S["decay_neg"], 1)
            dve.wait_ge(S["decay_neg"], 1)

            def enter_norm(n):
                dve.wait_ge(S["rstd1"], n + 1)
                if n >= 1:
                    dve.wait_ge(S["affined1"], n)
                dve.tensor_tensor(hn1, bank[0][:, :], rs1, ALU.mult).then_inc(S["normed1"], 1)

            def enter_mix(n):
                l = n // NG
                dve.wait_ge(S["diff1"], n + 1)
                for i, dst in enumerate((xk, xv, xr)):
                    if n >= 1:
                        dve.wait_ge(S["kvr_done"], 3 * (n - 1) + i + 1)
                    dve.scalar_tensor_tensor(out=seqs(dst), in0=seqs(dif1), scalar=vec[:, l, MK + i:MK + i + 1],
                                             in1=h1[:, :, 0:T], op0=ALU.mult, op1=ALU.add).then_inc(S["mixed1"], 1)

            def scan_a(n):
                l = n // NG
                if n % NG == 0:
                    if n:
                        dve.wait_ge(S["p_scanned"], n)
                    dve.tensor_scalar(dec, reset[:, :], negdec[:, l:l + 1], None, ALU.add).then_inc(S["decay_bc"], 1)
                    dve.wait_ge(S["decay_bc"], l + 1)
                dve.wait_ge(S["k_copied"], n + 1)
                if n >= 1:
                    dve.wait_ge(S["a1_done"], n)
                    dve.wait_ge(S["a2_done"], n)
                    dve.wait_ge(S["d1_done"], n)
                dve.tensor_tensor_scan(pm, dec, kp[n % 2], FAR, ALU.add, ALU.max).then_inc(S["p_scanned"], 1)
                dve.wait_ge(S["p_scanned"], n + 1)
                if n >= 1:
                    dve.wait_ge(S["e3_done"], n)
                dve.scalar_tensor_tensor(out=seqs(a1), in0=prev(pm), scalar=negdec[:, l:l + 1], in1=cur(pm),
                                         op0=ALU.add, op1=ALU.subtract).then_inc(S["a1_done"], 1)
                if n >= 1:
                    dve.wait_ge(S["e1_done"], n)
                dve.scalar_tensor_tensor(out=seqs(d1), in0=cur(kp[n % 2]), scalar=vec[:, l, FIRST:FIRST + 1],
                                         in1=prev(pm), op0=ALU.add, op1=ALU.subtract).then_inc(S["d1_done"], 1)

            def scan_b(n):
                dve.wait_ge(S["e4_done"], n + 1)
                dve.wait_ge(S["v_copied"], n + 1)
                if n >= 1:
                    dve.wait_ge(S["aa_scanned"], n)
                dve.tensor_tensor(cur(kvb[:, :]), cur(e4b[:, :]), seqs(vs[n % 2]), ALU.mult).then_inc(S["kv_done"], 1)
                dve.wait_ge(S["e3_done"], n + 1)
                if n >= 1:
                    dve.wait_ge(S["t3_done"], n)
                    dve.wait_ge(S["t1_done"], n)
                dve.tensor_tensor_scan(bb[:, :], e3b[:, :], e4b[:, :], 0.0, ALU.mult, ALU.add).then_inc(S["bb_scanned"], 1)
                dve.wait_ge(S["kv_done"], n + 1)
                dve.tensor_tensor_scan(aa[:, :], e3b[:, :], kvb[:, :], 0.0, ALU.mult, ALU.add).then_inc(S["aa_scanned"], 1)
                dve.wait_ge(S["e1_done"], n + 1)
                dve.wait_ge(S["e2_done"], n + 1)
                dve.wait_ge(S["bb_scanned"], n + 1)
                if n >= 1:
                    dve.wait_ge(S["den_done"], n)
                    dve.wait_ge(S["num_done"], n)
                dve.tensor_tensor(seqs(t3), seqs(e1), prev(bb[:, :]), ALU.mult).then_inc(S["t3_done"], 1)
                dve.tensor_tensor(t2, e2, vs[n % 2], ALU.mult).then_inc(S["t2_done"], 1)
                dve.wait_ge(S["aa_scanned"], n + 1)
                dve.tensor_tensor(seqs(t1), seqs(e1), prev(aa[:, :]), ALU.mult).then_inc(S["t1_done"], 1)
                dve.wait_ge(S["t3_done"], n + 1)
                if n >= 1:
                    dve.wait_ge(S["den2_done"], n)
                dve.tensor_tensor(dn, e2, t3, ALU.add).then_inc(S["den_done"], 1)
                dve.wait_ge(S["den_done"], n + 1)
                dve.wait_ge(S["r_exp"], n + 1)
                if n >= 1:
                    dve.wait_ge(S["rec_done"], n)
                dve.scalar_tensor_tensor(out=dn2, in0=er[n % 2], scalar=1.0, in1=dn,
                                         op0=ALU.add, op1=ALU.mult).then_inc(S["den2_done"], 1)
                dve.wait_ge(S["den2_done"], n + 1)
                if n >= 1:
                    dve.wait_ge(S["rw_done"], n)
                dve.reciprocal(rec, dn2).then_inc(S["rec_done"], 1)
                dve.wait_ge(S["rec_done"], n + 1)
                dve.wait_ge(S["num_done"], n + 1)
                if n >= 1:
                    dve.wait_ge(S["o_done"], n)
                dve.tensor_tensor(rw, num, rec, ALU.mult).then_inc(S["rw_done"], 1)

            def leave_add(n):
                g = n % NG
                dve.wait_ge(S["o_done"], n + 1)
                dve.wait_ge(S["centered1"], n + 1)
                r = rs[:, g * G:(g + 1) * G]
                dve.tensor_tensor(r, bank[3][:, :], r, ALU.add).then_inc(S["x_mid"], 1)

            def leave_norm(n):
                dve.wait_ge(S["rstd2"], n + 1)
                if n >= 1:
                    dve.wait_ge(S["affined2"], n)
                dve.tensor_tensor(hn2, bank[1][:, :], rs2, ALU.mult).then_inc(S["normed2"], 1)

            def leave_mix(n):
                l = n // NG
                dve.wait_ge(S["diff2"], n + 1)
                for i, dst in ((1, xcr), (0, xck)):
                    if n >= 1:
                        dve.wait_ge(S["ck_done"], 4 * n)
                        dve.wait_ge(S["cr_done"], n)
                    dve.scalar_tensor_tensor(out=seqs(dst), in0=seqs(dif2), scalar=vec[:, l, CMK + i:CMK + i + 1],
                                             in1=h2[:, :, 0:T], op0=ALU.mult, op1=ALU.add).then_inc(S["mixed2"], 1)

            def leave_tail(n):
                g = n % NG
                dve.wait_ge(S["cr_exp"], n + 1)
                dve.tensor_scalar(scr, ecr, 1.0, None, ALU.add).then_inc(S["cr_sum"], 1)
                dve.wait_ge(S["cr_sum"], n + 1)
                dve.reciprocal(rcr, scr).then_inc(S["cr_recip"], 1)
                dve.wait_ge(S["cr_recip"], n + 1)
                dve.wait_ge(S["cv_done"], n + 1)
                dve.tensor_tensor(kvg, bank[5][:, :], rcr, ALU.mult).then_inc(S["kv_gated"], 1)
                dve.wait_ge(S["kv_gated"], n + 1)
                dve.wait_ge(S["centered2"], n + 1)
                r = rs[:, g * G:(g + 1) * G]
                dve.tensor_tensor(r, kvg, r, ALU.add).then_inc(S["x_out"], 1)

            for s in range(STEPS):
                a, w, c = s < ITEMS, 1 <= s <= ITEMS, s >= 2
                if c:
                    leave_add(s - 2)
                if a:
                    enter_norm(s)
                if w:
                    scan_a(s - 1)
                if c:
                    leave_norm(s - 2)
                if a:
                    enter_mix(s)
                if c:
                    leave_mix(s - 2)
                if w:
                    scan_b(s - 1)
                if c:
                    leave_tail(s - 2)

            for g in range(NG):
                dve.wait_ge(S["x_out"], ITEMS - NG + g + 1)
                xg = x[:, g * G:(g + 1) * G]
                dve.tensor_tensor(xg, xg, rs[:, g * G:(g + 1) * G], ALU.add).then_inc(S["x3_added"], 1)

            layernorm(4 * NG)
            dve.wait_ge(S["rgate_in"], 16)
            dve.tensor_tensor(msk[:, 0, 0:E1], rgate[:, :], rgate[:, :], ALU.mult).then_inc(S["gw_sq"], 1)
            dve.wait_ge(S["gw_ss"], 1)
            dve.tensor_scalar(gn[:, 2, 0:E1], bank[7][:, 0:E1], NORM_EPS2, None, ALU.max).then_inc(S["gw_guard"], 1)
            dve.wait_ge(S["gw_inv"], 1)
            routing(NG, E1, K1)
            with dve.Fori(1, NG + 1) as g:
                for c in range(C1):
                    m = P
                    n = C1 * g + c
                    dve.wait_ge(S["silu_done"], n + 1)
                    dve.wait_ge(S["u_done"], n + 1)
                    if c < C1 - 1:
                        dve.wait_ge(S["h1_done"], C1 * g + c)
                        dve.tensor_tensor(yt[:, :], bank[2 + c % 2][:, :], hr[:, c % 2, :], ALU.mult).then_inc(S["su_done"], 1)
                        dve.wait_ge(S["su_done"], n + 1)
                        dve.wait_ge(S["cbc_done"], (C1 - 1) * g + c + 1)
                        dve.wait_ge(S["down1_done"], C1 * g + max(c - 2, 0))
                        dve.tensor_tensor(hh[:, c % 3, :], bank[4 + c % 2][:, :], yt[:, :], ALU.mult).then_inc(S["h1_done"], 1)
                    else:
                        dve.wait_ge(S["down1_done"], C1 * g + c - 2)
                        dve.tensor_tensor(hh[0:m, c % 3, :], bank[2 + c % 2][0:m, :], hr[0:m, c % 2, :],
                                          ALU.mult).then_inc(S["su_done"], 1)
                        dve.wait_ge(S["su_done"], n + 1)
                        dve.sem_inc(S["h1_done"], 1)
                dve.wait_ge(S["down1_done"], C1 * g + C1)
                xg = x[:, bass.ds((g - 1) * G, G)]
                dve.tensor_tensor(xg, bank[6][:, :], xg, ALU.add).then_inc(S["y_added"], 1)


def arrays_for(inputs):
    import numpy as np
    f = lambda a: np.ascontiguousarray(a)
    i = {k: np.asarray(v) for k, v in inputs.items()}
    c = lambda k: i["L1_attn_" + k]
    eye = np.eye(P, dtype=np.float32)
    tri = np.triu(np.ones((P, P), np.float32))
    one = np.ones((P, P), np.float32)
    consts = np.concatenate([eye - one / P, one / P, eye, one, tri, one, tri], axis=1)

    def selector(E, chunks):
        s = np.zeros((3 * E, chunks * P), np.float32)
        for part in range(3):
            for e in range(E):
                s[part * E + e, e * 64:(e + 1) * 64] = 1.0
        return s

    wf = i["L0_attn_W_feat"]
    half = np.full((HD, NF), -0.5, np.float32)
    wfeat = np.stack([np.concatenate([wf, half]), np.concatenate([half, wf])], axis=1)
    lay = []
    for l in range(L):
        ws = [c("Wk")[l].T, c("Wv")[l].T, c("Wr")[l].T, c("Wo")[l].T]
        ws += [c("Wck")[l][j * P:(j + 1) * P].T for j in range(FC)]
        ws += [c("Wcr")[l].T]
        ws += [c("Wcv")[l][:, j * P:(j + 1) * P].T for j in range(FC)]
        lay.append(np.stack(ws, axis=1))
    wrwkv = np.stack(lay, axis=1)
    vec = np.zeros((P, L + 1, NVEC), np.float32)
    for l in range(L):
        for j, k in enumerate(("ln1_w", "ln1_b", "tmk", "tmv", "tmr", "time_decay", "time_first",
                               "ln2_w", "ln2_b", "cmk", "cmr")):
            vec[:, l, j] = c(k)[l]
    vec[:, L, 0] = LN_EPS
    vec[:, L, 1] = c("ln0_w")
    vec[:, L, 2] = c("ln0_b")
    m = lambda k: i["L1_ffn_" + k]
    ed = lambda a: a.transpose(1, 0, 2).reshape(P, E1 * 64)
    pad = np.zeros((P, 64), np.float32)
    wgu = np.stack([np.concatenate([ed(m("w_gate")), m("sw_gate"), pad], axis=1),
                    np.concatenate([ed(m("w_up")), m("sw_up"), pad], axis=1)], axis=1)
    wdn = np.zeros((P, C1, P), np.float32)
    wdn[:, :C1 - 1] = m("w_down").reshape(C1 - 1, P, P).transpose(1, 0, 2)
    wdn[:64, C1 - 1] = m("sw_down")
    return {k: f(v) for k, v in {
        "x": i["L0_attn_x"].transpose(2, 0, 1).reshape(P, N),
        "consts": consts,
        "wq": i["L0_attn_Wq"], "wk": i["L0_attn_Wk"], "wv": i["L0_attn_Wv"],
        "wfeat": wfeat,
        "wo": i["L0_attn_Wo"].reshape(NP, P, P).transpose(1, 0, 2),
        "vec": vec,
        "esel": i["L0_ffn_expert_sel"].T,
        "sel0": selector(E0, C0),
        "keys": i["L0_ffn_keys"].transpose(1, 0, 2).reshape(P, E0 * 64),
        "vals": i["L0_ffn_values"].reshape(C0, P, P).transpose(1, 0, 2),
        "wrwkv": wrwkv,
        "rgate": m("gate_w").T,
        "wgu": wgu, "wdn": wdn,
        "sel1": selector(E1, C1 - 1),
    }.items()}


def kernel(**inputs):
    import numpy as _np
    import concourse.bacc as _bacc
    from concourse import mybir as _mybir
    from concourse.bass_utils import run_bass_kernel_spmd as _run

    nc = _bacc.Bacc("TRN2", target_bir_lowering=False, num_devices=1)
    laid = arrays_for(inputs)
    arrays, args = {}, {}
    for name, a in laid.items():
        arrays[f"in_{name}_dram"] = a
        args[name] = nc.dram_tensor(f"in_{name}_dram", a.shape, _mybir.dt.from_np(a.dtype), kind="ExternalInput").ap()
    out = nc.dram_tensor("out_dram", (P, N), F32, kind="ExternalOutput").ap()
    two_blocks(nc, args, out)
    r = _run(nc, [arrays], core_ids=[0])
    got = r.results[0]["out_dram"]
    return _np.ascontiguousarray(_np.asarray(got).reshape(P, B, T).transpose(1, 2, 0))
```

```python
from contextlib import ExitStack

import concourse.bass as bass
from concourse import mybir

F32 = mybir.dt.float32
BF16 = mybir.dt.bfloat16
ALU = mybir.AluOpType
ACT = mybir.ActivationFunctionType
AX = mybir.AxisListType

P = 128
B, T = 8, 256
N = B * T
G = 512
NG = N // G
NT = G // P
SEQ = G // T
H, HD, NF = 16, 64, 128
NP = H // 2
E0, K0 = 32, 4
C0 = E0 // 2
E1, K1 = 16, 8
C1 = E1 // 2 + 1
L = 4
FC = 4
T1 = T + 1
NVEC = 12
LNW, LNB, MK, MV, MR, DECAY, FIRST, LN2W, LN2B, CMK, CMR = range(11)
LN_EPS = 1e-5
DEN_EPS = 1e-6 * NF
NORM_EPS2 = 1e-24
SIG_MIN = -38.0
FAR = -1e38
TAKEN = 3e38
UNUSED = -3e38

PER_GROUP = [
    (2 * NT, ["v_done", "v_evac"]),
    (NP, ["yt_done", "yt_copied", "wo_done"]),
    (16, ["proj_done", "stack_odd", "stack_even", "odd_copied", "av_done", "ynormed",
         "up_done", "gbc_done", "relu_done", "h_done", "down_done"]),
    (32, ["feat_done", "feat_exp", "score_done", "masked", "den_ready"]),
    (C1, ["g_done", "u_done", "silu_done", "su_done", "h1_done", "down1_done"]),
    (C1 - 1, ["cbc_done"]),
    (3, ["gate_norm"]),
    (2, ["logit_scaled"]),
    (1, ["ng_ready", "x1_added", "x2_added", "y_added", "rng_ready", "logit_done", "logit_copied", "logit_bounded",
        "top_found", "top_packed", "top_replaced", "gate_exp", "gate_sum", "gate_recip", "gate_mask",
        "gate_masked", "part_hi", "part_r1", "part_mid", "parts_ready", "gt_done", "gt_copied", "sq_ready",
        "ss_guard", "ss_inv"]),
]
SEMS = [
    "x_in_1", "x_in_2", "x_in_3", "x_in_4", "wqkv_in", "wfeat_in", "wo_in", "const_in", "sel0_in", "keys_in", "vals_in", "wrwkv_in", "vec_in",
    "rgate_in", "wgu_in", "wdn_in", "shared_in", "esel_in", "sel1_in",
    "ln_centered", "ln_squared", "ln_var", "ln_logged", "ln_rstd", "ln_normed",
    "const_ready", "sel_ready", "ones_ready",
    "ng_ready", "v_done", "v_evac", "proj_done", "stack_odd", "stack_even", "odd_copied", "feat_done", "feat_exp",
    "score_done", "masked", "av_done", "den_ready", "ynormed", "yt_done", "yt_copied", "wo_done", "x1_added",
    "rng_ready", "logit_done", "logit_copied", "logit_bounded", "top_found", "top_packed", "top_replaced", "gate_exp", "gate_sum",
    "gate_recip", "gate_mask", "gate_masked", "gate_norm", "part_hi", "part_r1", "part_mid", "part_r2", "parts_ready", "gt_done", "gt_copied",
    "up_done", "gbc_done", "relu_done", "h_done", "down_done", "x2_added",
    "ln0_affined", "decay_exp", "decay_neg", "decay_bc",
    "centered1", "squared1", "var1", "logged1", "rstd1", "normed1", "affined1", "diff1", "mixed1", "kvr_done",
    "k_copied", "v_copied", "r_bounded", "r_exp", "p_scanned", "a1_done", "a2_done", "d1_done", "d_below", "d_above",
    "e3_done", "e4_done", "e1_done", "e2_done", "kv_done", "aa_scanned", "bb_scanned", "t1_done", "t2_done",
    "num_done", "t3_done", "den_done", "den2_done", "den_logged", "rec_done", "rw_done", "o_done", "x_mid",
    "centered2", "squared2", "var2", "logged2", "rstd2", "normed2", "affined2", "diff2", "mixed2",
    "ck_done", "ck_relu", "even_squared", "odd_squared", "cr_done", "cr_bounded", "cr_exp", "cr_logged", "cr_sig",
    "cv_done", "kv_gated", "x_out",
    "gw_sq", "gw_ss", "gw_guard", "gw_inv", "sq_ready", "ss_guard", "ss_inv", "logit_scaled", "x3_added",
    "g_done", "u_done", "cbc_done", "silu_done", "su_done", "h1_done", "down1_done", "y_added", "out_stored",
]


def two_blocks(nc, ins, out):
    with ExitStack() as ctx:
        def sb(name, shape, dt=F32):
            return ctx.enter_context(nc.sbuf_tensor(name, shape, dt))

        S = {name: ctx.enter_context(nc.semaphore(name)) for name in SEMS}
        bank = [ctx.enter_context(nc.psum_tensor(f"bank{i}", [P, G], F32)) for i in range(8)]

        x = sb("x", [P, N])
        nrm = sb("nrm", [P, N])
        ng = sb("ng", [P, G])
        wq, wk, wv = (sb(n, [P, H * HD]) for n in ("wq", "wk", "wv"))
        wfeat = sb("wfeat", [P, 2, NF])
        wo = sb("wo", [P, NP, P])
        consts = sb("consts", [P, 4 * P + 3 * P])
        center, mean, ident, ones = (consts[:, i * P:(i + 1) * P] for i in range(4))
        causal = consts[:, 4 * P:7 * P]
        esel = sb("esel", [P, E0])
        big = sb("big", [P, 4096 + 2 * C1 * P + C1 * P])
        keys = big[:, 0:E0 * 64]
        vals = big[:, E0 * 64:E0 * 64 + C0 * P].rearrange("p (c d) -> p c d", c=C0)
        wrwkv = sb("wrwkv", [P, L, 13, P])
        vec = sb("vec", [P, L + 1, NVEC])
        rgate = sb("rgate", [P, E1])
        wgu = big[:, 4096:4096 + 2 * C1 * P].rearrange("p (s e) -> p s e", s=2)
        wdn = big[:, 4096 + 2 * C1 * P:4096 + 2 * C1 * P + C1 * P].rearrange("p (c d) -> p c d", c=C1)
        sel = sb("sel", [3 * E0, C0 * P], BF16)
        self32 = sb("self32", [3 * E0, C0 * P])
        lnsq = sb("lnsq", [P, NG, G])
        lnr = sb("lnr", [P, NG, G])
        gt = sb("gt", [3 * E0, N], BF16)

        stack = sb("stack", [P, 2, 2, G])
        feat = sb("feat", [P, 2, 2, 2, G])
        v_aug = sb("v_aug", [P, NT, H, HD + 1])
        scores = sb("scores", [P, 4, 3 * P])
        den = sb("den", [P, 2, 4])
        rden = sb("rden", [P, 2, 4])
        ynorm = sb("ynorm", [P, NT, 2, HD])
        yt = sb("yt", [P, G])

        lg = sb("lg", [P, NT, E0 + 4])
        ex = sb("ex", [P, NT, E0])
        gs = sb("gs", [P, NT, E0])
        gr = sb("gr", [P, NT, E0])
        top = sb("top", [P, NT, 8])
        top2 = sb("top2", [P, NT, 8])
        repl = sb("repl", [P, NT, E0 + 4])
        msk = sb("msk", [P, NT, E0])
        gm = sb("gm", [P, NT, E0])
        gn = sb("gn", [P, NT, E0])
        gsum = sb("gsum", [P, NT])
        gsr = sb("gsr", [P, NT])
        r1 = sb("r1", [P, NT, E0])
        r2 = sb("r2", [P, NT, E0])
        parts = sb("parts", [P, NT, 3 * E0], BF16)
        identb = sb("identb", [P, P], BF16)
        hr = sb("hr", [P, 2, G])
        hh = sb("hh", [P, 3, G])

        minus_half = sb("minus_half", [P, E1])
        expdec = sb("expdec", [P, L])
        negdec = sb("negdec", [P, L])

        def ones_half(n):
            return minus_half[:, 0:n]

        def dec_col(l):
            return expdec[:, l:l + 1]

        def fixed(eng):
            eng.wait_ge(S["const_in"], 16)

        def Ccol(i):
            return vec[:, L, i:i + 1]

        def group(buf, g):
            return buf[:, (g - 1) * G:g * G] if isinstance(g, int) else buf[:, bass.ds((g - 1) * G, G)]

        block = ctx.enter_context(nc.Block())

        dram = ins

        @block.sync
        def _(sp):
            sp.dma_start(consts[:, :], dram["consts"]).then_inc(S["const_in"], 16)
            for g in range(1, NG + 1):
                sp.dma_start(group(x, g), dram["x"][:, (g - 1) * G:g * G]).then_inc(S[f"x_in_{g}"], 16)
            sp.dma_start(wv[:, :], dram["wv"]).then_inc(S["wqkv_in"], 16)
            sp.dma_start(wq[:, :], dram["wq"]).then_inc(S["wqkv_in"], 16)
            sp.dma_start(wk[:, :], dram["wk"]).then_inc(S["wqkv_in"], 16)
            sp.dma_start(wfeat[:, :, :], dram["wfeat"]).then_inc(S["wfeat_in"], 16)
            sp.dma_start(wo[:, :, :], dram["wo"]).then_inc(S["wo_in"], 16)
            sp.dma_start(vec[:, :, :], dram["vec"]).then_inc(S["vec_in"], 16)
            sp.dma_start(esel[:, :], dram["esel"]).then_inc(S["esel_in"], 16)
            sp.dma_start(self32[:, :], dram["sel0"]).then_inc(S["sel0_in"], 16)
            sp.dma_start(keys, dram["keys"]).then_inc(S["keys_in"], 16)
            sp.dma_start(vals, dram["vals"]).then_inc(S["vals_in"], 16)
            sp.dma_start(wrwkv[:, :, :, :], dram["wrwkv"]).then_inc(S["wrwkv_in"], 16)
            sp.dma_start(rgate[:, :], dram["rgate"]).then_inc(S["rgate_in"], 16)
            sp.dma_start(wgu, dram["wgu"]).then_inc(S["wgu_in"], 16)
            sp.dma_start(wdn, dram["wdn"]).then_inc(S["wdn_in"], 16)
            sp.wait_ge(S["sel_ready"], 1)
            sp.dma_start(self32[0:3 * E1, 0:(C1 - 1) * P], dram["sel1"]).then_inc(S["sel1_in"], 16)
            with sp.Fori(1, NG + 1) as g:
                sp.wait_ge(S["y_added"], g + 1)
                sp.dma_start(out[:, bass.ds((g - 1) * G, G)], x[:, bass.ds((g - 1) * G, G)]).then_inc(S["out_stored"], 16)
            sp.wait_ge(S["out_stored"], 16 * NG)

        rs = sb("rs", [P, N])
        h1 = stack[:, :, :, :].rearrange("p a b c -> p (a b c)")[:, 0:SEQ * T1].rearrange("p (s t) -> p s t", s=SEQ)
        h2 = stack[:, :, :, :].rearrange("p a b c -> p (a b c)")[:, 1024:1024 + SEQ * T1].rearrange("p (s t) -> p s t", s=SEQ)
        fb = feat[:, :, :, :, :].rearrange("p a b c d -> p (a b c) d")
        va = v_aug[:, :, :, :].rearrange("p a b c -> p (a b c)")
        hn1, dif1 = fb[:, 0, :], fb[:, 1, :]
        xk, xv, xr = fb[:, 2, :], fb[:, 3, :], fb[:, 4, :]
        hn2, dif2 = fb[:, 5, :], fb[:, 6, :]
        xck = fb[:, 7, :]
        xcr = yt[:, :]
        kp = [va[:, i * 514:(i + 1) * 514] for i in range(2)]
        vs = [va[:, 1028 + i * G:1028 + (i + 1) * G] for i in range(2)]
        er = [va[:, 2052 + i * G:2052 + (i + 1) * G] for i in range(2)]
        pm = va[:, 3076:3076 + 514]
        dec = va[:, 3590:3590 + 514]
        W2 = SEQ * T1
        d2 = big[:, 6 * W2:6 * W2 + G]
        e3b = big[:, 0 * W2:1 * W2]
        e4b = big[:, 1 * W2:2 * W2]
        kvb = big[:, 2 * W2:3 * W2]
        aa = big[:, 3 * W2:4 * W2]
        bb = big[:, 4 * W2:5 * W2]
        reset = big[:, 5 * W2:6 * W2]
        a1, a2 = wq[:, 0:G], wq[:, G:2 * G]
        d1, e1 = wk[:, 0:G], wk[:, G:2 * G]
        e2, t1 = wv[:, 0:G], wv[:, G:2 * G]
        wof = wo[:, :, :].rearrange("p a b -> p (a b)")
        t2, t3 = wof[:, 0:G], wof[:, G:2 * G]
        scf = scores[:, :, :].rearrange("p a b -> p (a b)")
        dn, dn2, rec = scf[:, 0:G], scf[:, G:2 * G], scf[:, 2 * G:3 * G]
        num = hr[:, 0, :]
        rw = hr[:, 1, :]
        ckr = lnsq
        sq1, rs1 = hh[:, 0, :], hh[:, 1, :]
        sq2, rs2 = hh[:, 2, :], ng[:, :]
        ecr = lnr[:, 0, :]
        scr = lnr[:, 1, :]
        rcr = lnr[:, 2, :]
        kvg = lnr[:, 3, :]

        def seqs(ap):
            return ap.rearrange("p (s t) -> p s t", s=SEQ)

        def cur(buf):
            return buf.rearrange("p (s t) -> p s t", s=SEQ)[:, :, 1:T1]

        def prev(buf):
            return buf.rearrange("p (s t) -> p s t", s=SEQ)[:, :, 0:T]

        ITEMS = L * NG
        STEPS = ITEMS + 3

        SIDE0 = (lnsq[:, 0, :], lnsq[:, 1, :], lnsq[:, 2, :], lnr[:, 0, :])
        SIDE1 = (xk, xv, xr, hn1)
        tokens_sq = dif1
        twice = lnsq[:, 3, :]

        def norm_moe0(j):
            return NG + j

        def norm_pre(j):
            return 2 * NG + 2 * j - 1

        def norm_ln0(j):
            return 2 * NG + 2 * j

        def norm_moe1(j):
            return 4 * NG + j

        @block.tensor
        def _(pe):
            def center_group(i, src, b):
                if not isinstance(i, int) or i > NG:
                    pe.wait_ge(S["ln_logged"], i - 1)
                pe.matmul(bank[b][:, :], center, src, start=True, stop=True).then_inc(S["ln_centered"], 1)

            def variance_group(i, sq, b):
                pe.wait_ge(S["ln_squared"], i)
                pe.matmul(bank[b][:, :], mean, sq, start=True, stop=True).then_inc(S["ln_var"], 1)

            def logits(n, E, b):
                static, sq, w = (SIDE0[2], None, esel) if E == E0 else (SIDE1[2], tokens_sq, rgate)
                cols = E0 if E == E0 else E1 + 1
                fixed(pe)
                pe.wait_ge(S["rng_ready"], n + 1)
                if E == E1:
                    pe.wait_ge(S["sq_ready"], n - NG + 1)
                for t in range(NT):
                    mm = pe.matmul(bank[b][:, t * cols:t * cols + E], static[:, t * P:(t + 1) * P], w[:, :],
                                   start=True, stop=True)
                    if E == E1:
                        mm = pe.matmul(bank[b][:, t * cols + E:t * cols + E + 1], sq[:, t * P:(t + 1) * P],
                                       ones[:, 0:1], start=True, stop=True)
                mm.then_inc(S["logit_done"], 1)

            def turn_gates(n, E, b):
                fixed(pe)
                pe.wait_ge(S["parts_ready"], n + 1)
                for t in range(NT):
                    mm = pe.transpose(bank[b][0:3 * E, :].bitcast(BF16)[:, t * P:(t + 1) * P],
                                      parts[:, t, 0:3 * E], identb[:, :])
                mm.then_inc(S["gt_done"], 1)

            pe.wait_ge(S["const_in"], 16)
            for g in range(1, NG + 1):
                pe.wait_ge(S[f"x_in_{g}"], 16)
                center_group(g, group(x, g), g - 1)
                if g >= 2:
                    variance_group(g - 1, lnsq[:, g - 2, :], NG + g - 2)
            variance_group(NG, lnsq[:, NG - 1, :], 2 * NG - 1)

            pe.wait_ge(S["ln_normed"], NG)
            pe.wait_ge(S["wqkv_in"], 48)
            pe.wait_ge(S["wfeat_in"], 16)
            pe.wait_ge(S["wo_in"], 16)
            pe.wait_ge(S["esel_in"], 16)
            PROJ, FEAT, SC, AV, YT, OUT = (0, 1), (2, 3), 4, 5, 6, 7

            def values(g, k):
                if k == 0:
                    pe.wait_ge(S["ng_ready"], g + 1)
                if k < 2:
                    pe.wait_ge(S["stack_odd"], 16 * g)
                    pe.wait_ge(S["stack_even"], 16 * g)
                else:
                    pe.wait_ge(S["v_evac"], 8 * g + k - 1)
                t, half = k % NT, k // NT
                pe.matmul(bank[PROJ[k % 2]][:, :], ng[:, t * P:(t + 1) * P], wv[:, half * G:(half + 1) * G],
                          start=True, stop=True).then_inc(S["v_done"], 1)

            def attend_group(g, first, final):
                def proj(p, s):
                    if p == 0:
                        pe.wait_ge(S["v_evac"], 8 * g + 7 + s)
                    else:
                        pe.wait_ge(S["stack_odd"], 16 * g + 2 * (p - 1) + s + 1)
                        pe.wait_ge(S["stack_even"], 16 * g + 2 * (p - 1) + s + 1)
                    w = wq if s == 0 else wk
                    pe.matmul(bank[PROJ[s]][:, :], w[:, p * P:(p + 1) * P], ng[:, :], start=True,
                              stop=True).then_inc(S["proj_done"], 1)

                def features(p, s, h):
                    f = 4 * p + 2 * s + h
                    pe.wait_ge(S["stack_odd"], 16 * g + 2 * p + s + 1)
                    pe.wait_ge(S["stack_even"], 16 * g + 2 * p + s + 1)
                    pe.wait_ge(S["feat_exp"], 32 * g + max(f - 1, 0))
                    pe.matmul(bank[FEAT[f % 2]][:, :], wfeat[:, h, :], stack[:, s, h, :], start=True,
                              stop=True).then_inc(S["feat_done"], 1)

                def score(p, i):
                    b, h = i // 2, i % 2
                    fq, fk = feat[:, p % 2, 0, h, :], feat[:, p % 2, 1, h, :]
                    pe.wait_ge(S["feat_exp"], 32 * g + 4 * p + 4)
                    pe.wait_ge(S["masked"], 32 * g + 4 * p + i)
                    pe.matmul(bank[SC][:, 0:T], fk[:, b * T:b * T + P], fq[:, b * T:(b + 1) * T],
                              start=True, stop=True)
                    pe.matmul(bank[SC][:, T:T + P], fk[:, b * T + P:(b + 1) * T],
                              fq[:, b * T + P:(b + 1) * T], start=True, stop=True).then_inc(S["score_done"], 1)

                def attend(p, b):
                    pe.wait_ge(S["masked"], 32 * g + 4 * p + 2 * b + 2)
                    pe.wait_ge(S["ynormed"], 16 * g + 2 * p + b)
                    W = HD + 1
                    for h in range(2):
                        sc = scores[:, 2 * b + h, :]
                        o = bank[AV][:, 2 * h * W:(2 * h + 1) * W]
                        pe.matmul(o, sc[:, 0:P], v_aug[:, 2 * b, 2 * p + h, :], start=True, stop=True)
                        o = bank[AV][:, (2 * h + 1) * W:(2 * h + 2) * W]
                        pe.matmul(o, sc[:, P:2 * P], v_aug[:, 2 * b, 2 * p + h, :], start=True, stop=False)
                        mm = pe.matmul(o, sc[:, 2 * P:3 * P], v_aug[:, 2 * b + 1, 2 * p + h, :],
                                       start=False, stop=True)
                    mm.then_inc(S["av_done"], 1)

                def turn(p):
                    pe.wait_ge(S["ynormed"], 16 * g + 2 * p + 2)
                    pe.wait_ge(S["yt_copied"], 8 * g + p)
                    for t in range(NT):
                        mm = pe.transpose(bank[YT][:, t * P:(t + 1) * P],
                                          ynorm[:, t, :, :].rearrange("p h e -> p (h e)"), ident)
                    mm.then_inc(S["yt_done"], 1)

                def project_out(p):
                    pe.wait_ge(S["yt_copied"], 8 * g + p + 1)
                    if p == 0:
                        pe.wait_ge(S["x1_added"], g)
                        pe.wait_ge(S["gt_copied"], g)
                    pe.matmul(bank[OUT][:, :], wo[:, p, :], yt[:, :], start=(p == 0),
                              stop=(p == NP - 1)).then_inc(S["wo_done"], 1)

                j = g - 1
                for p in range(NP + 2):
                    a, c, d = p < NP, 1 <= p <= NP, p >= 2
                    side = not first
                    if a:
                        proj(p, 0)
                    if side and p == 0:
                        pe.wait_ge(S["x1_added"], j + 1)
                        center_group(norm_moe0(j), group(x, j), OUT)
                    if c:
                        score(p - 1, 0)
                    if side and p == 2:
                        turn_gates(j, E0, OUT)
                    if p == NP and not final:
                        values(g + 1, 0)
                    if p == NP + 1 and not final:
                        values(g + 1, 4)
                    if d:
                        turn(p - 2)
                    if c:
                        score(p - 1, 1)
                    if a:
                        proj(p, 1)
                    if p == NP and not final:
                        values(g + 1, 1)
                    if p == NP + 1 and not final:
                        values(g + 1, 5)
                    if side and p == 1:
                        logits(j, E0, OUT)
                    if d:
                        project_out(p - 2)
                    if c:
                        score(p - 1, 2)
                    if p == NP and not final:
                        values(g + 1, 2)
                    if a:
                        features(p, 0, 0)
                    if c:
                        attend(p - 1, 0)
                        score(p - 1, 3)
                    if p == NP and not final:
                        values(g + 1, 3)
                    if a:
                        features(p, 0, 1)
                    if side and p == 0:
                        variance_group(norm_moe0(j), SIDE0[0], OUT)
                    if a:
                        features(p, 1, 0)
                    if c:
                        attend(p - 1, 1)
                    if a:
                        features(p, 1, 1)
                    if p == NP + 1 and not final:
                        values(g + 1, 6)
                        values(g + 1, 7)

            for k in range(2 * NT):
                values(1, k)
            attend_group(1, True, False)
            with pe.Fori(1, NG - 1) as j:
                attend_group(j + 1, False, False)
            attend_group(NG, False, True)

            pe.wait_ge(S["keys_in"], 16)
            pe.wait_ge(S["vals_in"], 16)
            pe.wait_ge(S["sel_ready"], 1)
            SIDE = 7

            def experts0(g, first):
                pe.wait_ge(S["gt_copied"], g + 1)

                def up(c):
                    pe.wait_ge(S["relu_done"], 16 * g + max(c - 1, 0))
                    pe.matmul(bank[2 + c % 2][:, :], keys[:, c * P:(c + 1) * P], group(nrm, g),
                              start=True, stop=True).then_inc(S["up_done"], 1)
                    pe.wait_ge(S["h_done"], 16 * g + max(c - 1, 0))
                    pe.matmul(bank[4 + c % 2][:, :], sel[:, c * P:(c + 1) * P], group(gt, g),
                              start=True, stop=True).then_inc(S["gbc_done"], 1)

                def down(c):
                    if c == 0:
                        pe.wait_ge(S["x2_added"], g)
                    pe.wait_ge(S["h_done"], 16 * g + c + 1)
                    pe.matmul(bank[6][:, :], vals[:, c, :], hh[:, c % 3, :], start=(c == 0),
                              stop=(c == C0 - 1)).then_inc(S["down_done"], 1)

                for c in range(C0 + 2):
                    if c < C0:
                        up(c)
                    if c >= 2:
                        down(c - 2)
                    if first:
                        if c == 1:
                            pe.wait_ge(S["x1_added"], NG + 1)
                            center_group(norm_moe0(NG), group(x, NG), SIDE)
                        if c == 3:
                            variance_group(norm_moe0(NG), SIDE0[0], SIDE)
                        if c == 6:
                            logits(NG, E0, SIDE)
                        if c == 12:
                            turn_gates(NG, E0, SIDE)
                    else:
                        j = g - 1
                        if c == 1:
                            pe.wait_ge(S["x2_added"], j + 1)
                            pe.wait_ge(S["gt_copied"], NG + 1)
                            center_group(norm_pre(j), group(x, j), SIDE)
                        if c == 3:
                            variance_group(norm_pre(j), SIDE0[0], SIDE)
                        if c == 6:
                            pe.wait_ge(S["ln_normed"], norm_pre(j))
                            center_group(norm_ln0(j), SIDE0[2], SIDE)
                        if c == 8:
                            variance_group(norm_ln0(j), SIDE0[0], SIDE)

            experts0(1, True)
            with pe.Fori(1, NG) as j:
                experts0(j + 1, False)

            pe.wait_ge(S["wrwkv_in"], 16)
            CEN1, CEN2, VAR, OV, KCR, RCV = 0, 1, 2, 3, 4, 5

            def center1(n):
                g = n % NG
                if n < NG:
                    pe.wait_ge(S["ln0_affined"], n + 1)
                else:
                    pe.wait_ge(S["x_out"], n - NG + 1)
                if n >= 1:
                    pe.wait_ge(S["normed1"], n)
                pe.matmul(bank[CEN1][:, :], center, rs[:, g * G:(g + 1) * G], start=True,
                          stop=True).then_inc(S["centered1"], 1)

            def variance1(n):
                pe.wait_ge(S["squared1"], n + 1)
                if n >= 3:
                    pe.wait_ge(S["logged2"], n - 2)
                pe.matmul(bank[VAR][:, :], mean, sq1, start=True, stop=True).then_inc(S["var1"], 1)

            def kvr(n):
                for i, (b, src) in enumerate(((KCR, xk), (OV, xv), (RCV, xr))):
                    pe.wait_ge(S["mixed1"], 3 * n + i + 1)
                    if n >= 1:
                        pe.wait_ge(S[("k_copied", "v_copied", "r_bounded")[i]], n)
                    lag = (3, 2, 3)[i]
                    if n >= lag:
                        pe.wait_ge(S[("cr_bounded", "x_mid", "kv_gated")[i]], n - lag + 1)
                    pe.matmul(bank[b][:, :], wrwkv[:, n // NG, i, :], src, start=True,
                              stop=True).then_inc(S["kvr_done"], 1)

            def output(n):
                pe.wait_ge(S["rw_done"], n + 1)
                pe.wait_ge(S["v_copied"], min(n + 2, ITEMS))
                pe.matmul(bank[OV][:, :], wrwkv[:, n // NG, 3, :], rw, start=True, stop=True).then_inc(S["o_done"], 1)

            def center2(n):
                g = n % NG
                pe.wait_ge(S["x_mid"], n + 1)
                if n >= 1:
                    pe.wait_ge(S["normed2"], n)
                pe.matmul(bank[CEN2][:, :], center, rs[:, g * G:(g + 1) * G], start=True,
                          stop=True).then_inc(S["centered2"], 1)

            def variance2(n):
                pe.wait_ge(S["squared2"], n + 1)
                pe.wait_ge(S["logged1"], min(n + 3, ITEMS))
                pe.matmul(bank[VAR][:, :], mean, sq2, start=True, stop=True).then_inc(S["var2"], 1)

            def ffn_gate(n):
                pe.wait_ge(S["mixed2"], 2 * n + 1)
                pe.wait_ge(S["k_copied"], min(n + 3, ITEMS))
                pe.matmul(bank[KCR][:, :], wrwkv[:, n // NG, 8, :], xcr, start=True,
                          stop=True).then_inc(S["cr_done"], 1)

            def ffn_up(n, j):
                pe.wait_ge(S["mixed2"], 2 * n + 2)
                if 4 * n + j >= 2:
                    pe.wait_ge(S["ck_relu"], 4 * n + j - 1)
                pe.matmul(bank[6 + j % 2][:, :], wrwkv[:, n // NG, 4 + j, :], xck, start=True,
                          stop=True).then_inc(S["ck_done"], 1)

            def ffn_down(n, j):
                pe.wait_ge(S[("even_squared", "odd_squared")[j % 2]], 2 * n + j // 2 + 1)
                if j == 0:
                    pe.wait_ge(S["r_bounded"], min(n + 3, ITEMS))
                mm = pe.matmul(bank[RCV][:, :], wrwkv[:, n // NG, 9 + j, :], ckr[:, j, :], start=(j == 0),
                               stop=(j == FC - 1))
                if j == FC - 1:
                    mm.then_inc(S["cv_done"], 1)

            def before_rwkv(s):
                if s == 0:
                    pe.wait_ge(S["x2_added"], NG + 1)
                    center_group(norm_pre(NG), group(x, NG), SIDE)
                if s == 1:
                    variance_group(norm_pre(NG), SIDE0[0], SIDE)
                if s == 2:
                    pe.wait_ge(S["ln_normed"], norm_pre(NG))
                    center_group(norm_ln0(NG), SIDE0[2], SIDE)
                if s == 3:
                    variance_group(norm_ln0(NG), SIDE0[0], SIDE)

            def after_rwkv(j):
                pe.wait_ge(S["x3_added"], j)
                if j == 3:
                    pe.wait_ge(S["x_mid"], ITEMS)
                center_group(norm_moe1(j), group(x, j), TAIL[j - 1])

            TAIL = (CEN1, CEN1, OV)
            for s in range(STEPS):
                a, m, f = s < ITEMS, 2 <= s < ITEMS + 2, s >= 3
                if s < 2:
                    before_rwkv(2 * s)
                if s == ITEMS:
                    pe.wait_ge(S["gw_sq"], 1)
                    pe.wait_ge(S["normed1"], ITEMS)
                    pe.matmul(bank[CEN1][:, 0:E1], ones, msk[:, 0, 0:E1], start=True,
                              stop=True).then_inc(S["gw_ss"], 1)
                    pe.wait_ge(S["gw_guard"], 1)
                if s >= ITEMS:
                    after_rwkv(s - ITEMS + 1)
                if a:
                    center1(s)
                if f:
                    ffn_gate(s - 3)
                    ffn_up(s - 3, 0)
                if a:
                    variance1(s)
                if f:
                    ffn_up(s - 3, 1)
                if m:
                    output(s - 2)
                if f:
                    ffn_up(s - 3, 2)
                    ffn_up(s - 3, 3)
                if m:
                    center2(s - 2)
                if s < 2:
                    before_rwkv(2 * s + 1)
                if f:
                    ffn_down(s - 3, 0)
                    ffn_down(s - 3, 1)
                if s >= ITEMS:
                    variance_group(norm_moe1(s - ITEMS + 1), SIDE1[0], TAIL[s - ITEMS])
                if m:
                    variance2(s - 2)
                if f:
                    ffn_down(s - 3, 2)
                    ffn_down(s - 3, 3)
                if a:
                    kvr(s)
                if s == ITEMS + 1:
                    pe.wait_ge(S["rgate_in"], 16)
                    pe.wait_ge(S["ln_normed"], norm_moe1(2))
                    logits(NG + 1, E1, CEN1)

            pe.wait_ge(S["x3_added"], NG)
            pe.wait_ge(S["ck_relu"], FC * ITEMS)
            center_group(norm_moe1(NG), group(x, NG), SIDE)
            turn_gates(NG + 1, E1, CEN1)
            pe.wait_ge(S["wgu_in"], 16)
            pe.wait_ge(S["wdn_in"], 16)
            pe.wait_ge(S["sel_ready"], 2)
            variance_group(norm_moe1(NG), SIDE1[0], SIDE)

            def experts1(g, final):
                pe.wait_ge(S["gt_copied"], NG + g + 1)

                def up1(c):
                    m = P
                    fixed(pe)
                    pe.wait_ge(S["silu_done"], C1 * g + max(c - 1, 0))
                    pe.matmul(bank[0 + c % 2][0:m, :], wgu[:, 0, c * P:c * P + m], group(nrm, g),
                              start=True, stop=True).then_inc(S["g_done"], 1)
                    fixed(pe)
                    pe.wait_ge(S["su_done"], C1 * g + max(c - 1, 0))
                    pe.matmul(bank[2 + c % 2][0:m, :], wgu[:, 1, c * P:c * P + m], group(nrm, g),
                              start=True, stop=True).then_inc(S["u_done"], 1)
                    if c < C1 - 1:
                        fixed(pe)
                        pe.wait_ge(S["h1_done"], C1 * g + max(c - 1, 0))
                        pe.matmul(bank[4 + c % 2][:, :], sel[0:3 * E1, c * P:(c + 1) * P],
                                  group(gt[0:3 * E1, :], g), start=True, stop=True).then_inc(S["cbc_done"], 1)

                def down1(c):
                    m = P
                    if c == 0:
                        pe.wait_ge(S["y_added"], g)
                    pe.wait_ge(S["h1_done"], C1 * g + c + 1)
                    pe.matmul(bank[6][:, :], wdn[0:m, c, :], hh[0:m, c % 3, :], start=(c == 0),
                              stop=(c == C1 - 1)).then_inc(S["down1_done"], 1)

                for c in range(C1 + 2):
                    if c < C1:
                        up1(c)
                    if c >= 2:
                        down1(c - 2)
                    if not final and c == 3:
                        pe.wait_ge(S["gt_copied"], NG + g + 1)
                        pe.wait_ge(S["ln_normed"], 5 * NG)
                        logits(NG + g + 1, E1, SIDE)
                    if not final and c == 8:
                        turn_gates(NG + g + 1, E1, SIDE)

            with pe.Fori(1, NG) as g:
                experts1(g, False)
            experts1(NG, True)

        @block.scalar
        def _(act):
            nc.scalar.preload_act_table_set("natural_log_exp_and_others")
            act.wait_ge(S["vec_in"], 16)

            def square_group(i, side, b):
                act.wait_ge(S["ln_centered"], i)
                act.wait_ge(S["ln_var"], i - 1)
                act.wait_ge(S["ln_normed"], i - 1)
                act.activation(side[0], bank[b][:, :], ACT.Square)
                act.activation(side[1], bank[b][:, :], ACT.Identity).then_inc(S["ln_squared"], 1)

            def rstd_group(i, side, b):
                act.wait_ge(S["ln_var"], i)
                act.wait_ge(S["ln_normed"], i - 1)
                act.activation(side[3], bank[b][:, :], ACT.Ln, bias=Ccol(0)).then_inc(S["ln_logged"], 1)
                act.wait_ge(S["ln_logged"], i)
                act.activation(side[3], side[3], ACT.Exp, scale=-0.5).then_inc(S["ln_rstd"], 1)

            def gate_exp(n, E, by_tanh=False):
                if E == E1:
                    act.wait_ge(S["logit_scaled"], 2 * (n - NG) + 2)
                else:
                    act.wait_ge(S["logit_bounded"], n + 1)
                act.wait_ge(S["gate_sum"], n)
                src = gn if E == E0 else lg
                act.activation(ex[:, :, 0:E], src[:, :, 0:E], ACT.Tanh if by_tanh else ACT.Exp,
                               scale=0.5 if by_tanh else -1.0).then_inc(S["gate_exp"], 1)

            def square_tokens(n):
                act.wait_ge(S["rng_ready"], n + 1)
                act.wait_ge(S["logit_done"], n)
                act.activation(tokens_sq, SIDE1[2], ACT.Square).then_inc(S["sq_ready"], 1)

            for g in range(1, NG + 1):
                act.wait_ge(S["ln_centered"], g)
                act.activation(lnsq[:, g - 1, :], bank[g - 1][:, :], ACT.Square).then_inc(S["ln_squared"], 1)
                for i in ([g - 1] if g < NG else [g - 1, g]):
                    if i:
                        act.wait_ge(S["ln_var"], i)
                        act.activation(lnr[:, i - 1, :], bank[NG + i - 1][:, :], ACT.Ln,
                                       bias=Ccol(0)).then_inc(S["ln_logged"], 1)
                        act.wait_ge(S["ln_logged"], i)
                        act.activation(lnr[:, i - 1, :], lnr[:, i - 1, :], ACT.Exp, scale=-0.5).then_inc(S["ln_rstd"], 1)

            PROJ, FEAT, OUT = (0, 1), (2, 3), 7

            def attend_group(g, side):
                def squares(p, s):
                    act.wait_ge(S["proj_done"], 16 * g + 2 * p + s + 1)
                    act.wait_ge(S["feat_done"], 32 * g + (4 * (p - 1) + 2 * s + 2 if p else 0))
                    act.activation(stack[0:64, s, 0, :], bank[PROJ[s]][0:64, :], ACT.Identity)
                    act.activation(stack[64:128, s, 0, :], bank[PROJ[s]][0:64, :],
                                   ACT.Square).then_inc(S["stack_even"], 1)

                def exps(p, s):
                    for f in range(4 * p + 2 * s, 4 * p + 2 * s + 2):
                        act.wait_ge(S["feat_done"], 32 * g + f + 1)
                        act.wait_ge(S["score_done"], 32 * g + (4 * (p - 1) if p >= 2 else 0))
                        act.activation(feat[:, p % 2, (f // 2) % 2, f % 2, :], bank[FEAT[f % 2]][:, :],
                                       ACT.Exp).then_inc(S["feat_exp"], 1)

                j = g - 1
                for p in range(NP):
                    squares(p, 0)
                    if side and p == 0:
                        square_group(norm_moe0(j), SIDE0, OUT)
                    squares(p, 1)
                    exps(p, 0)
                    if side and p == 0:
                        rstd_group(norm_moe0(j), SIDE0, OUT)
                    if side and p == 1:
                        gate_exp(j, E0)
                    exps(p, 1)

            attend_group(1, False)
            with act.Fori(1, NG - 1) as j:
                attend_group(j + 1, True)
            attend_group(NG, True)

            SIDE = 7

            def ln0_affine(j):
                act.wait_ge(S["ln_normed"], norm_ln0(j))
                act.activation(group(rs, j), twice, ACT.Identity, bias=Ccol(2),
                               scale=Ccol(1)).then_inc(S["ln0_affined"], 1)

            def experts0(g, first):
                for c in range(C0):
                    act.wait_ge(S["up_done"], 16 * g + c + 1)
                    act.wait_ge(S["h_done"], 16 * g + max(c - 1, 0))
                    act.activation(hr[:, c % 2, :], bank[2 + c % 2][:, :], ACT.Relu).then_inc(S["relu_done"], 1)
                    if first:
                        if c == 1:
                            square_group(norm_moe0(NG), SIDE0, SIDE)
                        if c == 3:
                            rstd_group(norm_moe0(NG), SIDE0, SIDE)
                        if c == 7:
                            gate_exp(NG, E0)
                    else:
                        if c == 1:
                            square_group(norm_pre(g - 1), SIDE0, SIDE)
                        if c == 3:
                            rstd_group(norm_pre(g - 1), SIDE0, SIDE)
                        if c == 6:
                            square_group(norm_ln0(g - 1), SIDE0, SIDE)
                        if c == 8:
                            rstd_group(norm_ln0(g - 1), SIDE0, SIDE)
                        if c == 11:
                            ln0_affine(g - 1)

            experts0(1, True)
            with act.Fori(1, NG) as j:
                experts0(j + 1, False)

            for l in range(L):
                act.activation(dec_col(l), vec[:, l, DECAY:DECAY + 1], ACT.Exp).then_inc(S["decay_exp"], 1)

            def square1(n):
                act.wait_ge(S["centered1"], n + 1)
                if n >= 1:
                    act.wait_ge(S["var1"], n)
                act.activation(sq1, bank[0][:, :], ACT.Square).then_inc(S["squared1"], 1)

            def rstd1(n):
                act.wait_ge(S["var1"], n + 1)
                if n >= 1:
                    act.wait_ge(S["normed1"], n)
                act.activation(rs1, bank[2][:, :], ACT.Ln, bias=Ccol(0)).then_inc(S["logged1"], 1)
                act.wait_ge(S["logged1"], n + 1)
                act.activation(rs1, rs1, ACT.Exp, scale=-0.5).then_inc(S["rstd1"], 1)

            def affine1(n):
                l = n // NG
                act.wait_ge(S["normed1"], n + 1)
                if n >= 1:
                    act.wait_ge(S["mixed1"], 3 * n)
                act.activation(h1[:, :, 1:T1], seqs(hn1), ACT.Identity, bias=vec[:, l, LNB:LNB + 1],
                               scale=vec[:, l, LNW:LNW + 1]).then_inc(S["affined1"], 1)

            def copy_kv(n):
                act.wait_ge(S["kvr_done"], 3 * n + 1)
                if n >= 2:
                    act.wait_ge(S["rw_done"], n - 1)
                act.activation(cur(kp[n % 2]), seqs(bank[4][:, :]), ACT.Identity).then_inc(S["k_copied"], 1)
                act.wait_ge(S["kvr_done"], 3 * n + 2)
                act.activation(vs[n % 2], bank[3][:, :], ACT.Identity).then_inc(S["v_copied"], 1)

            def receptance(n):
                act.wait_ge(S["r_bounded"], n + 1)
                act.activation(er[n % 2], er[n % 2], ACT.Exp, scale=-1.0).then_inc(S["r_exp"], 1)

            def state_exps(n):
                act.wait_ge(S["a1_done"], n + 1)
                if n >= 1:
                    act.wait_ge(S["rw_done"], n)
                act.activation(cur(e3b[:, :]), seqs(a1), ACT.Exp).then_inc(S["e3_done"], 1)
                act.wait_ge(S["a2_done"], n + 1)
                act.activation(cur(e4b[:, :]), seqs(a2), ACT.Exp).then_inc(S["e4_done"], 1)

            def output_exps(n):
                act.wait_ge(S["d_above"], n + 1)
                act.activation(e1, d1, ACT.Exp, scale=-1.0).then_inc(S["e1_done"], 1)
                act.wait_ge(S["d_below"], n + 1)
                act.activation(e2, d2, ACT.Exp).then_inc(S["e2_done"], 1)

            def invert_den(n):
                act.wait_ge(S["den2_done"], n + 1)
                act.activation(rec, dn2, ACT.Ln).then_inc(S["den_logged"], 1)
                act.wait_ge(S["den_logged"], n + 1)
                act.activation(rec, rec, ACT.Exp, scale=-1.0).then_inc(S["rec_done"], 1)

            def square2(n):
                act.wait_ge(S["centered2"], n + 1)
                if n >= 1:
                    act.wait_ge(S["var2"], n)
                act.activation(sq2, bank[1][:, :], ACT.Square).then_inc(S["squared2"], 1)

            def rstd2(n):
                act.wait_ge(S["var2"], n + 1)
                if n >= 1:
                    act.wait_ge(S["normed2"], n)
                act.activation(rs2, bank[2][:, :], ACT.Ln, bias=Ccol(0)).then_inc(S["logged2"], 1)
                act.wait_ge(S["logged2"], n + 1)
                act.activation(rs2, rs2, ACT.Exp, scale=-0.5).then_inc(S["rstd2"], 1)

            def affine2(n):
                l = n // NG
                act.wait_ge(S["normed2"], n + 1)
                if n >= 1:
                    act.wait_ge(S["mixed2"], 2 * n)
                act.activation(h2[:, :, 1:T1], seqs(hn2), ACT.Identity, bias=vec[:, l, LN2B:LN2B + 1],
                               scale=vec[:, l, LN2W:LN2W + 1]).then_inc(S["affined2"], 1)

            def relu(n, j):
                act.wait_ge(S["ck_done"], 4 * n + j + 1)
                if n >= 1 and j == 0:
                    act.wait_ge(S["cv_done"], n)
                act.activation(ckr[:, j, :], bank[6 + j % 2][:, :], ACT.Relu).then_inc(S["ck_relu"], 1)

            def ffn_sigmoid(n):
                act.wait_ge(S["cr_bounded"], n + 1)
                act.activation(ecr, ecr, ACT.Exp, scale=-1.0).then_inc(S["cr_exp"], 1)
                act.wait_ge(S["cr_exp"], n + 1)
                act.activation(ecr, ecr, ACT.Ln, bias=1.0).then_inc(S["cr_logged"], 1)
                act.wait_ge(S["cr_logged"], n + 1)
                act.activation(scr, ecr, ACT.Exp, scale=-1.0).then_inc(S["cr_sig"], 1)

            for s in range(STEPS):
                a, w, m, f = s < ITEMS, 1 <= s <= ITEMS, 2 <= s < ITEMS + 2, s >= 3
                if w:
                    receptance(s - 1)
                if a:
                    square1(s)
                if s == 0:
                    square_group(norm_pre(NG), SIDE0, SIDE)
                if s == 1:
                    square_group(norm_ln0(NG), SIDE0, SIDE)
                if s >= ITEMS:
                    square_group(norm_moe1(s - ITEMS + 1), SIDE1, (0, 0, 3)[s - ITEMS])
                if w:
                    state_exps(s - 1)
                if f:
                    relu(s - 3, 0)
                if w:
                    output_exps(s - 1)
                if a:
                    rstd1(s)
                if f:
                    relu(s - 3, 1)
                if a:
                    affine1(s)
                if f:
                    relu(s - 3, 2)
                    relu(s - 3, 3)
                if m:
                    square2(s - 2)
                if w:
                    invert_den(s - 1)
                if s == 0:
                    rstd_group(norm_pre(NG), SIDE0, SIDE)
                if s == 1:
                    rstd_group(norm_ln0(NG), SIDE0, SIDE)
                    ln0_affine(NG)
                if s >= ITEMS:
                    rstd_group(norm_moe1(s - ITEMS + 1), SIDE1, (0, 0, 3)[s - ITEMS])
                if s == ITEMS + 1:
                    square_tokens(NG + 1)
                if s == ITEMS + 2:
                    gate_exp(NG + 1, E1)
                if f:
                    ffn_sigmoid(s - 3)
                if m:
                    rstd2(s - 2)
                    affine2(s - 2)
                if a:
                    copy_kv(s)

            square_group(norm_moe1(NG), SIDE1, SIDE)
            rstd_group(norm_moe1(NG), SIDE1, SIDE)

            def experts1(g, final):
                for c in range(C1):
                    m = P
                    act.wait_ge(S["g_done"], C1 * g + c + 1)
                    act.wait_ge(S["su_done"], C1 * g + max(c - 1, 0))
                    act.activation(hr[0:m, c % 2, :], bank[0 + c % 2][0:m, :], ACT.Silu).then_inc(S["silu_done"], 1)
                    if not final and c == 1:
                        square_tokens(NG + g + 1)
                    if not final and c == 5:
                        gate_exp(NG + g + 1, E1, by_tanh=True)

            with act.Fori(1, NG) as g:
                experts1(g, False)
            experts1(NG, True)

        @block.gpsimd
        def _(pool):
            for count, names in PER_GROUP:
                for name in names:
                    pool.sem_inc(S[name], count)
            pool.wait_ge(S["sel0_in"], 16)
            pool.tensor_copy(sel[:, :], self32[:, :]).then_inc(S["sel_ready"], 1)

            def attention_input(g):
                pool.wait_ge(S["ln_normed"], NG)
                pool.wait_ge(S["proj_done"], 16 * g)
                pool.tensor_copy(ng[:, :], group(nrm, g)).then_inc(S["ng_ready"], 1)

            def routing_input(n, i, dst, g):
                pool.wait_ge(S["ln_normed"], i)
                pool.wait_ge(S["logit_done"], n)
                if dst is SIDE1[2]:
                    pool.wait_ge(S["sq_ready"], n - NG)
                pool.tensor_copy(dst, group(nrm, g)).then_inc(S["rng_ready"], 1)

            def inverse_norms(j):
                pool.wait_ge(S["ss_guard"], j + 1)
                pool.wait_ge(S["logit_scaled"], 2 * j)
                pool.tensor_tensor(gsr[:, :], gsum[:, :], ones_half(NT), ALU.pow).then_inc(S["ss_inv"], 1)

            attention_input(1)
            attention_input(2)
            with pool.Fori(1, NG - 1) as j:
                routing_input(j, norm_moe0(j), SIDE0[2], j)
                attention_input(j + 2)
            routing_input(NG - 1, norm_moe0(NG - 1), SIDE0[2], NG - 1)
            routing_input(NG, norm_moe0(NG), SIDE0[2], NG)

            pool.wait_ge(S["x2_added"], NG + 1)
            pool.memset(h1[:, :, 0:1], 0.0)
            pool.memset(h2[:, :, 0:1], 0.0)
            for i in range(2):
                pool.memset(kp[i].rearrange("p (s t) -> p s t", s=SEQ)[:, :, 0:1], FAR)
            pool.memset(e3b[:, :], 0.0)
            pool.memset(e4b[:, :], 0.0)
            pool.memset(kvb[:, :], 0.0)
            pool.memset(reset[:, :], 0.0).then_inc(S["ones_ready"], 1)
            pool.wait_ge(S["ones_ready"], 1)
            pool.memset(reset[:, :].rearrange("p (s t) -> p s t", s=SEQ)[:, :, 0:1], FAR).then_inc(S["ones_ready"], 1)

            def shift1(n):
                pool.wait_ge(S["affined1"], n + 1)
                if n >= 1:
                    pool.wait_ge(S["mixed1"], 3 * n)
                pool.tensor_tensor(seqs(dif1), h1[:, :, 1:T1], h1[:, :, 0:T], ALU.subtract).then_inc(S["diff1"], 1)

            def key_below_max(n):
                pool.wait_ge(S["p_scanned"], n + 1)
                pool.wait_ge(S["k_copied"], n + 1)
                if n >= 1:
                    pool.wait_ge(S["e4_done"], n)
                pool.tensor_tensor(seqs(a2), cur(kp[n % 2]), cur(pm), ALU.subtract).then_inc(S["a2_done"], 1)

            def own_value(n):
                pool.wait_ge(S["e2_done"], n + 1)
                pool.wait_ge(S["v_copied"], n + 1)
                if n >= 1:
                    pool.wait_ge(S["num_done"], n)
                pool.tensor_tensor(t2, e2, vs[n % 2], ALU.mult).then_inc(S["t2_done"], 1)

            def numerator(n):
                pool.wait_ge(S["t1_done"], n + 1)
                pool.wait_ge(S["t2_done"], n + 1)
                if n >= 1:
                    pool.wait_ge(S["rw_done"], n)
                pool.tensor_tensor(num, t1, t2, ALU.add).then_inc(S["num_done"], 1)

            def shift2(n):
                pool.wait_ge(S["affined2"], n + 1)
                if n >= 1:
                    pool.wait_ge(S["mixed2"], 2 * n)
                pool.tensor_tensor(seqs(dif2), h2[:, :, 1:T1], h2[:, :, 0:T], ALU.subtract).then_inc(S["diff2"], 1)

            def square(n, j):
                pool.wait_ge(S["ck_relu"], 4 * n + j + 1)
                pool.tensor_tensor(ckr[:, j, :], ckr[:, j, :], ckr[:, j, :], ALU.mult).then_inc(S["odd_squared"], 1)

            for s in range(STEPS):
                a, w, m, f = s < ITEMS, 1 <= s <= ITEMS, 2 <= s < ITEMS + 2, s >= 3
                if w:
                    key_below_max(s - 1)
                    own_value(s - 1)
                if f:
                    square(s - 3, 1)
                if a:
                    shift1(s)
                if s == ITEMS:
                    pool.wait_ge(S["gw_guard"], 1)
                    pool.tensor_tensor(gn[:, 3, 0:E1], gn[:, 2, 0:E1], ones_half(E1), ALU.pow).then_inc(S["gw_inv"], 1)
                if s == ITEMS + 2:
                    inverse_norms(1)
                if f:
                    square(s - 3, 3)
                if w:
                    numerator(s - 1)
                if s == ITEMS + 1:
                    routing_input(NG + 1, norm_moe1(1), SIDE1[2], 1)
                if m:
                    shift2(s - 2)

            pool.wait_ge(S["sel1_in"], 16)
            pool.tensor_copy(sel[0:3 * E1, 0:(C1 - 1) * P], self32[0:3 * E1, 0:(C1 - 1) * P]).then_inc(S["sel_ready"], 1)
            with pool.Fori(1, NG) as g:
                routing_input(NG + g + 1, norm_moe1(g + 1), SIDE1[2], g + 1)
                inverse_norms(g + 1)

        @block.vector
        def _(dve):
            def norm_group(i, side, dst):
                dve.wait_ge(S["ln_rstd"], i)
                dve.tensor_tensor(dst, side[1], side[3], ALU.mult).then_inc(S["ln_normed"], 1)

            dve.wait_ge(S["const_in"], 16)
            dve.tensor_copy(identb[:, :], ident)
            dve.memset(minus_half[:, :], -0.5)
            dve.memset(lg[:, :, :], UNUSED)
            dve.memset(top2[:, :, :], UNUSED)
            dve.memset(v_aug[:, :, :, HD:HD + 1], 1.0).then_inc(S["const_ready"], 1)
            dve.wait_ge(S["const_ready"], 1)
            def guard_norms(j, b):
                raw = bank[b][:, 0:NT * (E1 + 1)].rearrange("p (t e) -> p t e", t=NT)
                dve.wait_ge(S["logit_done"], NG + j + 1)
                dve.tensor_scalar(gsum[:, :], raw[:, :, E1], NORM_EPS2, None, ALU.max).then_inc(S["ss_guard"], 1)

            def copy_logits(j, E, K, b):
                base = 0 if E == E0 else NG
                n = base + j + 1
                dve.wait_ge(S["logit_done"], n)
                dve.wait_ge(S["gate_exp"], base + j)
                if E == E0:
                    dve.tensor_copy(lg[:, :, 0:E], bank[b][:, 0:NT * E].rearrange("p (t e) -> p t e", t=NT)
                                    ).then_inc(S["logit_copied"], 1)
                    dve.wait_ge(S["logit_copied"], n)
                    dve.tensor_scalar(gn[:, :, 0:E], lg[:, :, 0:E], SIG_MIN, None,
                                      ALU.max).then_inc(S["logit_bounded"], 1)
                else:
                    raw = bank[b][:, 0:NT * (E + 1)].rearrange("p (t e) -> p t e", t=NT)
                    dve.wait_ge(S["ss_inv"], j + 1)
                    dve.tensor_tensor(lg[:, :, 0:E], raw[:, :, 0:E],
                                      gsr[:, :].unsqueeze(2).to_broadcast([P, NT, E]),
                                      ALU.mult).then_inc(S["logit_scaled"], 1)
                    dve.wait_ge(S["logit_scaled"], 2 * j + 1)
                    dve.tensor_tensor(lg[:, :, 0:E], lg[:, :, 0:E],
                                      gn[:, 3, 0:E].unsqueeze(1).to_broadcast([P, NT, E]),
                                      ALU.mult).then_inc(S["logit_scaled"], 1)
                    dve.wait_ge(S["logit_scaled"], 2 * j + 2)
                    dve.sem_inc(S["logit_copied"], 1)
                    fixed(dve)
                    dve.wait_ge(S["logit_copied"], n)
                for t in range(NT):
                    last = dve.max(top[:, t, :], lg[:, t, 0:E])
                last.then_inc(S["top_found"], 1)

            def choose(j, E, K):
                n = (0 if E == E0 else NG) + j + 1
                if K < 8:
                    dve.wait_ge(S["top_found"], n)
                    dve.tensor_copy(top2[:, :, 0:K], top[:, :, 0:K]).then_inc(S["top_packed"], 1)
                    fixed(dve)
                    dve.wait_ge(S["top_packed"], n)
                else:
                    fixed(dve)
                    dve.wait_ge(S["top_found"], n)
                for t in range(NT):
                    if K < 8:
                        last = dve.match_replace(repl[:, t, :], top2[:, t, :], lg[:, t, :], TAKEN)
                    else:
                        last = dve.match_replace(repl[:, t, 0:E], top[:, t, :], lg[:, t, 0:E], TAKEN)
                last.then_inc(S["top_replaced"], 1)
                dve.wait_ge(S["top_replaced"], n)
                dve.tensor_scalar(msk[:, :, 0:E], repl[:, :, 0:E], TAKEN, None,
                                  ALU.is_equal).then_inc(S["gate_mask"], 1)

            def weigh(j, E, by_tanh=False):
                n = (0 if E == E0 else NG) + j + 1
                dve.wait_ge(S["gate_exp"], n)
                if by_tanh:
                    dve.tensor_scalar(gs[:, :, 0:E], ex[:, :, 0:E], 0.5, None, ALU.mult).then_inc(S["gate_sum"], 1)
                    dve.wait_ge(S["gate_sum"], n)
                    dve.tensor_scalar(gr[:, :, 0:E], gs[:, :, 0:E], 0.5, None, ALU.add).then_inc(S["gate_recip"], 1)
                else:
                    dve.tensor_scalar(gs[:, :, 0:E], ex[:, :, 0:E], 1.0, None, ALU.add).then_inc(S["gate_sum"], 1)
                    dve.wait_ge(S["gate_sum"], n)
                    dve.reciprocal(gr[:, :, 0:E], gs[:, :, 0:E]).then_inc(S["gate_recip"], 1)
                dve.wait_ge(S["gate_recip"], n)
                dve.wait_ge(S["gate_mask"], n)
                dve.tensor_tensor(gm[:, :, 0:E], gr[:, :, 0:E], msk[:, :, 0:E], ALU.mult).then_inc(S["gate_masked"], 1)
                dve.wait_ge(S["gate_masked"], n)
                if E == E1:
                    dve.tensor_reduce(gsum[:, :], gm[:, :, 0:E], AX.X, ALU.add).then_inc(S["gate_norm"], 1)
                    dve.wait_ge(S["gate_norm"], 3 * j + 1)
                    dve.reciprocal(den[:, 0, :], gsum[:, :]).then_inc(S["gate_norm"], 1)
                    dve.wait_ge(S["gate_norm"], 3 * j + 2)
                    dve.tensor_tensor(gr[:, :, 0:E], gm[:, :, 0:E],
                                      den[:, 0, :].unsqueeze(2).to_broadcast([P, NT, E]),
                                      ALU.mult).then_inc(S["gate_norm"], 1)
                    dve.wait_ge(S["gate_norm"], 3 * j + 3)

            def split(j, E):
                base = 0 if E == E0 else NG
                n = base + j + 1
                gates = gm if E == E0 else gr
                dve.wait_ge(S["gt_done"], base + j)
                hi, mid, lo = (parts[:, :, i * E:(i + 1) * E] for i in range(3))
                dve.tensor_copy(hi, gates[:, :, 0:E]).then_inc(S["part_hi"], 1)
                dve.wait_ge(S["part_hi"], n)
                dve.tensor_tensor(r1[:, :, 0:E], gates[:, :, 0:E], hi, ALU.subtract).then_inc(S["part_r1"], 1)
                dve.wait_ge(S["part_r1"], n)
                dve.tensor_copy(mid, r1[:, :, 0:E]).then_inc(S["part_mid"], 1)
                dve.wait_ge(S["part_mid"], n)
                dve.tensor_tensor(lo, r1[:, :, 0:E], mid, ALU.subtract).then_inc(S["parts_ready"], 1)

            def copy_gates(j, E, b):
                n = (0 if E == E0 else NG) + j + 1
                dve.wait_ge(S["gt_done"], n)
                dve.tensor_copy(group(gt[0:3 * E, :], j),
                                bank[b][0:3 * E, :].bitcast(BF16)[:, 0:G]).then_inc(S["gt_copied"], 1)

            for g in range(1, NG + 1):
                dve.wait_ge(S["ln_rstd"], g)
                dve.tensor_tensor(group(nrm, g), bank[g - 1][:, :], lnr[:, g - 1, :], ALU.mult).then_inc(S["ln_normed"], 1)

            PROJ, SC, AV, YT, OUT = (0, 1), 4, 5, 6, 7

            def values(g, k):
                dve.wait_ge(S["av_done"], 16 * g - (8 if k < NT else 0))
                dve.wait_ge(S["v_done"], 8 * g + k + 1)
                t, half, hv = k % NT, k // NT, H // 2
                dve.tensor_copy(v_aug[:, t, half * hv:(half + 1) * hv, 0:HD],
                                bank[PROJ[k % 2]][:, :].rearrange("p (h e) -> p h e", h=hv)).then_inc(S["v_evac"], 1)

            def attend_group(g, first, final):
                def copies(p, s):
                    dve.wait_ge(S["proj_done"], 16 * g + 2 * p + s + 1)
                    dve.wait_ge(S["feat_done"], 32 * g + (4 * (p - 1) + 2 * s + 2 if p else 0))
                    y = stack[64:128, s, 1, :]
                    dve.tensor_copy(y, bank[PROJ[s]][64:128, :]).then_inc(S["odd_copied"], 1)
                    dve.wait_ge(S["odd_copied"], 16 * g + 2 * p + s + 1)
                    dve.tensor_tensor(stack[0:64, s, 1, :], y, y, ALU.mult).then_inc(S["stack_odd"], 1)

                def mask(p, i):
                    dve.wait_ge(S["score_done"], 32 * g + 4 * p + i + 1)
                    dve.wait_ge(S["av_done"], 16 * g + (2 * (p - 1) + i // 2 + 1 if p else 0))
                    dve.tensor_tensor(scores[:, i, :], bank[SC][:, 0:3 * P], causal, ALU.mult).then_inc(S["masked"], 1)

                def normalise(p, b):
                    n = 2 * p + b
                    av = bank[AV][:, 0:4 * (HD + 1)].rearrange("p (h j e) -> p h j e", h=2, j=2)
                    dve.wait_ge(S["av_done"], 16 * g + n + 1)
                    dve.tensor_scalar(den[:, b, :], av[:, :, :, HD], DEN_EPS, None, ALU.add).then_inc(S["den_ready"], 1)
                    dve.wait_ge(S["den_ready"], 32 * g + 2 * n + 1)
                    dve.reciprocal(rden[:, b, :], den[:, b, :]).then_inc(S["den_ready"], 1)
                    dve.wait_ge(S["den_ready"], 32 * g + 2 * n + 2)
                    dve.wait_ge(S["yt_done"], 8 * g + p)
                    for h in range(2):
                        ins_ = dve.tensor_tensor(ynorm[:, 2 * b:2 * b + 2, h, :], av[:, h, :, 0:HD],
                                                 rden[:, b, 2 * h:2 * h + 2].unsqueeze(2).to_broadcast([P, 2, HD]),
                                                 ALU.mult)
                    ins_.then_inc(S["ynormed"], 1)

                def copy_yt(p):
                    dve.wait_ge(S["yt_done"], 8 * g + p + 1)
                    dve.wait_ge(S["wo_done"], 8 * g + p)
                    dve.tensor_copy(yt[:, :], bank[YT][:, :]).then_inc(S["yt_copied"], 1)

                j = g - 1
                for p in range(NP + 2):
                    a, c, d = p < NP, 1 <= p <= NP, p >= 2
                    side, ahead = not first, not final
                    if c:
                        mask(p - 1, 0)
                    if p == NP and ahead:
                        values(g + 1, 0)
                    if p == NP + 1 and ahead:
                        values(g + 1, 4)
                    if d:
                        copy_yt(p - 2)
                    if a:
                        copies(p, 0)
                    if side and p == 2:
                        copy_gates(j, E0, OUT)
                    if c:
                        mask(p - 1, 1)
                    if p == NP and ahead:
                        values(g + 1, 1)
                    if p == NP + 1 and ahead:
                        values(g + 1, 5)
                        values(g + 1, 6)
                        values(g + 1, 7)
                    if a:
                        copies(p, 1)
                    if side and p == 0:
                        norm_group(norm_moe0(j), SIDE0, group(nrm, j))
                    if c:
                        mask(p - 1, 2)
                    if side and p == 1:
                        copy_logits(j, E0, K0, OUT)
                    if p == NP and ahead:
                        values(g + 1, 2)
                    if c:
                        normalise(p - 1, 0)
                    if side and p == 1:
                        choose(j, E0, K0)
                    if c:
                        mask(p - 1, 3)
                    if p == NP and ahead:
                        values(g + 1, 3)
                    if c:
                        normalise(p - 1, 1)
                    if side and p == 1:
                        weigh(j, E0)
                        split(j, E0)
                dve.wait_ge(S["wo_done"], 8 * g + 8)
                xg = group(x, g)
                dve.tensor_tensor(xg, bank[OUT][:, :], xg, ALU.add).then_inc(S["x1_added"], 1)

            for k in range(2 * NT):
                values(1, k)
            attend_group(1, True, False)
            with dve.Fori(1, NG - 1) as j:
                attend_group(j + 1, False, False)
            attend_group(NG, False, True)

            SIDE = 7

            def experts0(g, first):
                for c in range(C0):
                    dve.wait_ge(S["relu_done"], 16 * g + c + 1)
                    dve.wait_ge(S["gbc_done"], 16 * g + c + 1)
                    dve.wait_ge(S["down_done"], 16 * g + max(c - 2, 0))
                    dve.tensor_tensor(hh[:, c % 3, :], bank[4 + c % 2][:, :], hr[:, c % 2, :],
                                      ALU.mult).then_inc(S["h_done"], 1)
                    if first:
                        if c == 4:
                            norm_group(norm_moe0(NG), SIDE0, group(nrm, NG))
                        if c == 6:
                            copy_logits(NG, E0, K0, SIDE)
                        if c == 8:
                            choose(NG, E0, K0)
                        if c == 9:
                            weigh(NG, E0)
                        if c == 10:
                            split(NG, E0)
                        if c == 12:
                            copy_gates(NG, E0, SIDE)
                    else:
                        if c == 4:
                            norm_group(norm_pre(g - 1), SIDE0, SIDE0[2])
                        if c == 9:
                            norm_group(norm_ln0(g - 1), SIDE0, twice)
                dve.wait_ge(S["down_done"], 16 * g + C0)
                xg = group(x, g)
                dve.tensor_tensor(xg, bank[6][:, :], xg, ALU.add).then_inc(S["x2_added"], 1)

            experts0(1, True)
            with dve.Fori(1, NG) as j:
                experts0(j + 1, False)

            dve.wait_ge(S["decay_exp"], L)
            dve.wait_ge(S["ones_ready"], 2)
            dve.tensor_scalar(negdec[:, :], expdec[:, :], -1.0, None, ALU.mult).then_inc(S["decay_neg"], 1)
            dve.wait_ge(S["decay_neg"], 1)

            def norm1(n):
                dve.wait_ge(S["rstd1"], n + 1)
                if n >= 1:
                    dve.wait_ge(S["affined1"], n)
                dve.tensor_tensor(hn1, bank[0][:, :], rs1, ALU.mult).then_inc(S["normed1"], 1)

            def mix1(n):
                l = n // NG
                dve.wait_ge(S["diff1"], n + 1)
                for i, dst in enumerate((xk, xv, xr)):
                    if n >= 1:
                        dve.wait_ge(S["kvr_done"], 3 * (n - 1) + i + 1)
                    dve.scalar_tensor_tensor(out=seqs(dst), in0=seqs(dif1), scalar=vec[:, l, MK + i:MK + i + 1],
                                             in1=h1[:, :, 0:T], op0=ALU.mult, op1=ALU.add).then_inc(S["mixed1"], 1)

            def bound_r(n):
                dve.wait_ge(S["kvr_done"], 3 * n + 3)
                dve.tensor_scalar(er[n % 2], bank[5][:, :], SIG_MIN, None, ALU.max).then_inc(S["r_bounded"], 1)

            def maxima(n):
                l = n // NG
                if n % NG == 0:
                    dve.tensor_scalar(dec, reset[:, :], negdec[:, l:l + 1], None, ALU.add).then_inc(S["decay_bc"], 1)
                    dve.wait_ge(S["decay_bc"], l + 1)
                dve.wait_ge(S["k_copied"], n + 1)
                if n >= 1:
                    dve.wait_ge(S["a2_done"], n)
                dve.tensor_tensor_scan(pm, dec, kp[n % 2], FAR, ALU.add, ALU.max).then_inc(S["p_scanned"], 1)
                if n >= 1:
                    dve.wait_ge(S["e3_done"], n)
                dve.wait_ge(S["p_scanned"], n + 1)
                dve.scalar_tensor_tensor(out=seqs(a1), in0=prev(pm), scalar=negdec[:, l:l + 1], in1=cur(pm),
                                         op0=ALU.add, op1=ALU.subtract).then_inc(S["a1_done"], 1)
                if n >= 1:
                    dve.wait_ge(S["e1_done"], n)
                dve.scalar_tensor_tensor(out=seqs(d1), in0=cur(kp[n % 2]), scalar=vec[:, l, FIRST:FIRST + 1],
                                         in1=prev(pm), op0=ALU.add, op1=ALU.subtract).then_inc(S["d1_done"], 1)
                dve.wait_ge(S["d1_done"], n + 1)
                if n >= 1:
                    dve.wait_ge(S["e2_done"], n)
                dve.tensor_scalar(d2, d1, 0.0, None, ALU.min).then_inc(S["d_below"], 1)
                dve.wait_ge(S["d_below"], n + 1)
                dve.tensor_scalar(d1, d1, 0.0, None, ALU.max).then_inc(S["d_above"], 1)

            def states(n):
                dve.wait_ge(S["e4_done"], n + 1)
                dve.wait_ge(S["v_copied"], n + 1)
                dve.tensor_tensor(cur(kvb[:, :]), cur(e4b[:, :]), seqs(vs[n % 2]), ALU.mult).then_inc(S["kv_done"], 1)
                dve.wait_ge(S["e3_done"], n + 1)
                dve.tensor_tensor_scan(bb[:, :], e3b[:, :], e4b[:, :], 0.0, ALU.mult, ALU.add).then_inc(S["bb_scanned"], 1)
                dve.wait_ge(S["kv_done"], n + 1)
                dve.tensor_tensor_scan(aa[:, :], e3b[:, :], kvb[:, :], 0.0, ALU.mult, ALU.add).then_inc(S["aa_scanned"], 1)

            def quotient(n):
                dve.wait_ge(S["e1_done"], n + 1)
                dve.wait_ge(S["bb_scanned"], n + 1)
                dve.tensor_tensor(seqs(t3), seqs(e1), prev(bb[:, :]), ALU.mult).then_inc(S["t3_done"], 1)
                dve.wait_ge(S["aa_scanned"], n + 1)
                if n >= 1:
                    dve.wait_ge(S["num_done"], n)
                dve.tensor_tensor(seqs(t1), seqs(e1), prev(aa[:, :]), ALU.mult).then_inc(S["t1_done"], 1)
                dve.wait_ge(S["e2_done"], n + 1)
                dve.wait_ge(S["t3_done"], n + 1)
                dve.tensor_tensor(dn, e2, t3, ALU.add).then_inc(S["den_done"], 1)
                dve.wait_ge(S["den_done"], n + 1)
                dve.wait_ge(S["r_exp"], n + 1)
                if n >= 1:
                    dve.wait_ge(S["den_logged"], n)
                dve.scalar_tensor_tensor(out=dn2, in0=er[n % 2], scalar=1.0, in1=dn,
                                         op0=ALU.add, op1=ALU.mult).then_inc(S["den2_done"], 1)

            def receive(n):
                dve.wait_ge(S["rec_done"], n + 1)
                dve.wait_ge(S["num_done"], n + 1)
                if n >= 1:
                    dve.wait_ge(S["o_done"], n)
                dve.tensor_tensor(rw, num, rec, ALU.mult).then_inc(S["rw_done"], 1)

            def add_output(n):
                g = n % NG
                dve.wait_ge(S["o_done"], n + 1)
                dve.wait_ge(S["centered1"], n + 1)
                r = rs[:, g * G:(g + 1) * G]
                dve.tensor_tensor(r, bank[3][:, :], r, ALU.add).then_inc(S["x_mid"], 1)

            def norm2(n):
                dve.wait_ge(S["rstd2"], n + 1)
                if n >= 1:
                    dve.wait_ge(S["affined2"], n)
                dve.tensor_tensor(hn2, bank[1][:, :], rs2, ALU.mult).then_inc(S["normed2"], 1)

            def mix2(n):
                l = n // NG
                dve.wait_ge(S["diff2"], n + 1)
                for i, dst in ((1, xcr), (0, xck)):
                    if n >= 1:
                        dve.wait_ge(S["ck_done"], 4 * n)
                    dve.scalar_tensor_tensor(out=seqs(dst), in0=seqs(dif2), scalar=vec[:, l, CMK + i:CMK + i + 1],
                                             in1=h2[:, :, 0:T], op0=ALU.mult, op1=ALU.add).then_inc(S["mixed2"], 1)

            def bound_cr(n):
                dve.wait_ge(S["cr_done"], n + 1)
                if n >= 1:
                    dve.wait_ge(S["cr_sig"], n)
                dve.tensor_scalar(ecr, bank[4][:, :], SIG_MIN, None, ALU.max).then_inc(S["cr_bounded"], 1)

            def square(n, j):
                dve.wait_ge(S["ck_relu"], 4 * n + j + 1)
                dve.tensor_tensor(ckr[:, j, :], ckr[:, j, :], ckr[:, j, :], ALU.mult).then_inc(S["even_squared"], 1)

            def add_ffn(n):
                g = n % NG
                dve.wait_ge(S["cr_sig"], n + 1)
                dve.wait_ge(S["cv_done"], n + 1)
                if n >= 1:
                    dve.wait_ge(S["x_out"], n)
                dve.tensor_tensor(kvg, bank[5][:, :], scr, ALU.mult).then_inc(S["kv_gated"], 1)
                dve.wait_ge(S["kv_gated"], n + 1)
                dve.wait_ge(S["centered2"], n + 1)
                r = rs[:, g * G:(g + 1) * G]
                dve.tensor_tensor(r, kvg, r, ALU.add).then_inc(S["x_out"], 1)

            for s in range(STEPS):
                a, w, m, f = s < ITEMS, 1 <= s <= ITEMS, 2 <= s < ITEMS + 2, s >= 3
                if s == ITEMS:
                    dve.wait_ge(S["gw_ss"], 1)
                    dve.tensor_scalar(gn[:, 2, 0:E1], bank[0][:, 0:E1], NORM_EPS2, None,
                                      ALU.max).then_inc(S["gw_guard"], 1)
                if w:
                    maxima(s - 1)
                if f:
                    bound_cr(s - 3)
                if s == ITEMS + 2:
                    guard_norms(1, 0)
                if w:
                    states(s - 1)
                if a:
                    norm1(s)
                if m:
                    add_output(s - 2)
                if f:
                    square(s - 3, 0)
                if w:
                    quotient(s - 1)
                if f:
                    square(s - 3, 2)
                if s == ITEMS + 2:
                    dve.wait_ge(S["gw_inv"], 1)
                    copy_logits(1, E1, K1, 0)
                if a:
                    mix1(s)
                if w:
                    receive(s - 1)
                if s == 0:
                    norm_group(norm_pre(NG), SIDE0, SIDE0[2])
                if s == 1:
                    norm_group(norm_ln0(NG), SIDE0, twice)
                if s >= ITEMS:
                    norm_group(norm_moe1(s - ITEMS + 1), SIDE1, group(nrm, s - ITEMS + 1))
                if m:
                    norm2(s - 2)
                if f:
                    add_ffn(s - 3)
                if m:
                    mix2(s - 2)
                if a:
                    bound_r(s)
                if s == ITEMS - 1:
                    dve.wait_ge(S["rgate_in"], 16)
                    dve.tensor_tensor(msk[:, 0, 0:E1], rgate[:, :], rgate[:, :], ALU.mult).then_inc(S["gw_sq"], 1)
                if s >= ITEMS - 1:
                    g = s - ITEMS + 2
                    dve.wait_ge(S["x_out"], ITEMS - NG + g)
                    xg = group(x, g)
                    dve.tensor_tensor(xg, xg, group(rs, g), ALU.add).then_inc(S["x3_added"], 1)

            choose(1, E1, K1)
            weigh(1, E1)
            split(1, E1)
            norm_group(norm_moe1(NG), SIDE1, group(nrm, NG))
            copy_gates(1, E1, 0)
            SIDE = 7

            def experts1(g, final):
                for c in range(C1):
                    m = P
                    n = C1 * g + c
                    dve.wait_ge(S["silu_done"], n + 1)
                    dve.wait_ge(S["u_done"], n + 1)
                    if c < C1 - 1:
                        dve.wait_ge(S["h1_done"], C1 * g + c)
                        dve.tensor_tensor(yt[:, :], bank[2 + c % 2][:, :], hr[:, c % 2, :], ALU.mult).then_inc(S["su_done"], 1)
                        dve.wait_ge(S["su_done"], n + 1)
                        dve.wait_ge(S["cbc_done"], (C1 - 1) * g + c + 1)
                        dve.wait_ge(S["down1_done"], C1 * g + max(c - 2, 0))
                        dve.tensor_tensor(hh[:, c % 3, :], bank[4 + c % 2][:, :], yt[:, :], ALU.mult).then_inc(S["h1_done"], 1)
                    else:
                        dve.wait_ge(S["down1_done"], C1 * g + c - 2)
                        dve.tensor_tensor(hh[0:m, c % 3, :], bank[2 + c % 2][0:m, :], hr[0:m, c % 2, :],
                                          ALU.mult).then_inc(S["su_done"], 1)
                        dve.wait_ge(S["su_done"], n + 1)
                        dve.sem_inc(S["h1_done"], 1)
                    if not final:
                        if c == 3:
                            guard_norms(g + 1, SIDE)
                        if c == 4:
                            copy_logits(g + 1, E1, K1, SIDE)
                        if c == 5:
                            choose(g + 1, E1, K1)
                        if c == 6:
                            weigh(g + 1, E1, by_tanh=True)
                            split(g + 1, E1)
                        if c == C1 - 1:
                            copy_gates(g + 1, E1, SIDE)
                dve.wait_ge(S["down1_done"], C1 * g + C1)
                xg = group(x, g)
                dve.tensor_tensor(xg, bank[6][:, :], xg, ALU.add).then_inc(S["y_added"], 1)

            with dve.Fori(1, NG) as g:
                experts1(g, False)
            experts1(NG, True)


def arrays_for(inputs):
    import numpy as np
    f = lambda a: np.ascontiguousarray(a)
    i = {k: np.asarray(v) for k, v in inputs.items()}
    c = lambda k: i["L1_attn_" + k]
    eye = np.eye(P, dtype=np.float32)
    tri = np.triu(np.ones((P, P), np.float32))
    one = np.ones((P, P), np.float32)
    consts = np.concatenate([eye - one / P, one / P, eye, one, tri, one, tri], axis=1)

    def selector(E, chunks):
        s = np.zeros((3 * E, chunks * P), np.float32)
        for part in range(3):
            for e in range(E):
                s[part * E + e, e * 64:(e + 1) * 64] = 1.0
        return s

    wf = i["L0_attn_W_feat"]
    half = np.full((HD, NF), -0.5, np.float32)
    wfeat = np.stack([np.concatenate([wf, half]), np.concatenate([half, wf])], axis=1)
    lay = []
    for l in range(L):
        ws = [c("Wk")[l].T, c("Wv")[l].T, c("Wr")[l].T, c("Wo")[l].T]
        ws += [c("Wck")[l][j * P:(j + 1) * P].T for j in range(FC)]
        ws += [c("Wcr")[l].T]
        ws += [c("Wcv")[l][:, j * P:(j + 1) * P].T for j in range(FC)]
        lay.append(np.stack(ws, axis=1))
    wrwkv = np.stack(lay, axis=1)
    vec = np.zeros((P, L + 1, NVEC), np.float32)
    for l in range(L):
        for j, k in enumerate(("ln1_w", "ln1_b", "tmk", "tmv", "tmr", "time_decay", "time_first",
                               "ln2_w", "ln2_b", "cmk", "cmr")):
            vec[:, l, j] = c(k)[l]
    vec[:, L, 0] = LN_EPS
    vec[:, L, 1] = c("ln0_w")
    vec[:, L, 2] = c("ln0_b")
    m = lambda k: i["L1_ffn_" + k]
    ed = lambda a: a.transpose(1, 0, 2).reshape(P, E1 * 64)
    pad = np.zeros((P, 64), np.float32)
    wgu = np.stack([np.concatenate([ed(m("w_gate")), m("sw_gate"), pad], axis=1),
                    np.concatenate([ed(m("w_up")), m("sw_up"), pad], axis=1)], axis=1)
    wdn = np.zeros((P, C1, P), np.float32)
    wdn[:, :C1 - 1] = m("w_down").reshape(C1 - 1, P, P).transpose(1, 0, 2)
    wdn[:64, C1 - 1] = m("sw_down")
    return {k: f(v) for k, v in {
        "x": i["L0_attn_x"].transpose(2, 0, 1).reshape(P, N),
        "consts": consts,
        "wq": i["L0_attn_Wq"], "wk": i["L0_attn_Wk"], "wv": i["L0_attn_Wv"],
        "wfeat": wfeat,
        "wo": i["L0_attn_Wo"].reshape(NP, P, P).transpose(1, 0, 2),
        "vec": vec,
        "esel": i["L0_ffn_expert_sel"].T,
        "sel0": selector(E0, C0),
        "keys": i["L0_ffn_keys"].transpose(1, 0, 2).reshape(P, E0 * 64),
        "vals": i["L0_ffn_values"].reshape(C0, P, P).transpose(1, 0, 2),
        "wrwkv": wrwkv,
        "rgate": m("gate_w").T,
        "wgu": wgu, "wdn": wdn,
        "sel1": selector(E1, C1 - 1),
    }.items()}


def kernel(**inputs):
    import numpy as _np
    import concourse.bacc as _bacc
    from concourse import mybir as _mybir
    from concourse.bass_utils import run_bass_kernel_spmd as _run

    nc = _bacc.Bacc("TRN2", target_bir_lowering=False, num_devices=1)
    laid = arrays_for(inputs)
    arrays, args = {}, {}
    for name, a in laid.items():
        arrays[f"in_{name}_dram"] = a
        args[name] = nc.dram_tensor(f"in_{name}_dram", a.shape, _mybir.dt.from_np(a.dtype), kind="ExternalInput").ap()
    out = nc.dram_tensor("out_dram", (P, N), F32, kind="ExternalOutput").ap()
    two_blocks(nc, args, out)
    r = _run(nc, [arrays], core_ids=[0])
    got = r.results[0]["out_dram"]
    return _np.ascontiguousarray(_np.asarray(got).reshape(P, B, T).transpose(1, 2, 0))
```

```python
from contextlib import ExitStack

import concourse.bass as bass
from concourse import mybir

F32 = mybir.dt.float32
BF16 = mybir.dt.bfloat16
ALU = mybir.AluOpType
ACT = mybir.ActivationFunctionType
AX = mybir.AxisListType

P = 128
B, T = 8, 256
N = B * T
G = 512
NG = N // G
NT = G // P
SEQ = G // T
H, HD, NF = 16, 64, 128
NP = H // 2
E0, K0 = 32, 4
C0 = E0 // 2
E1, K1 = 16, 8
C1 = E1 // 2 + 1
L = 4
FC = 4
T1 = T + 1
NVEC = 11
LNW, LNB, MK, MV, MR, DECAY, FIRST, LN2W, LN2B, CMK, CMR = range(11)
LN_EPS = 1e-5
DEN_EPS = 1e-6 * NF
NORM_EPS2 = 1e-24
SIG_MIN = -38.0
FAR = -1e38
TAKEN = 3e38
UNUSED = -3e38

PER_GROUP = [
    (2 * NT, ["v_done", "v_evac"]),
    (NP, ["yt_done", "yt_copied", "wo_done"]),
    (16, ["proj_done", "stack_odd", "stack_even", "odd_copied", "av_done", "ynormed",
         "up_done", "gbc_done", "relu_done", "h_done", "down_done"]),
    (32, ["feat_done", "feat_exp", "score_done", "masked", "den_ready"]),
    (C1, ["g_done", "u_done", "silu_done", "su_done", "h1_done", "down1_done"]),
    (C1 - 1, ["cbc_done"]),
    (3, ["gate_norm"]),
    (2, ["logit_scaled"]),
    (1, ["ng_ready", "x1_added", "x2_added", "y_added", "rng_ready", "logit_done", "logit_copied", "logit_bounded",
        "top_found", "top_packed", "top_replaced", "gate_exp", "gate_sum", "gate_recip", "gate_mask",
        "gate_masked", "part_hi", "part_r1", "part_mid", "parts_ready", "gt_done", "gt_copied", "sq_ready",
        "ss_guard", "ss_inv"]),
]
SEMS = [
    "masks_in", "x_in_1", "x_in_2", "x_in_3", "x_in_4", "wqkv_in", "wfeat_in", "wo_in", "const_in", "sel0_in",
    "keys_in", "vals_in", "wrwkv_in", "vec_in", "rgate_in", "wgu_in", "wdn_in", "esel_in", "sel1_in",
    "ln_centered", "ln_squared", "ln_var", "ln_logged", "ln_rstd", "ln_normed", "const_ready", "sel_ready",
    "ones_ready", "ng_ready", "v_done", "v_evac", "proj_done", "stack_odd", "stack_even", "odd_copied",
    "feat_done", "feat_exp", "score_done", "masked", "av_done", "den_ready", "ynormed", "yt_done", "yt_copied",
    "wo_done", "x1_added", "rng_ready", "logit_done", "logit_copied", "logit_bounded", "top_found",
    "top_packed", "top_replaced", "gate_exp", "gate_sum", "gate_recip", "gate_mask", "gate_masked", "gate_norm",
    "part_hi", "part_r1", "part_mid", "parts_ready", "gt_done", "gt_copied", "up_done", "gbc_done", "relu_done",
    "h_done", "down_done", "x2_added", "ln0_affined", "decay_exp", "decay_neg", "decay_bc", "centered1",
    "squared1", "var1", "logged1", "rstd1", "normed1", "affined1", "diff1", "mixed1", "kvr_done", "k_copied",
    "v_copied", "r_bounded", "r_exp", "p_scanned", "a1_done", "a2_done", "d1_done", "d_below", "d_above",
    "e3_done", "e4_done", "e1_done", "e2_done", "kv_done", "aa_scanned", "bb_scanned", "t1_done", "t2_done",
    "num_done", "t3_done", "den_done", "den2_done", "den_logged", "rec_done", "rw_done", "o_done", "x_mid",
    "centered2", "squared2", "var2", "logged2", "rstd2", "normed2", "affined2", "diff2", "mixed2", "ck_done",
    "ck_relu", "ck_squared", "cr_done", "cr_bounded", "cr_exp", "cr_logged", "cr_sig", "cv_done", "kv_gated",
    "x_out", "gw_sq", "gw_ss", "gw_guard", "gw_inv", "sq_ready", "ss_guard", "ss_inv", "logit_scaled",
    "x3_added", "g_done", "u_done", "cbc_done", "silu_done", "su_done", "h1_done", "down1_done", "y_added",
    "out_stored",
]


def two_blocks(nc, ins, out):
    with ExitStack() as ctx:
        def sb(name, shape, dt=F32):
            return ctx.enter_context(nc.sbuf_tensor(name, shape, dt))

        S = {name: ctx.enter_context(nc.semaphore(name)) for name in SEMS}
        bank = [ctx.enter_context(nc.psum_tensor(f"bank{i}", [P, G], F32)) for i in range(8)]

        x = sb("x", [P, N])
        nrm = sb("nrm", [P, N])
        ng = sb("ng", [P, G])
        wq, wk, wv = (sb(n, [P, H * HD]) for n in ("wq", "wk", "wv"))
        wfeat = sb("wfeat", [P, 2, NF])
        wo = sb("wo", [P, NP, P])
        consts = sb("consts", [P, 4 * P + 3 * P])
        center, mean, ident, ones = (consts[:, i * P:(i + 1) * P] for i in range(4))
        causal = consts[:, 4 * P:7 * P]
        esel = sb("esel", [P, E0])
        wmoe0 = sb("wmoe0", [P, E0 * 64 + C0 * P])
        keys = wmoe0[:, 0:E0 * 64]
        vals = wmoe0[:, E0 * 64:].rearrange("p (c d) -> p c d", c=C0)
        wrwkv = sb("wrwkv", [P, L, 13, P])
        vec = sb("vec", [P, L + 1, NVEC])
        rgate = sb("rgate", [P, E1])
        wgu = sb("wgu", [P, 2, C1 * P])
        wdn = sb("wdn", [P, C1, P])
        sel = sb("sel", [3 * E0, C0 * P], BF16)
        self32 = sb("self32", [3 * E0, C0 * P])
        lnsq = sb("lnsq", [P, NG, G])
        lnr = sb("lnr", [P, NG, G])
        gt = sb("gt", [3 * E0, N], BF16)

        stack = sb("stack", [P, 2, 2, G])
        feat = sb("feat", [P, 2, 2, 2, G])
        v_aug = sb("v_aug", [P, NT, H, HD + 1])
        scores = sb("scores", [P, 4, 3 * P])
        den = sb("den", [P, 2, 4])
        rden = sb("rden", [P, 2, 4])
        ynorm = sb("ynorm", [P, NT, 2, HD])
        yt = sb("yt", [P, G])

        lg = sb("lg", [P, NT, E0 + 4])
        ex = sb("ex", [P, NT, E0])
        gs = sb("gs", [P, NT, E0])
        gr = sb("gr", [P, NT, E0])
        top = sb("top", [P, NT, 8])
        top2 = sb("top2", [P, NT, 8])
        repl = sb("repl", [P, NT, E0 + 4])
        msk = sb("msk", [P, NT, E0])
        gm = sb("gm", [P, NT, E0])
        gn = sb("gn", [P, NT, E0])
        gsum = sb("gsum", [P, NT])
        gsr = sb("gsr", [P, NT])
        r1 = sb("r1", [P, NT, E0])
        parts = sb("parts", [P, NT, 3 * E0], BF16)
        identb = sb("identb", [P, P], BF16)
        hr = sb("hr", [P, 2, G])
        hh = sb("hh", [P, 3, G])

        minus_half = sb("minus_half", [P, E1])
        expdec = sb("expdec", [P, L])
        negdec = sb("negdec", [P, L])

        def fixed(eng):
            eng.wait_ge(S["const_in"], 16)

        eps, ln0_w, ln0_b = (vec[:, L, i:i + 1] for i in range(3))

        def group(buf, g):
            return buf[:, (g - 1) * G:g * G] if isinstance(g, int) else buf[:, bass.ds((g - 1) * G, G)]

        block = ctx.enter_context(nc.Block())

        @block.sync
        def _(sp):
            sp.dma_start(consts[:, 0:2 * P], ins["consts"][:, 0:2 * P]).then_inc(S["const_in"], 16)
            for g in range(1, NG + 1):
                sp.dma_start(group(x, g), ins["x"][:, (g - 1) * G:g * G]).then_inc(S[f"x_in_{g}"], 16)
                if g == 1:
                    sp.dma_start(vec[:, :, :], ins["vec"]).then_inc(S["vec_in"], 16)
            sp.dma_start(wv[:, :], ins["wv"]).then_inc(S["wqkv_in"], 16)
            sp.dma_start(wq[:, :], ins["wq"]).then_inc(S["wqkv_in"], 16)
            sp.dma_start(wk[:, :], ins["wk"]).then_inc(S["wqkv_in"], 16)
            sp.dma_start(consts[:, 2 * P:7 * P], ins["consts"][:, 2 * P:7 * P]).then_inc(S["masks_in"], 16)
            sp.dma_start(wfeat[:, :, :], ins["wfeat"]).then_inc(S["wfeat_in"], 16)
            sp.dma_start(wo[:, :, :], ins["wo"]).then_inc(S["wo_in"], 16)
            sp.dma_start(esel[:, :], ins["esel"]).then_inc(S["esel_in"], 16)
            sp.dma_start(self32[:, :], ins["sel0"]).then_inc(S["sel0_in"], 16)
            sp.dma_start(keys, ins["keys"]).then_inc(S["keys_in"], 16)
            sp.dma_start(vals, ins["vals"]).then_inc(S["vals_in"], 16)
            sp.dma_start(wrwkv[:, :, :, :], ins["wrwkv"]).then_inc(S["wrwkv_in"], 16)
            sp.dma_start(rgate[:, :], ins["rgate"]).then_inc(S["rgate_in"], 16)
            sp.dma_start(wgu[:, :, :], ins["wgu"]).then_inc(S["wgu_in"], 16)
            sp.dma_start(wdn[:, :, :], ins["wdn"]).then_inc(S["wdn_in"], 16)
            sp.wait_ge(S["sel_ready"], 1)
            sp.dma_start(self32[0:3 * E1, 0:(C1 - 1) * P], ins["sel1"]).then_inc(S["sel1_in"], 16)
            with sp.Fori(1, NG + 1) as g:
                sp.wait_ge(S["y_added"], g + 1)
                sp.dma_start(out[:, bass.ds((g - 1) * G, G)], x[:, bass.ds((g - 1) * G, G)]).then_inc(S["out_stored"], 16)
            sp.wait_ge(S["out_stored"], 16 * NG)

        rs = sb("rs", [P, N])
        halves = stack[:, :, :, :].rearrange("p a b c -> p a (b c)")
        h1, h2 = (halves[:, i, 0:SEQ * T1].rearrange("p (s t) -> p s t", s=SEQ) for i in range(2))
        fb = feat[:, :, :, :, :].rearrange("p a b c d -> p (a b c) d")
        va = v_aug[:, :, :, :].rearrange("p a b c -> p (a b c)")
        hn1, dif1 = fb[:, 0, :], fb[:, 1, :]
        xk, xv, xr = fb[:, 2, :], fb[:, 3, :], fb[:, 4, :]
        hn2, dif2 = fb[:, 5, :], fb[:, 6, :]
        xck = fb[:, 7, :]
        xcr = yt[:, :]
        W2 = SEQ * T1
        kp = [va[:, i * W2:(i + 1) * W2] for i in range(2)]
        vs = [va[:, 2 * W2 + i * G:2 * W2 + (i + 1) * G] for i in range(2)]
        er = [va[:, 2 * W2 + (2 + i) * G:2 * W2 + (3 + i) * G] for i in range(2)]
        pm = va[:, 2 * W2 + 4 * G:3 * W2 + 4 * G]
        dec = va[:, 3 * W2 + 4 * G:4 * W2 + 4 * G]
        e3b, e4b, kvb, aa, bb, reset = (wmoe0[:, i * W2:(i + 1) * W2] for i in range(6))
        d2 = wmoe0[:, 6 * W2:6 * W2 + G]
        a1, a2 = wq[:, 0:G], wq[:, G:2 * G]
        d1, e1 = wk[:, 0:G], wk[:, G:2 * G]
        e2, t1 = wv[:, 0:G], wv[:, G:2 * G]
        wof = wo[:, :, :].rearrange("p a b -> p (a b)")
        t2, t3 = wof[:, 0:G], wof[:, G:2 * G]
        scf = scores[:, :, :].rearrange("p a b -> p (a b)")
        dn, dn2, rec = scf[:, 0:G], scf[:, G:2 * G], scf[:, 2 * G:3 * G]
        num = hr[:, 0, :]
        rw = hr[:, 1, :]
        ckr = lnsq
        sq1, rs1 = hh[:, 0, :], hh[:, 1, :]
        sq2, rs2 = hh[:, 2, :], ng[:, :]
        ecr = lnr[:, 0, :]
        scr = lnr[:, 1, :]
        kvg = lnr[:, 3, :]

        def seqs(ap):
            return ap.rearrange("p (s t) -> p s t", s=SEQ)

        def cur(buf):
            return buf.rearrange("p (s t) -> p s t", s=SEQ)[:, :, 1:T1]

        def prev(buf):
            return buf.rearrange("p (s t) -> p s t", s=SEQ)[:, :, 0:T]

        ITEMS = L * NG
        STEPS = ITEMS + 5
        LAST = ITEMS - NG

        def do(part, n, *which):
            if 0 <= n < ITEMS:
                part(n, *which)

        def finish(part, n):
            if LAST <= n < ITEMS - 1:
                part(n - LAST + 1)

        SIDE0 = (lnsq[:, 0, :], lnsq[:, 1, :], lnsq[:, 2, :], lnr[:, 0, :])
        SIDE1 = (xk, xv, xr, hn1)
        tokens_sq = dif1
        twice = lnsq[:, 3, :]

        def norm_moe0(j):
            return NG + j

        def norm_pre(j):
            return 2 * NG + 2 * j - 1

        def norm_ln0(j):
            return 2 * NG + 2 * j

        def norm_moe1(j):
            return 4 * NG + j

        @block.tensor
        def _(pe):
            def center_group(i, src, b):
                if not isinstance(i, int) or i > NG:
                    pe.wait_ge(S["ln_logged"], i - 1)
                pe.matmul(bank[b][:, :], center, src, start=True, stop=True).then_inc(S["ln_centered"], 1)

            def variance_group(i, sq, b):
                pe.wait_ge(S["ln_squared"], i)
                pe.matmul(bank[b][:, :], mean, sq, start=True, stop=True).then_inc(S["ln_var"], 1)

            def logits(n, E, b):
                static, sq, w = (SIDE0[2], None, esel) if E == E0 else (SIDE1[2], tokens_sq, rgate)
                cols = E0 if E == E0 else E1 + 1
                fixed(pe)
                pe.wait_ge(S["rng_ready"], n + 1)
                if E == E1:
                    pe.wait_ge(S["sq_ready"], n - NG + 1)
                for t in range(NT):
                    mm = pe.matmul(bank[b][:, t * cols:t * cols + E], static[:, t * P:(t + 1) * P], w[:, :],
                                   start=True, stop=True)
                    if E == E1:
                        mm = pe.matmul(bank[b][:, t * cols + E:t * cols + E + 1], sq[:, t * P:(t + 1) * P],
                                       ones[:, 0:1], start=True, stop=True)
                mm.then_inc(S["logit_done"], 1)

            def turn_gates(n, E, b):
                fixed(pe)
                pe.wait_ge(S["parts_ready"], n + 1)
                for t in range(NT):
                    mm = pe.transpose(bank[b][0:3 * E, :].bitcast(BF16)[:, t * P:(t + 1) * P],
                                      parts[:, t, 0:3 * E], identb[:, :])
                mm.then_inc(S["gt_done"], 1)

            pe.wait_ge(S["const_in"], 16)
            for g in range(1, NG + 1):
                pe.wait_ge(S[f"x_in_{g}"], 16)
                center_group(g, group(x, g), g - 1)
                if g >= 2:
                    variance_group(g - 1, lnsq[:, g - 2, :], NG + g - 2)
            variance_group(NG, lnsq[:, NG - 1, :], 2 * NG - 1)

            pe.wait_ge(S["ln_normed"], 2)
            pe.wait_ge(S["masks_in"], 16)
            pe.wait_ge(S["wqkv_in"], 48)
            pe.wait_ge(S["wfeat_in"], 16)
            pe.wait_ge(S["wo_in"], 16)
            pe.wait_ge(S["esel_in"], 16)
            PROJ, FEAT, SC, AV, YT, OUT = (0, 1), (2, 3), 4, 5, 6, 7

            def values(g, k):
                if k == 0:
                    pe.wait_ge(S["ng_ready"], g + 1)
                if k < 2:
                    pe.wait_ge(S["stack_odd"], 16 * g)
                    pe.wait_ge(S["stack_even"], 16 * g)
                else:
                    pe.wait_ge(S["v_evac"], 8 * g + k - 1)
                t, half = k % NT, k // NT
                pe.matmul(bank[PROJ[k % 2]][:, :], ng[:, t * P:(t + 1) * P], wv[:, half * G:(half + 1) * G],
                          start=True, stop=True).then_inc(S["v_done"], 1)

            def attend_group(g, first, final):
                def proj(p, s):
                    if p == 0:
                        pe.wait_ge(S["v_evac"], 8 * g + 7 + s)
                    else:
                        pe.wait_ge(S["stack_odd"], 16 * g + 2 * (p - 1) + s + 1)
                        pe.wait_ge(S["stack_even"], 16 * g + 2 * (p - 1) + s + 1)
                    w = wq if s == 0 else wk
                    pe.matmul(bank[PROJ[s]][:, :], w[:, p * P:(p + 1) * P], ng[:, :], start=True,
                              stop=True).then_inc(S["proj_done"], 1)

                def features(p, s, h):
                    f = 4 * p + 2 * s + h
                    pe.wait_ge(S["stack_odd"], 16 * g + 2 * p + s + 1)
                    pe.wait_ge(S["stack_even"], 16 * g + 2 * p + s + 1)
                    pe.wait_ge(S["feat_exp"], 32 * g + max(f - 1, 0))
                    pe.matmul(bank[FEAT[f % 2]][:, :], wfeat[:, h, :], stack[:, s, h, :], start=True,
                              stop=True).then_inc(S["feat_done"], 1)

                def score(p, i):
                    b, h = i // 2, i % 2
                    fq, fk = feat[:, p % 2, 0, h, :], feat[:, p % 2, 1, h, :]
                    pe.wait_ge(S["feat_exp"], 32 * g + 4 * p + 4)
                    pe.wait_ge(S["masked"], 32 * g + 4 * p + i)
                    pe.matmul(bank[SC][:, 0:T], fk[:, b * T:b * T + P], fq[:, b * T:(b + 1) * T],
                              start=True, stop=True)
                    pe.matmul(bank[SC][:, T:T + P], fk[:, b * T + P:(b + 1) * T],
                              fq[:, b * T + P:(b + 1) * T], start=True, stop=True).then_inc(S["score_done"], 1)

                def attend(p, b):
                    pe.wait_ge(S["masked"], 32 * g + 4 * p + 2 * b + 2)
                    pe.wait_ge(S["ynormed"], 16 * g + 2 * p + b)
                    W = HD + 1
                    for h in range(2):
                        sc = scores[:, 2 * b + h, :]
                        o = bank[AV][:, 2 * h * W:(2 * h + 1) * W]
                        pe.matmul(o, sc[:, 0:P], v_aug[:, 2 * b, 2 * p + h, :], start=True, stop=True)
                        o = bank[AV][:, (2 * h + 1) * W:(2 * h + 2) * W]
                        pe.matmul(o, sc[:, P:2 * P], v_aug[:, 2 * b, 2 * p + h, :], start=True, stop=False)
                        mm = pe.matmul(o, sc[:, 2 * P:3 * P], v_aug[:, 2 * b + 1, 2 * p + h, :],
                                       start=False, stop=True)
                    mm.then_inc(S["av_done"], 1)

                def turn(p):
                    pe.wait_ge(S["ynormed"], 16 * g + 2 * p + 2)
                    pe.wait_ge(S["yt_copied"], 8 * g + p)
                    for t in range(NT):
                        mm = pe.transpose(bank[YT][:, t * P:(t + 1) * P],
                                          ynorm[:, t, :, :].rearrange("p h e -> p (h e)"), ident)
                    mm.then_inc(S["yt_done"], 1)

                def project_out(p):
                    pe.wait_ge(S["yt_copied"], 8 * g + p + 1)
                    if p == 0:
                        pe.wait_ge(S["x1_added"], g)
                        pe.wait_ge(S["gt_copied"], g)
                    pe.matmul(bank[OUT][:, :], wo[:, p, :], yt[:, :], start=(p == 0),
                              stop=(p == NP - 1)).then_inc(S["wo_done"], 1)

                j = g - 1
                for p in range(NP + 2):
                    a, c, d = p < NP, 1 <= p <= NP, p >= 2
                    side = not first
                    if a:
                        proj(p, 0)
                    if side and p == 0:
                        pe.wait_ge(S["x1_added"], j + 1)
                        center_group(norm_moe0(j), group(x, j), OUT)
                    if p == NP and not final:
                        values(g + 1, 0)
                    if p == NP and final:
                        turn(p - 2)
                    if c:
                        score(p - 1, 0)
                    if p == NP + 1 and not final:
                        values(g + 1, 4)
                    if d and not (p == NP and final):
                        turn(p - 2)
                    if a:
                        proj(p, 1)
                    if c:
                        score(p - 1, 1)
                    if p == NP and not final:
                        values(g + 1, 1)
                    if p == NP + 1 and not final:
                        values(g + 1, 5)
                    if side and p == 1:
                        logits(j, E0, OUT)
                    late = side and p == 2
                    if d and not late:
                        project_out(p - 2)
                    if c:
                        score(p - 1, 2)
                    if p == NP and not final:
                        values(g + 1, 2)
                    if a:
                        features(p, 0, 0)
                    if late:
                        turn_gates(j, E0, OUT)
                    if c:
                        attend(p - 1, 0)
                        score(p - 1, 3)
                    if p == NP and not final:
                        values(g + 1, 3)
                    if a:
                        features(p, 0, 1)
                    if side and p == 0:
                        variance_group(norm_moe0(j), SIDE0[0], OUT)
                    if a:
                        features(p, 1, 0)
                    if c:
                        attend(p - 1, 1)
                    if late:
                        project_out(0)
                    if a:
                        features(p, 1, 1)
                    if p == NP + 1 and not final:
                        values(g + 1, 6)
                        values(g + 1, 7)

            for k in range(2 * NT):
                values(1, k)
            pe.wait_ge(S["ln_normed"], NG)
            attend_group(1, True, False)
            with pe.Fori(1, NG - 1) as j:
                attend_group(j + 1, False, False)
            attend_group(NG, False, True)

            pe.wait_ge(S["keys_in"], 16)
            pe.wait_ge(S["vals_in"], 16)
            pe.wait_ge(S["sel_ready"], 1)
            SIDE = 7

            def experts0(g, first):
                pe.wait_ge(S["gt_copied"], g + 1)

                def up(c):
                    pe.wait_ge(S["relu_done"], 16 * g + max(c - 1, 0))
                    pe.matmul(bank[2 + c % 2][:, :], keys[:, c * P:(c + 1) * P], group(nrm, g),
                              start=True, stop=True).then_inc(S["up_done"], 1)
                    pe.wait_ge(S["h_done"], 16 * g + max(c - 1, 0))
                    pe.matmul(bank[4 + c % 2][:, :], sel[:, c * P:(c + 1) * P], group(gt, g),
                              start=True, stop=True).then_inc(S["gbc_done"], 1)

                def down(c):
                    if c == 0:
                        pe.wait_ge(S["x2_added"], g)
                    pe.wait_ge(S["h_done"], 16 * g + c + 1)
                    pe.matmul(bank[6][:, :], vals[:, c, :], hh[:, c % 3, :], start=(c == 0),
                              stop=(c == C0 - 1)).then_inc(S["down_done"], 1)

                for c in range(C0 + 2):
                    if c < C0:
                        up(c)
                    if c >= 2:
                        down(c - 2)
                    if first:
                        if c == 1:
                            pe.wait_ge(S["x1_added"], NG + 1)
                            center_group(norm_moe0(NG), group(x, NG), SIDE)
                        if c == 3:
                            variance_group(norm_moe0(NG), SIDE0[0], SIDE)
                        if c == 6:
                            logits(NG, E0, SIDE)
                        if c == 12:
                            turn_gates(NG, E0, SIDE)
                    else:
                        j = g - 1
                        if c == 1:
                            pe.wait_ge(S["x2_added"], j + 1)
                            pe.wait_ge(S["gt_copied"], NG + 1)
                            center_group(norm_pre(j), group(x, j), SIDE)
                        if c == 3:
                            variance_group(norm_pre(j), SIDE0[0], SIDE)
                        if c == 6:
                            pe.wait_ge(S["ln_normed"], norm_pre(j))
                            center_group(norm_ln0(j), SIDE0[2], SIDE)
                        if c == 8:
                            variance_group(norm_ln0(j), SIDE0[0], SIDE)

            experts0(1, True)
            with pe.Fori(1, NG) as j:
                experts0(j + 1, False)

            pe.wait_ge(S["wrwkv_in"], 16)
            CEN1, CEN2, VAR, OV, KCR, RCV = 0, 1, 2, 3, 4, 5

            def center1(n):
                g = n % NG
                if n < NG:
                    pe.wait_ge(S["ln0_affined"], n + 1)
                else:
                    pe.wait_ge(S["x_out"], n - NG + 1)
                if n >= 1:
                    pe.wait_ge(S["normed1"], n)
                pe.matmul(bank[CEN1][:, :], center, rs[:, g * G:(g + 1) * G], start=True,
                          stop=True).then_inc(S["centered1"], 1)

            def variance1(n):
                pe.wait_ge(S["squared1"], n + 1)
                if n >= 3:
                    pe.wait_ge(S["logged2"], n - 2)
                pe.matmul(bank[VAR][:, :], mean, sq1, start=True, stop=True).then_inc(S["var1"], 1)

            def kvr(n, i):
                b, src = ((KCR, xk), (OV, xv), (RCV, xr))[i]
                pe.wait_ge(S["mixed1"], 3 * n + i + 1)
                if n >= 1:
                    pe.wait_ge(S[("k_copied", "v_copied", "r_bounded")[i]], n)
                lag = (3, 2, 3)[i]
                if n >= lag:
                    pe.wait_ge(S[("cr_bounded", "x_mid", "kv_gated")[i]], n - lag + 1)
                pe.matmul(bank[b][:, :], wrwkv[:, n // NG, i, :], src, start=True, stop=True).then_inc(S["kvr_done"], 1)

            def output(n):
                pe.wait_ge(S["rw_done"], n + 1)
                pe.wait_ge(S["v_copied"], min(n + 2, ITEMS))
                pe.matmul(bank[OV][:, :], wrwkv[:, n // NG, 3, :], rw, start=True, stop=True).then_inc(S["o_done"], 1)

            def center2(n):
                g = n % NG
                pe.wait_ge(S["x_mid"], n + 1)
                if n >= 1:
                    pe.wait_ge(S["normed2"], n)
                pe.matmul(bank[CEN2][:, :], center, rs[:, g * G:(g + 1) * G], start=True,
                          stop=True).then_inc(S["centered2"], 1)

            def variance2(n):
                pe.wait_ge(S["squared2"], n + 1)
                pe.wait_ge(S["logged1"], min(n + 3, ITEMS))
                pe.matmul(bank[VAR][:, :], mean, sq2, start=True, stop=True).then_inc(S["var2"], 1)

            def ffn_gate(n):
                pe.wait_ge(S["mixed2"], 2 * n + 2)
                pe.wait_ge(S["k_copied"], min(n + 3, ITEMS))
                pe.matmul(bank[KCR][:, :], wrwkv[:, n // NG, 8, :], xcr, start=True,
                          stop=True).then_inc(S["cr_done"], 1)

            def ffn_up(n, j):
                pe.wait_ge(S["mixed2"], 2 * n + 1)
                if 4 * n + j >= 2:
                    pe.wait_ge(S["ck_relu"], 4 * n + j - 1)
                pe.matmul(bank[6 + j % 2][:, :], wrwkv[:, n // NG, 4 + j, :], xck, start=True,
                          stop=True).then_inc(S["ck_done"], 1)

            def ffn_down(n, j):
                pe.wait_ge(S["ck_squared"], 4 * n + j + 1)
                if j == 0:
                    pe.wait_ge(S["r_bounded"], min(n + 3, ITEMS))
                mm = pe.matmul(bank[RCV][:, :], wrwkv[:, n // NG, 9 + j, :], ckr[:, j, :], start=(j == 0),
                               stop=(j == FC - 1))
                if j == FC - 1:
                    mm.then_inc(S["cv_done"], 1)

            TAIL = (CEN1, CEN1, OV)

            def center_moe1(j):
                pe.wait_ge(S["x3_added"], j)
                if j == 3:
                    pe.wait_ge(S["x_mid"], ITEMS)
                center_group(norm_moe1(j), group(x, j), TAIL[j - 1])

            def variance_moe1(j):
                variance_group(norm_moe1(j), SIDE1[0], TAIL[j - 1])

            for s in range(STEPS):
                for j in range(FC):
                    do(ffn_down, s - 4, j)
                if s == 2:
                    variance_group(norm_ln0(NG), SIDE0[0], SIDE)
                do(kvr, s - 1, 0)
                do(kvr, s - 1, 1)
                do(ffn_up, s - 3, 0)
                do(ffn_up, s - 3, 1)
                do(center1, s)
                do(output, s - 2)
                do(variance1, s)
                if s == 0:
                    pe.wait_ge(S["x2_added"], NG + 1)
                    center_group(norm_pre(NG), group(x, NG), SIDE)
                do(kvr, s - 1, 2)
                if s == 1:
                    pe.wait_ge(S["ln_normed"], norm_pre(NG))
                    center_group(norm_ln0(NG), SIDE0[2], SIDE)
                if s == ITEMS:
                    pe.wait_ge(S["gw_sq"], 1)
                    pe.wait_ge(S["normed1"], ITEMS)
                    pe.matmul(bank[CEN1][:, 0:E1], ones, msk[:, 0, 0:E1], start=True,
                              stop=True).then_inc(S["gw_ss"], 1)
                    pe.wait_ge(S["rgate_in"], 16)
                if s == LAST + 6:
                    pe.wait_ge(S["normed2"], ITEMS)
                    logits(NG + 1, E1, CEN2)
                finish(variance_moe1, s - 5)
                do(ffn_up, s - 3, 2)
                do(center2, s - 2)
                do(ffn_gate, s - 3)
                do(variance2, s - 2)
                do(ffn_up, s - 3, 3)
                if s == ITEMS:
                    pe.wait_ge(S["gw_guard"], 1)
                finish(center_moe1, s - 4)
                if s == 0:
                    variance_group(norm_pre(NG), SIDE0[0], SIDE)
                if s == LAST + 8:
                    turn_gates(NG + 1, E1, CEN2)

            pe.wait_ge(S["wgu_in"], 16)
            pe.wait_ge(S["wdn_in"], 16)
            pe.wait_ge(S["sel_ready"], 2)

            def experts1(g, first, final):
                pe.wait_ge(S["gt_copied"], NG + g + 1)

                def up1(c):
                    fixed(pe)
                    pe.wait_ge(S["silu_done"], C1 * g + max(c - 1, 0))
                    pe.matmul(bank[0 + c % 2][:, :], wgu[:, 0, c * P:(c + 1) * P], group(nrm, g),
                              start=True, stop=True).then_inc(S["g_done"], 1)
                    fixed(pe)
                    pe.wait_ge(S["su_done"], C1 * g + max(c - 1, 0))
                    pe.matmul(bank[2 + c % 2][:, :], wgu[:, 1, c * P:(c + 1) * P], group(nrm, g),
                              start=True, stop=True).then_inc(S["u_done"], 1)
                    if c < C1 - 1:
                        fixed(pe)
                        pe.wait_ge(S["h1_done"], C1 * g + max(c - 1, 0))
                        pe.matmul(bank[4 + c % 2][:, :], sel[0:3 * E1, c * P:(c + 1) * P],
                                  group(gt[0:3 * E1, :], g), start=True, stop=True).then_inc(S["cbc_done"], 1)

                def down1(c):
                    if c == 0:
                        pe.wait_ge(S["y_added"], g)
                    pe.wait_ge(S["h1_done"], C1 * g + c + 1)
                    pe.matmul(bank[6][:, :], wdn[:, c, :], hh[:, c % 3, :], start=(c == 0),
                              stop=(c == C1 - 1)).then_inc(S["down1_done"], 1)

                for c in range(C1 + 2):
                    if c < C1:
                        up1(c)
                    if c >= 2:
                        down1(c - 2)
                    if first and c == 0:
                        pe.wait_ge(S["x3_added"], NG)
                        pe.wait_ge(S["ck_relu"], FC * ITEMS)
                        center_group(norm_moe1(NG), group(x, NG), SIDE)
                    if first and c == 1:
                        variance_group(norm_moe1(NG), SIDE1[0], SIDE)
                    if not final and c == 3:
                        pe.wait_ge(S["gt_copied"], NG + g + 1)
                        pe.wait_ge(S["ln_logged"], norm_moe1(NG))
                        logits(NG + g + 1, E1, SIDE)
                    if not final and c == 8:
                        turn_gates(NG + g + 1, E1, SIDE)

            experts1(1, True, False)
            with pe.Fori(2, NG) as g:
                experts1(g, False, False)
            experts1(NG, False, True)

        @block.scalar
        def _(act):
            nc.scalar.preload_act_table_set("natural_log_exp_and_others")
            act.wait_ge(S["vec_in"], 16)

            def square_group(i, side, b):
                act.wait_ge(S["ln_centered"], i)
                act.wait_ge(S["ln_var"], i - 1)
                act.wait_ge(S["ln_normed"], i - 1)
                act.activation(side[0], bank[b][:, :], ACT.Square)
                act.activation(side[1], bank[b][:, :], ACT.Identity).then_inc(S["ln_squared"], 1)

            def log_group(i, side, b):
                act.wait_ge(S["ln_var"], i)
                act.wait_ge(S["ln_normed"], i - 1)
                act.activation(side[3], bank[b][:, :], ACT.Ln, bias=eps).then_inc(S["ln_logged"], 1)

            def exp_group(i, side):
                act.wait_ge(S["ln_logged"], i)
                act.activation(side[3], side[3], ACT.Exp, scale=-0.5).then_inc(S["ln_rstd"], 1)

            def rstd_group(i, side, b):
                log_group(i, side, b)
                exp_group(i, side)

            def gate_exp(n, E, by_tanh=False):
                if E == E1:
                    act.wait_ge(S["logit_scaled"], 2 * (n - NG) + 2)
                else:
                    act.wait_ge(S["logit_bounded"], n + 1)
                act.wait_ge(S["gate_sum"], n)
                src = gn if E == E0 else lg
                act.activation(ex[:, :, 0:E], src[:, :, 0:E], ACT.Tanh if by_tanh else ACT.Exp,
                               scale=0.5 if by_tanh else -1.0).then_inc(S["gate_exp"], 1)

            def square_tokens(n):
                act.wait_ge(S["rng_ready"], n + 1)
                act.wait_ge(S["logit_done"], n)
                act.activation(tokens_sq, SIDE1[2], ACT.Square).then_inc(S["sq_ready"], 1)

            for g in range(1, NG + 1):
                act.wait_ge(S["ln_centered"], g)
                act.activation(lnsq[:, g - 1, :], bank[g - 1][:, :], ACT.Square).then_inc(S["ln_squared"], 1)
                for i in ([g - 1] if g < NG else [g - 1, g]):
                    if i:
                        act.wait_ge(S["ln_var"], i)
                        act.activation(lnr[:, i - 1, :], bank[NG + i - 1][:, :], ACT.Ln,
                                       bias=eps).then_inc(S["ln_logged"], 1)
                        act.wait_ge(S["ln_logged"], i)
                        act.activation(lnr[:, i - 1, :], lnr[:, i - 1, :], ACT.Exp, scale=-0.5).then_inc(S["ln_rstd"], 1)

            PROJ, FEAT, OUT = (0, 1), (2, 3), 7

            def attend_group(g, side):
                def squares(p, s):
                    act.wait_ge(S["proj_done"], 16 * g + 2 * p + s + 1)
                    act.wait_ge(S["feat_done"], 32 * g + (4 * (p - 1) + 2 * s + 2 if p else 0))
                    act.activation(stack[0:64, s, 0, :], bank[PROJ[s]][0:64, :], ACT.Identity)
                    act.activation(stack[64:128, s, 0, :], bank[PROJ[s]][0:64, :],
                                   ACT.Square).then_inc(S["stack_even"], 1)

                def exps(p, s):
                    for f in range(4 * p + 2 * s, 4 * p + 2 * s + 2):
                        act.wait_ge(S["feat_done"], 32 * g + f + 1)
                        act.wait_ge(S["score_done"], 32 * g + (4 * (p - 1) if p >= 2 else 0))
                        act.activation(feat[:, p % 2, (f // 2) % 2, f % 2, :], bank[FEAT[f % 2]][:, :],
                                       ACT.Exp).then_inc(S["feat_exp"], 1)

                j = g - 1
                for p in range(NP):
                    squares(p, 0)
                    if side and p == 0:
                        square_group(norm_moe0(j), SIDE0, OUT)
                    squares(p, 1)
                    exps(p, 0)
                    if side and p == 0:
                        rstd_group(norm_moe0(j), SIDE0, OUT)
                    if side and p == 1:
                        gate_exp(j, E0)
                    exps(p, 1)

            attend_group(1, False)
            with act.Fori(1, NG - 1) as j:
                attend_group(j + 1, True)
            attend_group(NG, True)

            SIDE = 7

            def ln0_affine(j):
                act.wait_ge(S["ln_normed"], norm_ln0(j))
                act.activation(group(rs, j), twice, ACT.Identity, bias=ln0_b,
                               scale=ln0_w).then_inc(S["ln0_affined"], 1)

            def experts0(g, first):
                for c in range(C0):
                    act.wait_ge(S["up_done"], 16 * g + c + 1)
                    act.wait_ge(S["h_done"], 16 * g + max(c - 1, 0))
                    act.activation(hr[:, c % 2, :], bank[2 + c % 2][:, :], ACT.Relu).then_inc(S["relu_done"], 1)
                    if first:
                        if c == 1:
                            square_group(norm_moe0(NG), SIDE0, SIDE)
                        if c == 3:
                            rstd_group(norm_moe0(NG), SIDE0, SIDE)
                        if c == 7:
                            gate_exp(NG, E0)
                    else:
                        if c == 1:
                            square_group(norm_pre(g - 1), SIDE0, SIDE)
                        if c == 3:
                            rstd_group(norm_pre(g - 1), SIDE0, SIDE)
                        if c == 6:
                            square_group(norm_ln0(g - 1), SIDE0, SIDE)
                        if c == 8:
                            rstd_group(norm_ln0(g - 1), SIDE0, SIDE)
                        if c == 11:
                            ln0_affine(g - 1)

            experts0(1, True)
            with act.Fori(1, NG) as j:
                experts0(j + 1, False)

            for l in range(L):
                act.activation(expdec[:, l:l + 1], vec[:, l, DECAY:DECAY + 1], ACT.Exp).then_inc(S["decay_exp"], 1)

            def square1(n):
                act.wait_ge(S["centered1"], n + 1)
                if n >= 1:
                    act.wait_ge(S["var1"], n)
                act.activation(sq1, bank[0][:, :], ACT.Square).then_inc(S["squared1"], 1)

            def log_var1(n):
                act.wait_ge(S["var1"], n + 1)
                if n >= 1:
                    act.wait_ge(S["normed1"], n)
                act.activation(rs1, bank[2][:, :], ACT.Ln, bias=eps).then_inc(S["logged1"], 1)

            def rstd1(n):
                act.wait_ge(S["logged1"], n + 1)
                act.activation(rs1, rs1, ACT.Exp, scale=-0.5).then_inc(S["rstd1"], 1)

            def copy_k(n):
                act.wait_ge(S["kvr_done"], 3 * n + 1)
                if n >= 2:
                    act.wait_ge(S["a2_done"], n - 1)
                    act.wait_ge(S["d1_done"], n - 1)
                act.activation(cur(kp[n % 2]), seqs(bank[4][:, :]), ACT.Identity).then_inc(S["k_copied"], 1)

            def copy_v(n):
                act.wait_ge(S["kvr_done"], 3 * n + 2)
                if n >= 2:
                    act.wait_ge(S["kv_done"], n - 1)
                    act.wait_ge(S["t2_done"], n - 1)
                act.activation(vs[n % 2], bank[3][:, :], ACT.Identity).then_inc(S["v_copied"], 1)

            def exp_r(n):
                act.wait_ge(S["r_bounded"], n + 1)
                act.activation(er[n % 2], er[n % 2], ACT.Exp, scale=-1.0).then_inc(S["r_exp"], 1)

            def exp_past(n):
                act.wait_ge(S["a1_done"], n + 1)
                if n >= 1:
                    act.wait_ge(S["aa_scanned"], n)
                    act.wait_ge(S["bb_scanned"], n)
                act.activation(cur(e3b[:, :]), seqs(a1), ACT.Exp).then_inc(S["e3_done"], 1)

            def exp_key(n):
                act.wait_ge(S["a2_done"], n + 1)
                if n >= 1:
                    act.wait_ge(S["bb_scanned"], n)
                    act.wait_ge(S["kv_done"], n)
                act.activation(cur(e4b[:, :]), seqs(a2), ACT.Exp).then_inc(S["e4_done"], 1)

            def exp_state(n):
                act.wait_ge(S["d_above"], n + 1)
                if n >= 1:
                    act.wait_ge(S["t3_done"], n)
                    act.wait_ge(S["t1_done"], n)
                act.activation(e1, d1, ACT.Exp, scale=-1.0).then_inc(S["e1_done"], 1)

            def exp_own(n):
                act.wait_ge(S["d_below"], n + 1)
                if n >= 1:
                    act.wait_ge(S["t2_done"], n)
                    act.wait_ge(S["den_done"], n)
                act.activation(e2, d2, ACT.Exp).then_inc(S["e2_done"], 1)

            def log_den(n):
                act.wait_ge(S["den2_done"], n + 1)
                if n >= 1:
                    act.wait_ge(S["rw_done"], n)
                act.activation(rec, dn2, ACT.Ln).then_inc(S["den_logged"], 1)

            def invert_den(n):
                act.wait_ge(S["den_logged"], n + 1)
                act.activation(rec, rec, ACT.Exp, scale=-1.0).then_inc(S["rec_done"], 1)

            def square2(n):
                act.wait_ge(S["centered2"], n + 1)
                if n >= 1:
                    act.wait_ge(S["var2"], n)
                act.activation(sq2, bank[1][:, :], ACT.Square).then_inc(S["squared2"], 1)

            def log_var2(n):
                act.wait_ge(S["var2"], n + 1)
                if n >= 1:
                    act.wait_ge(S["normed2"], n)
                act.activation(rs2, bank[2][:, :], ACT.Ln, bias=eps).then_inc(S["logged2"], 1)

            def rstd2(n):
                act.wait_ge(S["logged2"], n + 1)
                act.activation(rs2, rs2, ACT.Exp, scale=-0.5).then_inc(S["rstd2"], 1)

            def relu(n, j):
                act.wait_ge(S["ck_done"], 4 * n + j + 1)
                if n >= 1 and j == 0:
                    act.wait_ge(S["cv_done"], n)
                act.activation(ckr[:, j, :], bank[6 + j % 2][:, :], ACT.Relu).then_inc(S["ck_relu"], 1)

            def square_relu(n, j):
                act.wait_ge(S["ck_relu"], 4 * n + j + 1)
                act.activation(ckr[:, j, :], ckr[:, j, :], ACT.Square).then_inc(S["ck_squared"], 1)

            def exp_gate(n):
                act.wait_ge(S["cr_bounded"], n + 1)
                act.activation(ecr, ecr, ACT.Exp, scale=-1.0).then_inc(S["cr_exp"], 1)

            def log_gate(n):
                act.wait_ge(S["cr_exp"], n + 1)
                act.activation(ecr, ecr, ACT.Ln, bias=1.0).then_inc(S["cr_logged"], 1)

            def sigmoid_gate(n):
                act.wait_ge(S["cr_logged"], n + 1)
                if n >= 1:
                    act.wait_ge(S["kv_gated"], n)
                act.activation(scr, ecr, ACT.Exp, scale=-1.0).then_inc(S["cr_sig"], 1)

            TAIL = (0, 0, 3)

            def square_moe1(j):
                square_group(norm_moe1(j), SIDE1, TAIL[j - 1])

            def log_moe1(j):
                log_group(norm_moe1(j), SIDE1, TAIL[j - 1])

            def exp_moe1(j):
                exp_group(norm_moe1(j), SIDE1)

            for s in range(STEPS):
                do(log_den, s - 2)
                do(sigmoid_gate, s - 4)
                do(copy_k, s - 1)
                do(invert_den, s - 2)
                do(copy_v, s - 1)
                finish(square_moe1, s - 5)
                if s == 1:
                    exp_group(norm_pre(NG), SIDE0)
                do(relu, s - 3, 0)
                do(square_relu, s - 3, 0)
                do(relu, s - 3, 1)
                do(square1, s)
                do(exp_key, s - 1)
                do(exp_past, s - 1)
                do(exp_own, s - 1)
                finish(log_moe1, s - 5)
                do(log_var1, s)
                do(exp_state, s - 1)
                do(rstd1, s)
                do(square_relu, s - 3, 1)
                finish(exp_moe1, s - 5)
                do(square2, s - 2)
                do(relu, s - 3, 2)
                if s == 1:
                    square_group(norm_ln0(NG), SIDE0, SIDE)
                do(exp_r, s - 1)
                if s == 1:
                    log_group(norm_ln0(NG), SIDE0, SIDE)
                do(log_var2, s - 2)
                do(rstd2, s - 2)
                if s == 0:
                    square_group(norm_pre(NG), SIDE0, SIDE)
                do(square_relu, s - 3, 2)
                if s == LAST + 6:
                    gate_exp(NG + 1, E1)
                do(relu, s - 3, 3)
                do(square_relu, s - 3, 3)
                if s == 2:
                    ln0_affine(NG)
                if s == 0:
                    log_group(norm_pre(NG), SIDE0, SIDE)
                if s == LAST + 5:
                    square_tokens(NG + 1)
                do(exp_gate, s - 3)
                if s == 1:
                    exp_group(norm_ln0(NG), SIDE0)
                do(log_gate, s - 3)

            def experts1(g, first, final):
                for c in range(C1):
                    act.wait_ge(S["g_done"], C1 * g + c + 1)
                    act.wait_ge(S["su_done"], C1 * g + max(c - 1, 0))
                    act.activation(hr[:, c % 2, :], bank[0 + c % 2][:, :], ACT.Silu).then_inc(S["silu_done"], 1)
                    if first and c == 0:
                        square_group(norm_moe1(NG), SIDE1, SIDE)
                    if first and c == 1:
                        rstd_group(norm_moe1(NG), SIDE1, SIDE)
                    if not final and c == 1:
                        square_tokens(NG + g + 1)
                    if not final and c == 5:
                        gate_exp(NG + g + 1, E1, by_tanh=True)

            experts1(1, True, False)
            with act.Fori(2, NG) as g:
                experts1(g, False, False)
            experts1(NG, False, True)

        @block.gpsimd
        def _(pool):
            for count, names in PER_GROUP:
                for name in names:
                    pool.sem_inc(S[name], count)
            def attention_input(g):
                pool.wait_ge(S["ln_normed"], g if isinstance(g, int) else NG)
                pool.wait_ge(S["proj_done"], 16 * g)
                pool.tensor_copy(ng[:, :], group(nrm, g)).then_inc(S["ng_ready"], 1)

            def routing_input(n, i, dst, g):
                pool.wait_ge(S["ln_normed"], i)
                pool.wait_ge(S["logit_done"], n)
                if dst is SIDE1[2]:
                    pool.wait_ge(S["sq_ready"], n - NG)
                pool.tensor_copy(dst, group(nrm, g)).then_inc(S["rng_ready"], 1)

            def inverse_norms(j):
                pool.wait_ge(S["ss_guard"], j + 1)
                pool.wait_ge(S["logit_scaled"], 2 * j)
                pool.tensor_tensor(gsr[:, :], gsum[:, :], minus_half[:, 0:NT], ALU.pow).then_inc(S["ss_inv"], 1)

            attention_input(1)
            pool.wait_ge(S["sel0_in"], 16)
            pool.tensor_copy(sel[:, :], self32[:, :]).then_inc(S["sel_ready"], 1)
            attention_input(2)
            with pool.Fori(1, NG - 1) as j:
                routing_input(j, norm_moe0(j), SIDE0[2], j)
                attention_input(j + 2)
            routing_input(NG - 1, norm_moe0(NG - 1), SIDE0[2], NG - 1)
            routing_input(NG, norm_moe0(NG), SIDE0[2], NG)

            pool.wait_ge(S["x2_added"], NG + 1)
            pool.memset(h1[:, :, 0:1], 0.0)
            pool.memset(h2[:, :, 0:1], 0.0)
            for i in range(2):
                pool.memset(kp[i].rearrange("p (s t) -> p s t", s=SEQ)[:, :, 0:1], FAR)
            pool.memset(e3b[:, :], 0.0)
            pool.memset(e4b[:, :], 0.0)
            pool.memset(kvb[:, :], 0.0)
            pool.memset(reset[:, :], 0.0).then_inc(S["ones_ready"], 1)
            pool.wait_ge(S["ones_ready"], 1)
            pool.memset(reset[:, :].rearrange("p (s t) -> p s t", s=SEQ)[:, :, 0:1], FAR).then_inc(S["ones_ready"], 1)

            def key_below_max(n):
                pool.wait_ge(S["p_scanned"], n + 1)
                pool.wait_ge(S["k_copied"], n + 1)
                if n >= 1:
                    pool.wait_ge(S["e4_done"], n)
                pool.tensor_tensor(seqs(a2), cur(kp[n % 2]), cur(pm), ALU.subtract).then_inc(S["a2_done"], 1)

            def weigh_value(n):
                pool.wait_ge(S["e4_done"], n + 1)
                pool.wait_ge(S["v_copied"], n + 1)
                if n >= 1:
                    pool.wait_ge(S["aa_scanned"], n)
                pool.tensor_tensor(cur(kvb[:, :]), cur(e4b[:, :]), seqs(vs[n % 2]), ALU.mult).then_inc(S["kv_done"], 1)

            def own_value(n):
                pool.wait_ge(S["e2_done"], n + 1)
                pool.wait_ge(S["v_copied"], n + 1)
                pool.tensor_tensor(t2, e2, vs[n % 2], ALU.mult).then_inc(S["t2_done"], 1)

            def state_den(n):
                pool.wait_ge(S["e1_done"], n + 1)
                pool.wait_ge(S["bb_scanned"], n + 1)
                pool.tensor_tensor(seqs(t3), seqs(e1), prev(bb[:, :]), ALU.mult).then_inc(S["t3_done"], 1)

            def denominator(n):
                pool.wait_ge(S["e2_done"], n + 1)
                pool.wait_ge(S["t3_done"], n + 1)
                if n >= 1:
                    pool.wait_ge(S["den2_done"], n)
                pool.tensor_tensor(dn, e2, t3, ALU.add).then_inc(S["den_done"], 1)

            def state_num(n):
                pool.wait_ge(S["e1_done"], n + 1)
                pool.wait_ge(S["aa_scanned"], n + 1)
                pool.tensor_tensor(seqs(t1), seqs(e1), prev(aa[:, :]), ALU.mult).then_inc(S["t1_done"], 1)

            def numerator(n):
                pool.wait_ge(S["t1_done"], n + 1)
                pool.wait_ge(S["t2_done"], n + 1)
                if n >= 1:
                    pool.wait_ge(S["rw_done"], n)
                pool.tensor_tensor(num, t1, t2, ALU.add).then_inc(S["num_done"], 1)

            def shift2(n):
                pool.wait_ge(S["affined2"], n + 1)
                if n >= 1:
                    pool.wait_ge(S["mixed2"], 2 * n)
                pool.tensor_tensor(seqs(dif2), h2[:, :, 1:T1], h2[:, :, 0:T], ALU.subtract).then_inc(S["diff2"], 1)

            def add_ffn(n):
                g = n % NG + 1
                pool.wait_ge(S["kv_gated"], n + 1)
                pool.wait_ge(S["centered2"], n + 1)
                pool.tensor_tensor(group(rs, g), kvg, group(rs, g), ALU.add).then_inc(S["x_out"], 1)

            for s in range(STEPS):
                do(key_below_max, s)
                do(weigh_value, s)
                do(own_value, s)
                if s == LAST + 4:
                    pool.wait_ge(S["sel1_in"], 16)
                    pool.tensor_copy(sel[0:3 * E1, 0:(C1 - 1) * P],
                                     self32[0:3 * E1, 0:(C1 - 1) * P]).then_inc(S["sel_ready"], 1)
                    routing_input(NG + 1, norm_moe1(1), SIDE1[2], 1)
                do(state_den, s)
                do(denominator, s)
                if s == LAST + 5:
                    pool.wait_ge(S["gw_guard"], 1)
                    pool.tensor_tensor(gn[:, 3, 0:E1], gn[:, 2, 0:E1], minus_half[:, 0:E1], ALU.pow).then_inc(S["gw_inv"], 1)
                    inverse_norms(1)
                do(state_num, s)
                do(shift2, s - 1)
                do(numerator, s)
                do(add_ffn, s - 2)

            with pool.Fori(1, NG) as g:
                routing_input(NG + g + 1, norm_moe1(g + 1), SIDE1[2], g + 1)
                inverse_norms(g + 1)

        @block.vector
        def _(dve):
            def norm_group(i, side, dst):
                dve.wait_ge(S["ln_rstd"], i)
                dve.tensor_tensor(dst, side[1], side[3], ALU.mult).then_inc(S["ln_normed"], 1)

            dve.memset(minus_half[:, :], -0.5)
            dve.memset(lg[:, :, :], UNUSED)
            dve.memset(top2[:, :, :], UNUSED)
            dve.memset(v_aug[:, :, :, HD:HD + 1], 1.0).then_inc(S["const_ready"], 1)
            dve.wait_ge(S["const_ready"], 1)
            def guard_norms(j, b):
                raw = bank[b][:, 0:NT * (E1 + 1)].rearrange("p (t e) -> p t e", t=NT)
                dve.wait_ge(S["logit_done"], NG + j + 1)
                dve.tensor_scalar(gsum[:, :], raw[:, :, E1], NORM_EPS2, None, ALU.max).then_inc(S["ss_guard"], 1)

            def copy_logits(j, E, K, b):
                base = 0 if E == E0 else NG
                n = base + j + 1
                dve.wait_ge(S["logit_done"], n)
                dve.wait_ge(S["gate_exp"], base + j)
                if E == E0:
                    dve.tensor_copy(lg[:, :, 0:E], bank[b][:, 0:NT * E].rearrange("p (t e) -> p t e", t=NT)
                                    ).then_inc(S["logit_copied"], 1)
                    dve.wait_ge(S["logit_copied"], n)
                    dve.tensor_scalar(gn[:, :, 0:E], lg[:, :, 0:E], SIG_MIN, None,
                                      ALU.max).then_inc(S["logit_bounded"], 1)
                else:
                    raw = bank[b][:, 0:NT * (E + 1)].rearrange("p (t e) -> p t e", t=NT)
                    dve.wait_ge(S["ss_inv"], j + 1)
                    dve.tensor_tensor(lg[:, :, 0:E], raw[:, :, 0:E],
                                      gsr[:, :].unsqueeze(2).to_broadcast([P, NT, E]),
                                      ALU.mult).then_inc(S["logit_scaled"], 1)
                    dve.wait_ge(S["logit_scaled"], 2 * j + 1)
                    dve.tensor_tensor(lg[:, :, 0:E], lg[:, :, 0:E],
                                      gn[:, 3, 0:E].unsqueeze(1).to_broadcast([P, NT, E]),
                                      ALU.mult).then_inc(S["logit_scaled"], 1)
                    dve.wait_ge(S["logit_scaled"], 2 * j + 2)
                    dve.sem_inc(S["logit_copied"], 1)
                    fixed(dve)
                    dve.wait_ge(S["logit_copied"], n)
                for t in range(NT):
                    last = dve.max(top[:, t, :], lg[:, t, 0:E])
                last.then_inc(S["top_found"], 1)

            def choose(j, E, K):
                n = (0 if E == E0 else NG) + j + 1
                if K < 8:
                    dve.wait_ge(S["top_found"], n)
                    dve.tensor_copy(top2[:, :, 0:K], top[:, :, 0:K]).then_inc(S["top_packed"], 1)
                    fixed(dve)
                    dve.wait_ge(S["top_packed"], n)
                else:
                    fixed(dve)
                    dve.wait_ge(S["top_found"], n)
                for t in range(NT):
                    if K < 8:
                        last = dve.match_replace(repl[:, t, :], top2[:, t, :], lg[:, t, :], TAKEN)
                    else:
                        last = dve.match_replace(repl[:, t, 0:E], top[:, t, :], lg[:, t, 0:E], TAKEN)
                last.then_inc(S["top_replaced"], 1)
                dve.wait_ge(S["top_replaced"], n)
                dve.tensor_scalar(msk[:, :, 0:E], repl[:, :, 0:E], TAKEN, None,
                                  ALU.is_equal).then_inc(S["gate_mask"], 1)

            def weigh(j, E, by_tanh=False):
                n = (0 if E == E0 else NG) + j + 1
                dve.wait_ge(S["gate_exp"], n)
                if by_tanh:
                    dve.tensor_scalar(gs[:, :, 0:E], ex[:, :, 0:E], 0.5, None, ALU.mult).then_inc(S["gate_sum"], 1)
                    dve.wait_ge(S["gate_sum"], n)
                    dve.tensor_scalar(gr[:, :, 0:E], gs[:, :, 0:E], 0.5, None, ALU.add).then_inc(S["gate_recip"], 1)
                else:
                    dve.tensor_scalar(gs[:, :, 0:E], ex[:, :, 0:E], 1.0, None, ALU.add).then_inc(S["gate_sum"], 1)
                    dve.wait_ge(S["gate_sum"], n)
                    dve.reciprocal(gr[:, :, 0:E], gs[:, :, 0:E]).then_inc(S["gate_recip"], 1)
                dve.wait_ge(S["gate_recip"], n)
                dve.wait_ge(S["gate_mask"], n)
                dve.tensor_tensor(gm[:, :, 0:E], gr[:, :, 0:E], msk[:, :, 0:E], ALU.mult).then_inc(S["gate_masked"], 1)
                dve.wait_ge(S["gate_masked"], n)
                if E == E1:
                    dve.tensor_reduce(gsum[:, :], gm[:, :, 0:E], AX.X, ALU.add).then_inc(S["gate_norm"], 1)
                    dve.wait_ge(S["gate_norm"], 3 * j + 1)
                    dve.reciprocal(den[:, 0, :], gsum[:, :]).then_inc(S["gate_norm"], 1)
                    dve.wait_ge(S["gate_norm"], 3 * j + 2)
                    dve.tensor_tensor(gr[:, :, 0:E], gm[:, :, 0:E],
                                      den[:, 0, :].unsqueeze(2).to_broadcast([P, NT, E]),
                                      ALU.mult).then_inc(S["gate_norm"], 1)
                    dve.wait_ge(S["gate_norm"], 3 * j + 3)

            def split(j, E):
                base = 0 if E == E0 else NG
                n = base + j + 1
                gates = gm if E == E0 else gr
                dve.wait_ge(S["gt_done"], base + j)
                hi, mid, lo = (parts[:, :, i * E:(i + 1) * E] for i in range(3))
                dve.tensor_copy(hi, gates[:, :, 0:E]).then_inc(S["part_hi"], 1)
                dve.wait_ge(S["part_hi"], n)
                dve.tensor_tensor(r1[:, :, 0:E], gates[:, :, 0:E], hi, ALU.subtract).then_inc(S["part_r1"], 1)
                dve.wait_ge(S["part_r1"], n)
                dve.tensor_copy(mid, r1[:, :, 0:E]).then_inc(S["part_mid"], 1)
                dve.wait_ge(S["part_mid"], n)
                dve.tensor_tensor(lo, r1[:, :, 0:E], mid, ALU.subtract).then_inc(S["parts_ready"], 1)

            def copy_gates(j, E, b):
                n = (0 if E == E0 else NG) + j + 1
                dve.wait_ge(S["gt_done"], n)
                dve.tensor_copy(group(gt[0:3 * E, :], j),
                                bank[b][0:3 * E, :].bitcast(BF16)[:, 0:G]).then_inc(S["gt_copied"], 1)

            for g in range(1, NG + 1):
                dve.wait_ge(S["ln_rstd"], g)
                dve.tensor_tensor(group(nrm, g), bank[g - 1][:, :], lnr[:, g - 1, :], ALU.mult).then_inc(S["ln_normed"], 1)

            PROJ, SC, AV, YT, OUT = (0, 1), 4, 5, 6, 7

            def values(g, k):
                dve.wait_ge(S["av_done"], 16 * g - (8 if k < NT else 0))
                dve.wait_ge(S["v_done"], 8 * g + k + 1)
                t, half, hv = k % NT, k // NT, H // 2
                dve.tensor_copy(v_aug[:, t, half * hv:(half + 1) * hv, 0:HD],
                                bank[PROJ[k % 2]][:, :].rearrange("p (h e) -> p h e", h=hv)).then_inc(S["v_evac"], 1)

            def attend_group(g, first, final):
                def copy_odd(p, s):
                    dve.wait_ge(S["proj_done"], 16 * g + 2 * p + s + 1)
                    dve.wait_ge(S["feat_done"], 32 * g + (4 * (p - 1) + 2 * s + 2 if p else 0))
                    y = stack[64:128, s, 1, :]
                    dve.tensor_copy(y, bank[PROJ[s]][64:128, :]).then_inc(S["odd_copied"], 1)

                def square_odd(p, s):
                    y = stack[64:128, s, 1, :]
                    dve.wait_ge(S["odd_copied"], 16 * g + 2 * p + s + 1)
                    dve.tensor_tensor(stack[0:64, s, 1, :], y, y, ALU.mult).then_inc(S["stack_odd"], 1)

                def mask(p, i):
                    dve.wait_ge(S["score_done"], 32 * g + 4 * p + i + 1)
                    dve.wait_ge(S["av_done"], 16 * g + (2 * (p - 1) + i // 2 + 1 if p else 0))
                    dve.tensor_tensor(scores[:, i, :], bank[SC][:, 0:3 * P], causal, ALU.mult).then_inc(S["masked"], 1)

                def normalise(p, b):
                    n = 2 * p + b
                    av = bank[AV][:, 0:4 * (HD + 1)].rearrange("p (h j e) -> p h j e", h=2, j=2)
                    dve.wait_ge(S["av_done"], 16 * g + n + 1)
                    dve.tensor_scalar(den[:, b, :], av[:, :, :, HD], DEN_EPS, None, ALU.add).then_inc(S["den_ready"], 1)
                    dve.wait_ge(S["den_ready"], 32 * g + 2 * n + 1)
                    dve.reciprocal(rden[:, b, :], den[:, b, :]).then_inc(S["den_ready"], 1)
                    dve.wait_ge(S["den_ready"], 32 * g + 2 * n + 2)
                    dve.wait_ge(S["yt_done"], 8 * g + p)
                    for h in range(2):
                        ins_ = dve.tensor_tensor(ynorm[:, 2 * b:2 * b + 2, h, :], av[:, h, :, 0:HD],
                                                 rden[:, b, 2 * h:2 * h + 2].unsqueeze(2).to_broadcast([P, 2, HD]),
                                                 ALU.mult)
                    ins_.then_inc(S["ynormed"], 1)

                def copy_yt(p):
                    dve.wait_ge(S["yt_done"], 8 * g + p + 1)
                    dve.wait_ge(S["wo_done"], 8 * g + p)
                    dve.tensor_copy(yt[:, :], bank[YT][:, :]).then_inc(S["yt_copied"], 1)

                j = g - 1
                for p in range(NP + 2):
                    a, c, d = p < NP, 1 <= p <= NP, p >= 2
                    side, ahead = not first, not final
                    if p == NP and ahead:
                        values(g + 1, 0)
                    if c:
                        mask(p - 1, 0)
                    if p == NP + 1 and ahead:
                        values(g + 1, 4)
                    if d:
                        copy_yt(p - 2)
                    if a:
                        copy_odd(p, 0)
                    if c:
                        mask(p - 1, 1)
                    if a:
                        square_odd(p, 0)
                    if side and p == 2:
                        split(j, E0)
                    if p == NP and ahead:
                        values(g + 1, 1)
                    if p == NP + 1 and ahead:
                        values(g + 1, 5)
                        values(g + 1, 6)
                        values(g + 1, 7)
                    if a:
                        copy_odd(p, 1)
                        square_odd(p, 1)
                    if side and p == 0:
                        norm_group(norm_moe0(j), SIDE0, group(nrm, j))
                    if c:
                        mask(p - 1, 2)
                    if side and p == 1:
                        copy_logits(j, E0, K0, OUT)
                    if p == NP and ahead:
                        values(g + 1, 2)
                    if c:
                        normalise(p - 1, 0)
                    if side and p == 2:
                        copy_gates(j, E0, OUT)
                    if side and p == 1:
                        choose(j, E0, K0)
                    if c:
                        mask(p - 1, 3)
                    if p == NP and ahead:
                        values(g + 1, 3)
                    if c:
                        normalise(p - 1, 1)
                    if side and p == 1:
                        weigh(j, E0)
                dve.wait_ge(S["wo_done"], 8 * g + 8)
                xg = group(x, g)
                dve.tensor_tensor(xg, bank[OUT][:, :], xg, ALU.add).then_inc(S["x1_added"], 1)

            for k in range(2 * NT):
                values(1, k)
            dve.wait_ge(S["masks_in"], 16)
            dve.tensor_copy(identb[:, :], ident).then_inc(S["const_ready"], 1)
            attend_group(1, True, False)
            with dve.Fori(1, NG - 1) as j:
                attend_group(j + 1, False, False)
            attend_group(NG, False, True)

            SIDE = 7

            def experts0(g, first):
                for c in range(C0):
                    dve.wait_ge(S["relu_done"], 16 * g + c + 1)
                    dve.wait_ge(S["gbc_done"], 16 * g + c + 1)
                    dve.wait_ge(S["down_done"], 16 * g + max(c - 2, 0))
                    dve.tensor_tensor(hh[:, c % 3, :], bank[4 + c % 2][:, :], hr[:, c % 2, :],
                                      ALU.mult).then_inc(S["h_done"], 1)
                    if first:
                        if c == 4:
                            norm_group(norm_moe0(NG), SIDE0, group(nrm, NG))
                        if c == 6:
                            copy_logits(NG, E0, K0, SIDE)
                        if c == 8:
                            choose(NG, E0, K0)
                        if c == 9:
                            weigh(NG, E0)
                        if c == 10:
                            split(NG, E0)
                        if c == 12:
                            copy_gates(NG, E0, SIDE)
                    else:
                        if c == 4:
                            norm_group(norm_pre(g - 1), SIDE0, SIDE0[2])
                        if c == 9:
                            norm_group(norm_ln0(g - 1), SIDE0, twice)
                dve.wait_ge(S["down_done"], 16 * g + C0)
                xg = group(x, g)
                dve.tensor_tensor(xg, bank[6][:, :], xg, ALU.add).then_inc(S["x2_added"], 1)

            experts0(1, True)
            with dve.Fori(1, NG) as j:
                experts0(j + 1, False)

            dve.wait_ge(S["decay_exp"], L)
            dve.wait_ge(S["ones_ready"], 2)
            dve.tensor_scalar(negdec[:, :], expdec[:, :], -1.0, None, ALU.mult).then_inc(S["decay_neg"], 1)
            dve.wait_ge(S["decay_neg"], 1)

            def norm1(n):
                dve.wait_ge(S["rstd1"], n + 1)
                if n >= 1:
                    dve.wait_ge(S["affined1"], n)
                dve.tensor_tensor(hn1, bank[0][:, :], rs1, ALU.mult).then_inc(S["normed1"], 1)

            def affine1(n):
                l = n // NG
                dve.wait_ge(S["normed1"], n + 1)
                dve.tensor_scalar(h1[:, :, 1:T1], seqs(hn1), vec[:, l, LNW:LNW + 1], vec[:, l, LNB:LNB + 1],
                                  ALU.mult, ALU.add).then_inc(S["affined1"], 1)

            def shift1(n):
                dve.wait_ge(S["affined1"], n + 1)
                dve.tensor_tensor(seqs(dif1), h1[:, :, 1:T1], h1[:, :, 0:T], ALU.subtract).then_inc(S["diff1"], 1)

            def mix1(n, i):
                l = n // NG
                dve.wait_ge(S["diff1"], n + 1)
                if n >= 1:
                    dve.wait_ge(S["kvr_done"], 3 * (n - 1) + i + 1)
                dve.scalar_tensor_tensor(out=seqs((xk, xv, xr)[i]), in0=seqs(dif1), scalar=vec[:, l, MK + i:MK + i + 1],
                                         in1=h1[:, :, 0:T], op0=ALU.mult, op1=ALU.add).then_inc(S["mixed1"], 1)

            def bound_r(n):
                dve.wait_ge(S["kvr_done"], 3 * n + 3)
                dve.tensor_scalar(er[n % 2], bank[5][:, :], SIG_MIN, None, ALU.max).then_inc(S["r_bounded"], 1)

            def running_max(n):
                l = n // NG
                if n % NG == 0:
                    dve.tensor_scalar(dec, reset[:, :], negdec[:, l:l + 1], None, ALU.add).then_inc(S["decay_bc"], 1)
                    dve.wait_ge(S["decay_bc"], l + 1)
                dve.wait_ge(S["k_copied"], n + 1)
                if n >= 1:
                    dve.wait_ge(S["a2_done"], n)
                dve.tensor_tensor_scan(pm, dec, kp[n % 2], FAR, ALU.add, ALU.max).then_inc(S["p_scanned"], 1)

            def past_below_max(n):
                l = n // NG
                dve.wait_ge(S["p_scanned"], n + 1)
                if n >= 1:
                    dve.wait_ge(S["e3_done"], n)
                dve.scalar_tensor_tensor(out=seqs(a1), in0=prev(pm), scalar=negdec[:, l:l + 1], in1=cur(pm),
                                         op0=ALU.add, op1=ALU.subtract).then_inc(S["a1_done"], 1)

            def own_minus_past(n):
                l = n // NG
                dve.wait_ge(S["p_scanned"], n + 1)
                if n >= 1:
                    dve.wait_ge(S["e1_done"], n)
                dve.scalar_tensor_tensor(out=seqs(d1), in0=cur(kp[n % 2]), scalar=vec[:, l, FIRST:FIRST + 1],
                                         in1=prev(pm), op0=ALU.add, op1=ALU.subtract).then_inc(S["d1_done"], 1)

            def own_below(n):
                dve.wait_ge(S["d1_done"], n + 1)
                if n >= 1:
                    dve.wait_ge(S["e2_done"], n)
                dve.tensor_scalar(d2, d1, 0.0, None, ALU.min).then_inc(S["d_below"], 1)

            def own_above(n):
                dve.wait_ge(S["d_below"], n + 1)
                dve.tensor_scalar(d1, d1, 0.0, None, ALU.max).then_inc(S["d_above"], 1)

            def scan_bb(n):
                dve.wait_ge(S["e3_done"], n + 1)
                dve.wait_ge(S["e4_done"], n + 1)
                if n >= 1:
                    dve.wait_ge(S["t3_done"], n)
                dve.tensor_tensor_scan(bb[:, :], e3b[:, :], e4b[:, :], 0.0, ALU.mult, ALU.add).then_inc(S["bb_scanned"], 1)

            def scan_aa(n):
                dve.wait_ge(S["kv_done"], n + 1)
                if n >= 1:
                    dve.wait_ge(S["t1_done"], n)
                dve.tensor_tensor_scan(aa[:, :], e3b[:, :], kvb[:, :], 0.0, ALU.mult, ALU.add).then_inc(S["aa_scanned"], 1)

            def receive_den(n):
                dve.wait_ge(S["den_done"], n + 1)
                dve.wait_ge(S["r_exp"], n + 1)
                if n >= 1:
                    dve.wait_ge(S["den_logged"], n)
                dve.scalar_tensor_tensor(out=dn2, in0=er[n % 2], scalar=1.0, in1=dn,
                                         op0=ALU.add, op1=ALU.mult).then_inc(S["den2_done"], 1)

            def receive(n):
                dve.wait_ge(S["rec_done"], n + 1)
                dve.wait_ge(S["num_done"], n + 1)
                if n >= 1:
                    dve.wait_ge(S["o_done"], n)
                dve.tensor_tensor(rw, num, rec, ALU.mult).then_inc(S["rw_done"], 1)

            def add_output(n):
                g = n % NG + 1
                dve.wait_ge(S["o_done"], n + 1)
                dve.wait_ge(S["centered1"], n + 1)
                dve.tensor_tensor(group(rs, g), bank[3][:, :], group(rs, g), ALU.add).then_inc(S["x_mid"], 1)

            def norm2(n):
                dve.wait_ge(S["rstd2"], n + 1)
                dve.tensor_tensor(hn2, bank[1][:, :], rs2, ALU.mult).then_inc(S["normed2"], 1)

            def affine2(n):
                l = n // NG
                dve.wait_ge(S["normed2"], n + 1)
                dve.tensor_scalar(h2[:, :, 1:T1], seqs(hn2), vec[:, l, LN2W:LN2W + 1], vec[:, l, LN2B:LN2B + 1],
                                  ALU.mult, ALU.add).then_inc(S["affined2"], 1)

            def mix2(n, i):
                l = n // NG
                dve.wait_ge(S["diff2"], n + 1)
                if n >= 1:
                    if i == 0:
                        dve.wait_ge(S["ck_done"], 4 * n)
                    else:
                        dve.wait_ge(S["cr_done"], n)
                dve.scalar_tensor_tensor(out=seqs((xck, xcr)[i]), in0=seqs(dif2), scalar=vec[:, l, CMK + i:CMK + i + 1],
                                         in1=h2[:, :, 0:T], op0=ALU.mult, op1=ALU.add).then_inc(S["mixed2"], 1)

            def bound_cr(n):
                dve.wait_ge(S["cr_done"], n + 1)
                if n >= 1:
                    dve.wait_ge(S["cr_sig"], n)
                dve.tensor_scalar(ecr, bank[4][:, :], SIG_MIN, None, ALU.max).then_inc(S["cr_bounded"], 1)

            def gate_ffn(n):
                dve.wait_ge(S["cr_sig"], n + 1)
                dve.wait_ge(S["cv_done"], n + 1)
                if n >= 1:
                    dve.wait_ge(S["x_out"], n)
                dve.tensor_tensor(kvg, bank[5][:, :], scr, ALU.mult).then_inc(S["kv_gated"], 1)

            def norm_group_moe1(j):
                norm_group(norm_moe1(j), SIDE1, group(nrm, j))

            def add_rwkv(n):
                g = n - LAST + 1
                dve.wait_ge(S["x_out"], n + 1)
                dve.tensor_tensor(group(x, g), group(x, g), group(rs, g), ALU.add).then_inc(S["x3_added"], 1)

            for s in range(STEPS):
                finish(norm_group_moe1, s - 6)
                do(shift1, s - 1)
                do(mix1, s - 1, 0)
                do(norm2, s - 3)
                do(affine2, s - 3)
                do(receive_den, s - 2)
                do(mix1, s - 1, 1)
                if s == LAST + 7:
                    weigh(1, E1)
                do(mix2, s - 3, 0)
                if s == LAST + 7:
                    split(1, E1)
                do(mix1, s - 1, 2)
                do(gate_ffn, s - 4)
                do(running_max, s - 1)
                do(receive, s - 2)
                do(own_minus_past, s - 1)
                do(past_below_max, s - 1)
                do(own_below, s - 1)
                do(add_output, s - 2)
                if s == LAST + 6:
                    guard_norms(1, 1)
                if s == 1:
                    norm_group(norm_pre(NG), SIDE0, SIDE0[2])
                do(own_above, s - 1)
                do(mix2, s - 3, 1)
                if s == LAST + 6:
                    dve.wait_ge(S["gw_inv"], 1)
                    copy_logits(1, E1, K1, 1)
                if s == LAST + 7:
                    copy_gates(1, E1, 1)
                do(scan_bb, s - 1)
                do(bound_r, s - 1)
                do(scan_aa, s - 1)
                do(norm1, s)
                do(affine1, s)
                if s == ITEMS:
                    dve.wait_ge(S["gw_ss"], 1)
                    dve.tensor_scalar(gn[:, 2, 0:E1], bank[0][:, 0:E1], NORM_EPS2, None,
                                      ALU.max).then_inc(S["gw_guard"], 1)
                if s - 4 >= LAST:
                    do(add_rwkv, s - 4)
                if s == 2:
                    norm_group(norm_ln0(NG), SIDE0, twice)
                if s == LAST + 6:
                    choose(1, E1, K1)
                do(bound_cr, s - 3)
                if s == ITEMS - 3:
                    dve.wait_ge(S["rgate_in"], 16)
                    dve.tensor_tensor(msk[:, 0, 0:E1], rgate[:, :], rgate[:, :], ALU.mult).then_inc(S["gw_sq"], 1)

            SIDE = 7

            def experts1(g, first, final):
                for c in range(C1):
                    n = C1 * g + c
                    dve.wait_ge(S["silu_done"], n + 1)
                    dve.wait_ge(S["u_done"], n + 1)
                    if c < C1 - 1:
                        dve.wait_ge(S["h1_done"], C1 * g + c)
                        dve.tensor_tensor(yt[:, :], bank[2 + c % 2][:, :], hr[:, c % 2, :], ALU.mult).then_inc(S["su_done"], 1)
                        dve.wait_ge(S["su_done"], n + 1)
                        dve.wait_ge(S["cbc_done"], (C1 - 1) * g + c + 1)
                        dve.wait_ge(S["down1_done"], C1 * g + max(c - 2, 0))
                        dve.tensor_tensor(hh[:, c % 3, :], bank[4 + c % 2][:, :], yt[:, :], ALU.mult).then_inc(S["h1_done"], 1)
                    else:
                        dve.wait_ge(S["down1_done"], C1 * g + c - 2)
                        dve.tensor_tensor(hh[:, c % 3, :], bank[2 + c % 2][:, :], hr[:, c % 2, :],
                                          ALU.mult).then_inc(S["su_done"], 1)
                        dve.wait_ge(S["su_done"], n + 1)
                        dve.sem_inc(S["h1_done"], 1)
                    if first and c == 2:
                        norm_group(norm_moe1(NG), SIDE1, group(nrm, NG))
                    if not final:
                        if c == 3:
                            guard_norms(g + 1, SIDE)
                        if c == 4:
                            copy_logits(g + 1, E1, K1, SIDE)
                        if c == 5:
                            choose(g + 1, E1, K1)
                        if c == 6:
                            weigh(g + 1, E1, by_tanh=True)
                            split(g + 1, E1)
                        if c == C1 - 1:
                            copy_gates(g + 1, E1, SIDE)
                dve.wait_ge(S["down1_done"], C1 * g + C1)
                xg = group(x, g)
                dve.tensor_tensor(xg, bank[6][:, :], xg, ALU.add).then_inc(S["y_added"], 1)

            experts1(1, True, False)
            with dve.Fori(2, NG) as g:
                experts1(g, False, False)
            experts1(NG, False, True)


def arrays_for(inputs):
    import numpy as np
    f = lambda a: np.ascontiguousarray(a)
    i = {k: np.asarray(v) for k, v in inputs.items()}
    c = lambda k: i["L1_attn_" + k]
    eye = np.eye(P, dtype=np.float32)
    tri = np.triu(np.ones((P, P), np.float32))
    one = np.ones((P, P), np.float32)
    consts = np.concatenate([eye - one / P, one / P, eye, one, tri, one, tri], axis=1)

    def selector(E, chunks):
        s = np.zeros((3 * E, chunks * P), np.float32)
        for part in range(3):
            for e in range(E):
                s[part * E + e, e * 64:(e + 1) * 64] = 1.0
        return s

    wf = i["L0_attn_W_feat"]
    half = np.full((HD, NF), -0.5, np.float32)
    wfeat = np.stack([np.concatenate([wf, half]), np.concatenate([half, wf])], axis=1)
    lay = []
    for l in range(L):
        ws = [c("Wk")[l].T, c("Wv")[l].T, c("Wr")[l].T, c("Wo")[l].T]
        ws += [c("Wck")[l][j * P:(j + 1) * P].T for j in range(FC)]
        ws += [c("Wcr")[l].T]
        ws += [c("Wcv")[l][:, j * P:(j + 1) * P].T for j in range(FC)]
        lay.append(np.stack(ws, axis=1))
    wrwkv = np.stack(lay, axis=1)
    vec = np.zeros((P, L + 1, NVEC), np.float32)
    for l in range(L):
        for j, k in enumerate(("ln1_w", "ln1_b", "tmk", "tmv", "tmr", "time_decay", "time_first",
                               "ln2_w", "ln2_b", "cmk", "cmr")):
            vec[:, l, j] = c(k)[l]
    vec[:, L, 0] = LN_EPS
    vec[:, L, 1] = c("ln0_w")
    vec[:, L, 2] = c("ln0_b")
    m = lambda k: i["L1_ffn_" + k]
    ed = lambda a: a.transpose(1, 0, 2).reshape(P, E1 * 64)
    pad = np.zeros((P, 64), np.float32)
    wgu = np.stack([np.concatenate([ed(m("w_gate")), m("sw_gate"), pad], axis=1),
                    np.concatenate([ed(m("w_up")), m("sw_up"), pad], axis=1)], axis=1)
    wdn = np.zeros((P, C1, P), np.float32)
    wdn[:, :C1 - 1] = m("w_down").reshape(C1 - 1, P, P).transpose(1, 0, 2)
    wdn[:64, C1 - 1] = m("sw_down")
    return {k: f(v) for k, v in {
        "x": i["L0_attn_x"].transpose(2, 0, 1).reshape(P, N),
        "consts": consts,
        "wq": i["L0_attn_Wq"], "wk": i["L0_attn_Wk"], "wv": i["L0_attn_Wv"],
        "wfeat": wfeat,
        "wo": i["L0_attn_Wo"].reshape(NP, P, P).transpose(1, 0, 2),
        "vec": vec,
        "esel": i["L0_ffn_expert_sel"].T,
        "sel0": selector(E0, C0),
        "keys": i["L0_ffn_keys"].transpose(1, 0, 2).reshape(P, E0 * 64),
        "vals": i["L0_ffn_values"].reshape(C0, P, P).transpose(1, 0, 2),
        "wrwkv": wrwkv,
        "rgate": m("gate_w").T,
        "wgu": wgu, "wdn": wdn,
        "sel1": selector(E1, C1 - 1),
    }.items()}


def kernel(**inputs):
    import numpy as _np
    import concourse.bacc as _bacc
    from concourse import mybir as _mybir
    from concourse.bass_utils import run_bass_kernel_spmd as _run

    nc = _bacc.Bacc("TRN2", target_bir_lowering=False, num_devices=1)
    laid = arrays_for(inputs)
    arrays, args = {}, {}
    for name, a in laid.items():
        arrays[f"in_{name}_dram"] = a
        args[name] = nc.dram_tensor(f"in_{name}_dram", a.shape, _mybir.dt.from_np(a.dtype), kind="ExternalInput").ap()
    out = nc.dram_tensor("out_dram", (P, N), F32, kind="ExternalOutput").ap()
    two_blocks(nc, args, out)
    r = _run(nc, [arrays], core_ids=[0])
    got = r.results[0]["out_dram"]
    return _np.ascontiguousarray(_np.asarray(got).reshape(P, B, T).transpose(1, 2, 0))
```
